# Optimizing a Trainium2 kernel written in Bass

```python
import numpy as np
import jax
import jax.numpy as jnp

def _softmax(x, axis=-1):
    return jax.nn.softmax(x, axis=axis)

def _gelu(x):
    return jax.nn.gelu(x, approximate=True)

def _silu(x):
    return jax.nn.silu(x)

def _sigmoid(x):
    return jax.nn.sigmoid(x)

def _layernorm(x, axis=-1, eps=1e-05):
    m = jnp.mean(x, axis=axis, keepdims=True)
    v = jnp.var(x, axis=axis, keepdims=True)
    return (x - m) / jnp.sqrt(v + eps)

def _scatter_add(tgt, idx, src, axis=0):
    return tgt.at[idx].add(src)

def _segment_sum(src, seg, n):
    return jax.ops.segment_sum(src, seg, n)
kernel_name = 'mk_flamingo_gated_d4_seqx_r4_61c94e'

def setup_inputs(seed: int=0):
    np.random.seed(seed)
    _w = jnp.asarray

    def _rec_inputs():
        import jax
        import jax.numpy as jnp
        _rk = jax.random.key(seed)
        x = 7.22e-05 + 1 * jax.random.normal(jax.random.fold_in(_rk, 1), (2, 1024, 256), jnp.float32)
        _lenS = 1024 - jax.random.randint(jax.random.fold_in(_rk, 7), (2,), 0, max(1, 1024 // 4) + 1, jnp.int32)
        _lenS2 = 154 - jax.random.randint(jax.random.fold_in(_rk, 8), (2,), 0, max(1, 154 // 4) + 1, jnp.int32)
        _ctx_1024P = jax.random.normal(jax.random.fold_in(_rk, 11), (2, 16, 256), jnp.float32)
        _ctx_1024c = jax.random.dirichlet(jax.random.fold_in(_rk, 511), 0.3 * jnp.ones((16,), jnp.float32), (2, 154))
        _ctx_1024t = jnp.einsum('bsk,bkd->bsd', _ctx_1024c, _ctx_1024P)
        _ctx_1024t = _ctx_1024t * jax.lax.rsqrt(jnp.mean(jnp.square(_ctx_1024t)) + 1e-12) * 0.953939
        ctx_1024 = 4.13588e-05 + 0.999923 * (_ctx_1024t + 0.3 * jax.random.normal(jax.random.fold_in(_rk, 611), (2, 154, 256), jnp.float32))
        _validS = jnp.arange(1024)[None, :] < _lenS[:, None]
        _validS2 = jnp.arange(154)[None, :] < _lenS2[:, None]
        _causal = jnp.tril(jnp.ones((1024, 1024), dtype=bool))
        mask_BxS2_bk0 = jnp.logical_not(jnp.broadcast_to(_validS2[:, :], (2, 154)))
        _g = jax.random.normal(jax.random.fold_in(_rk, 9001), (2, 4), jnp.float32)
        _g = jnp.sign(_g) * jnp.maximum(jnp.abs(_g), 1.0) + (_g == 0) * 1.0
        g_xattn = _g[0]
        g_ffn = _g[1]
        return (x, ctx_1024, mask_BxS2_bk0, g_xattn, g_ffn)
    x, ctx_1024, mask_BxS2_bk0, g_xattn, g_ffn = _rec_inputs()

    def _L0_xattn_setup():
        import jax, jax.numpy as jnp
        import numpy as np
        D_MODEL = 256
        key = jax.random.key(seed)
        ks = jax.random.split(key, 6)
        B, S, D = (4, 512, D_MODEL)
        q = jax.random.normal(ks[0], (B, S, D), dtype=jnp.float32)
        k = jax.random.normal(ks[1], (B, S, D), dtype=jnp.float32)
        v = jax.random.normal(ks[2], (B, S, D), dtype=jnp.float32)
        scale = 1.0 / np.sqrt(D)
        w_q = jax.random.uniform(ks[3], (D, D), jnp.float32, -scale, scale)
        w_k = jax.random.uniform(ks[4], (D, D), jnp.float32, -scale, scale)
        w_v = jax.random.uniform(ks[5], (D, D), jnp.float32, -scale, scale)
        return {'q': q, 'k': k, 'v': v, 'w_q': w_q, 'w_k': w_k, 'w_v': w_v}
    _L0_xattn_all = _L0_xattn_setup()
    _L0_xattn_in = {k: v for k, v in _L0_xattn_all.items() if k in ('w_q', 'w_k', 'w_v')}
    del _L0_xattn_all

    def _L0_ffn_setup():
        import jax, jax.numpy as jnp
        import numpy as np
        B, S, D, E, F = (2, 512, 256, 8, 1024)
        key = jax.random.key(seed)
        ks = jax.random.split(key, 4)
        return {'hidden_states': jax.random.normal(ks[0], (B, S, D), dtype=jnp.float32), 'Wr': jax.random.normal(ks[1], (D, E), dtype=jnp.float32) * (1.0 / np.sqrt(D)), 'W1': jax.random.normal(ks[2], (E, D, F), dtype=jnp.float32) * (1.0 / np.sqrt(D)), 'b1': jnp.zeros((E, F), dtype=jnp.float32), 'W2': jax.random.normal(ks[3], (E, F, D), dtype=jnp.float32) * (1.0 / np.sqrt(F)), 'b2': jnp.zeros((E, D), dtype=jnp.float32)}
    _L0_ffn_all = _L0_ffn_setup()
    _L0_ffn_in = {k: v for k, v in _L0_ffn_all.items() if k in ('Wr', 'W1', 'b1', 'W2', 'b2')}
    del _L0_ffn_all

    def _L1_xattn_setup():
        import jax, jax.numpy as jnp
        import numpy as np
        DIM = 256
        DIM_LATENT = 256
        DIM_HEAD = 64
        INNER = max(DIM, DIM_LATENT)
        HEADS = INNER // DIM_HEAD
        SCALE = DIM_HEAD ** (-0.5)
        LN_EPS = 1e-05
        RMS_EPS = 1e-08

        def layernorm(x, g, b):
            mu = jnp.mean(x, axis=-1, keepdims=True)
            var = jnp.mean(jnp.square(x - mu), axis=-1, keepdims=True)
            return (x - mu) * jax.lax.rsqrt(var + LN_EPS) * g + b

        def rmsnorm(x, gamma):
            n = jnp.linalg.norm(x, axis=-1, keepdims=True) * x.shape[-1] ** (-0.5)
            return x / jnp.maximum(n, RMS_EPS) * gamma
        key = jax.random.key(seed)
        ks = jax.random.split(key, 8)
        b, n, nl = (8, 512, 128)
        x = jax.random.normal(ks[0], (b, n, DIM), dtype=jnp.float32)
        latents = jax.random.normal(ks[1], (b, nl, DIM_LATENT), dtype=jnp.float32)
        mask = jax.random.randint(ks[2], (b, n), 0, 2).astype(bool)
        init = lambda k, shape, fan_in: jax.random.normal(k, shape, jnp.float32) * fan_in ** (-0.5)
        return {'x': x, 'latents': latents, 'mask': mask, 'ln_x_g': jnp.ones((DIM,), jnp.float32), 'ln_x_b': jnp.zeros((DIM,), jnp.float32), 'ln_l_g': jnp.ones((DIM_LATENT,), jnp.float32), 'ln_l_b': jnp.zeros((DIM_LATENT,), jnp.float32), 'q_gamma': jnp.ones((DIM_HEAD,), jnp.float32), 'k_gamma': jnp.ones((DIM_HEAD,), jnp.float32), 'W_q': init(ks[3], (DIM_LATENT, INNER), DIM_LATENT), 'W_kv': init(ks[4], (DIM, 2 * INNER), DIM), 'W_out': init(ks[5], (INNER, DIM_LATENT), INNER), 'b_out': jnp.zeros((DIM_LATENT,), jnp.float32)}
    _L1_xattn_all = _L1_xattn_setup()
    _L1_xattn_in = {k: v for k, v in _L1_xattn_all.items() if k in ('ln_x_g', 'ln_x_b', 'ln_l_g', 'ln_l_b', 'q_gamma', 'k_gamma', 'W_q', 'W_kv', 'W_out', 'b_out')}
    del _L1_xattn_all

    def _L1_ffn_setup():
        import jax, jax.numpy as jnp
        import numpy as np
        DIM = 256
        HID = 512
        OUT = 256
        NE = 8
        TOPK = 2

        def _xavier(key, shape):
            fan_in, fan_out = (shape[-2], shape[-1])
            lim = jnp.sqrt(6.0 / (fan_in + fan_out))
            return jax.random.uniform(key, shape, jnp.float32, -lim, lim)
        key = jax.random.key(seed)
        ks = jax.random.split(key, 8)
        X = jax.random.normal(ks[0], (4, 256, DIM), jnp.float32)
        W1 = _xavier(ks[1], (NE, DIM, HID))
        W3 = _xavier(ks[2], (NE, DIM, HID))
        W2 = _xavier(ks[3], (NE, HID, OUT))
        b1 = jnp.zeros((NE, HID), jnp.float32)
        b3 = jnp.zeros((NE, HID), jnp.float32)
        b2 = jnp.zeros((NE, OUT), jnp.float32)
        Wg = _xavier(ks[4], (DIM, NE))
        bg = jnp.zeros((NE,), jnp.float32)
        Wf = _xavier(ks[5], (OUT, OUT))
        bf = jnp.zeros((OUT,), jnp.float32)
        return {'X': X, 'W1': W1, 'b1': b1, 'W3': W3, 'b3': b3, 'W2': W2, 'b2': b2, 'Wg': Wg, 'bg': bg, 'Wf': Wf, 'bf': bf}
    _L1_ffn_all = _L1_ffn_setup()
    _L1_ffn_in = {k: v for k, v in _L1_ffn_all.items() if k in ('W1', 'b1', 'W3', 'b3', 'W2', 'b2', 'Wg', 'bg', 'Wf', 'bf')}
    del _L1_ffn_all

    def _L2_xattn_setup():
        import jax, jax.numpy as jnp
        import numpy as np
        B, L_ENC, L_DEC, D = (16, 128, 128, 256)
        key = jax.random.key(seed)
        k1, k2, k3, k4, k5, k6 = jax.random.split(key, 6)
        encoder_hc = jax.random.normal(k1, (B, L_ENC, D), dtype=jnp.float32)
        decoder_hq = jax.random.normal(k2, (B, L_DEC, D), dtype=jnp.float32)
        w_sim = jax.random.normal(k3, (3 * D,), dtype=jnp.float32) * 0.02
        b_sim = jax.random.normal(k4, (1,), dtype=jnp.float32) * 0.02
        W_qv = jax.random.normal(k5, (4 * D, D), dtype=jnp.float32) * 0.02
        b_qv = jax.random.normal(k6, (D,), dtype=jnp.float32) * 0.02
        return {'encoder_hc': encoder_hc, 'decoder_hq': decoder_hq, 'w_sim': w_sim, 'b_sim': b_sim, 'W_qv': W_qv, 'b_qv': b_qv}
    _L2_xattn_all = _L2_xattn_setup()
    _L2_xattn_in = {k: v for k, v in _L2_xattn_all.items() if k in ('w_sim', 'b_sim', 'W_qv', 'b_qv')}
    del _L2_xattn_all

    def _L2_ffn_setup():
        import jax, jax.numpy as jnp
        import numpy as np
        TEMPERATURE = 0.5
        CAPACITY_FACTOR = 1.25
        TOP_K = 1
        key = jax.random.key(seed)
        ks = jax.random.split(key, 5)
        B, S, D, H, E = (4, 512, 256, 512, 8)
        s = 0.02
        return {'x': jax.random.normal(ks[0], (B, S, D), jnp.float32), 'gate_w': jax.random.normal(ks[1], (E, D), jnp.float32) * s, 'gate_b': jnp.zeros((E,), jnp.float32), 'rms_w': jnp.ones((E,), jnp.float32), 'w1': jax.random.normal(ks[2], (E, D, H), jnp.float32) * s, 'b1': jnp.zeros((E, H), jnp.float32), 'w2': jax.random.normal(ks[3], (E, H, D), jnp.float32) * s, 'b2': jnp.zeros((E, D), jnp.float32)}
    _L2_ffn_all = _L2_ffn_setup()
    _L2_ffn_in = {k: v for k, v in _L2_ffn_all.items() if k in ('gate_w', 'gate_b', 'rms_w', 'w1', 'b1', 'w2', 'b2')}
    del _L2_ffn_all

    def _L3_xattn_setup():
        import jax, jax.numpy as jnp
        import numpy as np
        DIM = 256
        HEADS = 16
        DIM_HEAD = 64
        INNER = HEADS * DIM_HEAD
        EPS = 1e-05

        def _split_heads(t):
            b, n, _ = t.shape
            return t.reshape(b, n, HEADS, DIM_HEAD).transpose(0, 2, 1, 3)
        key = jax.random.key(seed)
        ks = jax.random.split(key, 9)
        b, n, m = (2, 512, 64)
        s = DIM ** (-0.5)
        return {'x': jax.random.normal(ks[0], (b, n, DIM), jnp.float32), 'memories': jax.random.normal(ks[1], (b, m, DIM), jnp.float32), 'ln_g': jnp.ones((DIM,), jnp.float32), 'ln_b': jnp.zeros((DIM,), jnp.float32), 'Wq': jax.random.normal(ks[2], (DIM, INNER), jnp.float32) * s, 'Wkv': jax.random.normal(ks[3], (DIM, 2 * INNER), jnp.float32) * s, 'Wm': jax.random.normal(ks[4], (DIM, INNER), jnp.float32) * s, 'Wo': jax.random.normal(ks[5], (INNER, DIM), jnp.float32) * s, 'bo': jnp.zeros((DIM,), jnp.float32)}
    _L3_xattn_all = _L3_xattn_setup()
    _L3_xattn_in = {k: v for k, v in _L3_xattn_all.items() if k in ('ln_g', 'ln_b', 'Wq', 'Wkv', 'Wm', 'Wo', 'bo')}
    del _L3_xattn_all

    def _L3_ffn_setup():
        import jax, jax.numpy as jnp
        import numpy as np
        DIM = 256
        INTER = 256
        E = 32
        K = 4
        G = 8
        LG = 4
        ROUTE_SCALE = 1.0
        CAP_FACTOR = 1.25
        B, S = (4, 512)

        def _gate(xf, wg):
            logits = xf @ wg.T
            scores = jax.nn.softmax(logits, axis=-1)
            sg = scores.reshape(-1, G, E // G)
            group_scores = sg.max(axis=-1)
            _, gtop = jax.lax.top_k(group_scores, LG)
            keep_g = jnp.sum(jax.nn.one_hot(gtop, G, dtype=jnp.float32), axis=1) > 0
            masked = jnp.where(keep_g[:, :, None], sg, -jnp.inf).reshape(-1, E)
            _, idx = jax.lax.top_k(masked, K)
            w = jnp.take_along_axis(scores, idx, axis=1)
            w = w / (w.sum(-1, keepdims=True) + 1e-09) * ROUTE_SCALE
            return (w.astype(xf.dtype), idx)

        def _forward(x, wg, w1, w2, w3, sw1, sw2, sw3):
            shape = x.shape
            xf = x.reshape(-1, DIM)
            N = xf.shape[0]
            cap = max(1, int(CAP_FACTOR * N * K / E))
            w, idx = _gate(xf, wg)
            fe = idx.reshape(-1)
            oh = jax.nn.one_hot(fe, E, dtype=jnp.int32)
            pos = (jnp.cumsum(oh, axis=0) * oh).sum(-1) - 1
            keep = pos < cap
            dest = jnp.where(keep, fe * cap + pos, E * cap)
            tok = jnp.arange(N * K, dtype=jnp.int32) // K
            buf_tok = jnp.full((E * cap + 1,), N, jnp.int32).at[dest].set(tok)[:-1]
            buf_w = jnp.zeros((E * cap + 1,), x.dtype).at[dest].set(w.reshape(-1))[:-1]
            xp = jnp.concatenate([xf, jnp.zeros((1, DIM), x.dtype)], axis=0)
            xe = xp[buf_tok].reshape(E, cap, DIM)
            h = jax.nn.silu(jnp.einsum('ecd,edh->ech', xe, w1)) * jnp.einsum('ecd,edh->ech', xe, w3)
            out = jnp.einsum('ech,ehd->ecd', h, w2) * buf_w.reshape(E, cap, 1)
            y = jnp.zeros((N + 1, DIM), x.dtype).at[buf_tok].add(out.reshape(E * cap, DIM))[:N]
            z = jax.nn.silu(xf @ sw1) * (xf @ sw3) @ sw2
            return (y + z).reshape(shape)
        key = jax.random.key(seed)
        ks = jax.random.split(key, 9)
        sd = DIM ** (-0.5)
        si = INTER ** (-0.5)
        x = jax.random.normal(ks[0], (B, S, DIM), jnp.float32)
        wg = jax.random.normal(ks[1], (E, DIM), jnp.float32) * sd
        w1 = jax.random.normal(ks[2], (E, DIM, INTER), jnp.float32) * sd
        w3 = jax.random.normal(ks[3], (E, DIM, INTER), jnp.float32) * sd
        w2 = jax.random.normal(ks[4], (E, INTER, DIM), jnp.float32) * si
        sw1 = jax.random.normal(ks[5], (DIM, INTER), jnp.float32) * sd
        sw3 = jax.random.normal(ks[6], (DIM, INTER), jnp.float32) * sd
        sw2 = jax.random.normal(ks[7], (INTER, DIM), jnp.float32) * si
        return dict(x=x, wg=wg, w1=w1, w2=w2, w3=w3, sw1=sw1, sw2=sw2, sw3=sw3)
    _L3_ffn_all = _L3_ffn_setup()
    _L3_ffn_in = {k: v for k, v in _L3_ffn_all.items() if k in ('wg', 'w1', 'w2', 'w3', 'sw1', 'sw2', 'sw3')}
    del _L3_ffn_all
    return {'x': x, 'ctx_1024': ctx_1024, 'mask_BxS2_bk0': mask_BxS2_bk0, 'g_xattn': g_xattn, 'g_ffn': g_ffn, 'L0_xattn_w_q': _L0_xattn_in['w_q'], 'L0_xattn_w_k': _L0_xattn_in['w_k'], 'L0_xattn_w_v': _L0_xattn_in['w_v'], 'L0_ffn_Wr': _L0_ffn_in['Wr'], 'L0_ffn_W1': _L0_ffn_in['W1'], 'L0_ffn_b1': _L0_ffn_in['b1'], 'L0_ffn_W2': _L0_ffn_in['W2'], 'L0_ffn_b2': _L0_ffn_in['b2'], 'L1_xattn_ln_x_g': _L1_xattn_in['ln_x_g'], 'L1_xattn_ln_x_b': _L1_xattn_in['ln_x_b'], 'L1_xattn_ln_l_g': _L1_xattn_in['ln_l_g'], 'L1_xattn_ln_l_b': _L1_xattn_in['ln_l_b'], 'L1_xattn_q_gamma': _L1_xattn_in['q_gamma'], 'L1_xattn_k_gamma': _L1_xattn_in['k_gamma'], 'L1_xattn_W_q': _L1_xattn_in['W_q'], 'L1_xattn_W_kv': _L1_xattn_in['W_kv'], 'L1_xattn_W_out': _L1_xattn_in['W_out'], 'L1_xattn_b_out': _L1_xattn_in['b_out'], 'L1_ffn_W1': _L1_ffn_in['W1'], 'L1_ffn_b1': _L1_ffn_in['b1'], 'L1_ffn_W3': _L1_ffn_in['W3'], 'L1_ffn_b3': _L1_ffn_in['b3'], 'L1_ffn_W2': _L1_ffn_in['W2'], 'L1_ffn_b2': _L1_ffn_in['b2'], 'L1_ffn_Wg': _L1_ffn_in['Wg'], 'L1_ffn_bg': _L1_ffn_in['bg'], 'L1_ffn_Wf': _L1_ffn_in['Wf'], 'L1_ffn_bf': _L1_ffn_in['bf'], 'L2_xattn_w_sim': _L2_xattn_in['w_sim'], 'L2_xattn_b_sim': _L2_xattn_in['b_sim'], 'L2_xattn_W_qv': _L2_xattn_in['W_qv'], 'L2_xattn_b_qv': _L2_xattn_in['b_qv'], 'L2_ffn_gate_w': _L2_ffn_in['gate_w'], 'L2_ffn_gate_b': _L2_ffn_in['gate_b'], 'L2_ffn_rms_w': _L2_ffn_in['rms_w'], 'L2_ffn_w1': _L2_ffn_in['w1'], 'L2_ffn_b1': _L2_ffn_in['b1'], 'L2_ffn_w2': _L2_ffn_in['w2'], 'L2_ffn_b2': _L2_ffn_in['b2'], 'L3_xattn_ln_g': _L3_xattn_in['ln_g'], 'L3_xattn_ln_b': _L3_xattn_in['ln_b'], 'L3_xattn_Wq': _L3_xattn_in['Wq'], 'L3_xattn_Wkv': _L3_xattn_in['Wkv'], 'L3_xattn_Wm': _L3_xattn_in['Wm'], 'L3_xattn_Wo': _L3_xattn_in['Wo'], 'L3_xattn_bo': _L3_xattn_in['bo'], 'L3_ffn_wg': _L3_ffn_in['wg'], 'L3_ffn_w1': _L3_ffn_in['w1'], 'L3_ffn_w2': _L3_ffn_in['w2'], 'L3_ffn_w3': _L3_ffn_in['w3'], 'L3_ffn_sw1': _L3_ffn_in['sw1'], 'L3_ffn_sw2': _L3_ffn_in['sw2'], 'L3_ffn_sw3': _L3_ffn_in['sw3']}

def reference(x, ctx_1024, mask_BxS2_bk0, g_xattn, g_ffn, L0_xattn_w_q, L0_xattn_w_k, L0_xattn_w_v, L0_ffn_Wr, L0_ffn_W1, L0_ffn_b1, L0_ffn_W2, L0_ffn_b2, L1_xattn_ln_x_g, L1_xattn_ln_x_b, L1_xattn_ln_l_g, L1_xattn_ln_l_b, L1_xattn_q_gamma, L1_xattn_k_gamma, L1_xattn_W_q, L1_xattn_W_kv, L1_xattn_W_out, L1_xattn_b_out, L1_ffn_W1, L1_ffn_b1, L1_ffn_W3, L1_ffn_b3, L1_ffn_W2, L1_ffn_b2, L1_ffn_Wg, L1_ffn_bg, L1_ffn_Wf, L1_ffn_bf, L2_xattn_w_sim, L2_xattn_b_sim, L2_xattn_W_qv, L2_xattn_b_qv, L2_ffn_gate_w, L2_ffn_gate_b, L2_ffn_rms_w, L2_ffn_w1, L2_ffn_b1, L2_ffn_w2, L2_ffn_b2, L3_xattn_ln_g, L3_xattn_ln_b, L3_xattn_Wq, L3_xattn_Wkv, L3_xattn_Wm, L3_xattn_Wo, L3_xattn_bo, L3_ffn_wg, L3_ffn_w1, L3_ffn_w2, L3_ffn_w3, L3_ffn_sw1, L3_ffn_sw2, L3_ffn_sw3):
    import jax
    import jax.numpy as jnp

    def _L0_xattn_ref(q, k, v, w_q, w_k, w_v):
        import jax, jax.numpy as jnp
        import numpy as np
        D_MODEL = 256
        query = jnp.einsum('bsd,od->bso', q, w_q)
        key_ = jnp.einsum('bsd,od->bso', k, w_k)
        value = jnp.einsum('bsd,od->bso', v, w_v)
        scores = jnp.einsum('bqd,bkd->bqk', query, key_) / jnp.sqrt(jnp.float32(D_MODEL))
        attn = jax.nn.softmax(scores, axis=-1)
        out = jnp.einsum('bqk,bkd->bqd', attn, value)
        return out

    def _L0_ffn_ref(hidden_states, Wr, W1, b1, W2, b2):
        import jax, jax.numpy as jnp
        import numpy as np
        B, S, D, E, F = (2, 512, 256, 8, 1024)
        b, s, d = hidden_states.shape
        e = Wr.shape[1]
        x = hidden_states.reshape(b * s, d)
        router_logits = x @ Wr
        router_probs = jax.nn.softmax(router_logits, axis=-1)
        expert_idx = jnp.argmax(router_probs, axis=-1)
        p_max = jnp.max(router_probs, axis=-1, keepdims=True)

        def expert_mlp(w1, bb1, w2, bb2):
            h = jax.nn.gelu(x @ w1 + bb1, approximate=False)
            return h @ w2 + bb2
        outs = jax.vmap(expert_mlp)(W1, b1, W2, b2)
        onehot = jax.nn.one_hot(expert_idx, e, dtype=x.dtype)
        next_states = jnp.einsum('te,etd->td', onehot, outs)
        out = p_max * next_states
        return out.reshape(b, s, d)

    def _L1_xattn_ref(x, latents, mask, ln_x_g, ln_x_b, ln_l_g, ln_l_b, q_gamma, k_gamma, W_q, W_kv, W_out, b_out):
        import jax, jax.numpy as jnp
        import numpy as np
        DIM = 256
        DIM_LATENT = 256
        DIM_HEAD = 64
        INNER = max(DIM, DIM_LATENT)
        HEADS = INNER // DIM_HEAD
        SCALE = DIM_HEAD ** (-0.5)
        LN_EPS = 1e-05
        RMS_EPS = 1e-08

        def layernorm(x, g, b):
            mu = jnp.mean(x, axis=-1, keepdims=True)
            var = jnp.mean(jnp.square(x - mu), axis=-1, keepdims=True)
            return (x - mu) * jax.lax.rsqrt(var + LN_EPS) * g + b

        def rmsnorm(x, gamma):
            n = jnp.linalg.norm(x, axis=-1, keepdims=True) * x.shape[-1] ** (-0.5)
            return x / jnp.maximum(n, RMS_EPS) * gamma
        b, n, _ = x.shape
        nl = latents.shape[1]
        xn = layernorm(x, ln_x_g, ln_x_b)
        ln = layernorm(latents, ln_l_g, ln_l_b)
        q = ln @ W_q
        kv = jnp.concatenate([xn @ W_kv, ln @ W_kv], axis=1)
        k, v = (kv[..., :INNER], kv[..., INNER:])
        to_heads = lambda t: t.reshape(t.shape[0], t.shape[1], HEADS, DIM_HEAD).transpose(0, 2, 1, 3)
        q, k, v = (to_heads(q), to_heads(k), to_heads(v))
        qn = rmsnorm(q, q_gamma) * SCALE
        kn = rmsnorm(k, k_gamma)
        sim = jnp.einsum('bhid,bhjd->bhij', qn, kn)
        full_mask = jnp.pad(mask, ((0, 0), (0, nl)), constant_values=True)
        neg = -jnp.finfo(sim.dtype).max
        sim = jnp.where(full_mask[:, None, None, :], sim, neg)
        attn = jax.nn.softmax(sim.astype(jnp.float32), axis=-1).astype(sim.dtype)
        out = jnp.einsum('bhij,bhjd->bhid', attn, v)
        out = out.transpose(0, 2, 1, 3).reshape(b, nl, INNER)
        return out @ W_out + b_out

    def _L1_ffn_ref(X, W1, b1, W3, b3, W2, b2, Wg, bg, Wf, bf):
        import jax, jax.numpy as jnp
        import numpy as np
        DIM = 256
        HID = 512
        OUT = 256
        NE = 8
        TOPK = 2

        def _xavier(key, shape):
            fan_in, fan_out = (shape[-2], shape[-1])
            lim = jnp.sqrt(6.0 / (fan_in + fan_out))
            return jax.random.uniform(key, shape, jnp.float32, -lim, lim)
        gating = jax.nn.softmax(X @ Wg + bg, axis=-1)
        top_k_indices = jnp.argsort(gating, axis=-1)[..., -TOPK:]
        h1 = jnp.einsum('bsd,edh->bseh', X, W1) + b1
        h3 = jnp.einsum('bsd,edh->bseh', X, W3) + b3
        h = jax.nn.silu(h1 * h3)
        expert_outputs = jnp.einsum('bseh,eho->bseo', h, W2) + b2
        topk_out = jnp.take_along_axis(expert_outputs, top_k_indices[..., None], axis=2)
        topk_w = jnp.take_along_axis(gating, top_k_indices, axis=-1)
        mixed = jnp.sum(topk_w[..., None] * topk_out, axis=2)
        return mixed @ Wf + bf

    def _L2_xattn_ref(encoder_hc, decoder_hq, w_sim, b_sim, W_qv, b_qv):
        import jax, jax.numpy as jnp
        import numpy as np
        B, L_ENC, L_DEC, D = (16, 128, 128, 256)
        d = encoder_hc.shape[-1]
        w1, w2, w3 = (w_sim[:d], w_sim[d:2 * d], w_sim[2 * d:])
        Sim = (encoder_hc @ w1)[:, :, None] + (decoder_hq @ w2)[:, None, :] + jnp.einsum('bid,bjd->bij', encoder_hc * w3, decoder_hq) + b_sim[0]
        A = jax.nn.softmax(Sim, axis=2)
        hq_hat = jnp.einsum('bij,bjd->bid', A, decoder_hq)
        Batt = jax.nn.softmax(jnp.max(Sim, axis=2), axis=1)
        hc_bar = jnp.einsum('bi,bid->bd', Batt, encoder_hc)[:, None, :]
        hc_hat = jnp.broadcast_to(hc_bar, encoder_hc.shape)
        feats = jnp.concatenate([encoder_hc, hq_hat, encoder_hc * hq_hat, encoder_hc * hc_hat], axis=-1)
        hcq = feats @ W_qv + b_qv
        return hcq

    def _L2_ffn_ref(x, gate_w, gate_b, rms_w, w1, b1, w2, b2):
        import jax, jax.numpy as jnp
        import numpy as np
        TEMPERATURE = 0.5
        CAPACITY_FACTOR = 1.25
        TOP_K = 1
        B, S, D = x.shape
        E = gate_w.shape[0]
        xf = x.reshape(-1, D)
        N = xf.shape[0]
        logits = xf @ gate_w.T + gate_b
        eps = jnp.finfo(logits.dtype).eps
        ms = jnp.mean(logits * logits, axis=-1, keepdims=True)
        logits = logits * jax.lax.rsqrt(ms + eps) * rms_w
        gates = jax.nn.softmax(logits / TEMPERATURE, axis=-1)
        g, idx = jax.lax.top_k(gates, TOP_K)
        g, idx = (g[:, 0], idx[:, 0])
        capacity = min(int(np.ceil(N * TOP_K / E * CAPACITY_FACTOR)), N)
        counts = jnp.zeros((E,), jnp.int32).at[idx].add(1)
        active = (counts > 0) & (capacity >= 1)
        mask = active[idx].astype(gates.dtype)
        masked = g * mask
        norm_g = masked / (masked + 1e-06)
        h = jax.nn.gelu(jnp.einsum('nd,edh->neh', xf, w1) + b1, approximate=False)
        y = jnp.einsum('neh,ehd->ned', h, w2) + b2
        out = (y * norm_g[:, None, None]).sum(axis=1)
        return out.reshape(B, S, D)

    def _L3_xattn_ref(x, memories, ln_g, ln_b, Wq, Wkv, Wm, Wo, bo):
        import jax, jax.numpy as jnp
        import numpy as np
        DIM = 256
        HEADS = 16
        DIM_HEAD = 64
        INNER = HEADS * DIM_HEAD
        EPS = 1e-05

        def _split_heads(t):
            b, n, _ = t.shape
            return t.reshape(b, n, HEADS, DIM_HEAD).transpose(0, 2, 1, 3)
        mu = jnp.mean(x, axis=-1, keepdims=True)
        var = jnp.mean(jnp.square(x - mu), axis=-1, keepdims=True)
        xn = (x - mu) * jax.lax.rsqrt(var + EPS) * ln_g + ln_b
        q = _split_heads(xn @ Wq)
        kv = xn @ Wkv
        k = _split_heads(kv[..., :INNER])
        v = _split_heads(kv[..., INNER:])
        mem = _split_heads(memories @ Wm)
        k = jnp.concatenate([k, mem], axis=2)
        v = jnp.concatenate([v, mem], axis=2)
        scale = DIM_HEAD ** (-0.5)
        dots = jnp.einsum('bhid,bhjd->bhij', q, k) * scale
        attn = jax.nn.softmax(dots, axis=-1)
        out = jnp.einsum('bhij,bhjd->bhid', attn, v)
        b, h, n, d = out.shape
        out = out.transpose(0, 2, 1, 3).reshape(b, n, h * d)
        return out @ Wo + bo

    def _L3_ffn_ref(x, wg, w1, w2, w3, sw1, sw2, sw3):
        import jax, jax.numpy as jnp
        import numpy as np
        DIM = 256
        INTER = 256
        E = 32
        K = 4
        G = 8
        LG = 4
        ROUTE_SCALE = 1.0
        CAP_FACTOR = 1.25
        B, S = (4, 512)

        def _gate(xf, wg):
            logits = xf @ wg.T
            scores = jax.nn.softmax(logits, axis=-1)
            sg = scores.reshape(-1, G, E // G)
            group_scores = sg.max(axis=-1)
            _, gtop = jax.lax.top_k(group_scores, LG)
            keep_g = jnp.sum(jax.nn.one_hot(gtop, G, dtype=jnp.float32), axis=1) > 0
            masked = jnp.where(keep_g[:, :, None], sg, -jnp.inf).reshape(-1, E)
            _, idx = jax.lax.top_k(masked, K)
            w = jnp.take_along_axis(scores, idx, axis=1)
            w = w / (w.sum(-1, keepdims=True) + 1e-09) * ROUTE_SCALE
            return (w.astype(xf.dtype), idx)

        def _forward(x, wg, w1, w2, w3, sw1, sw2, sw3):
            shape = x.shape
            xf = x.reshape(-1, DIM)
            N = xf.shape[0]
            cap = max(1, int(CAP_FACTOR * N * K / E))
            w, idx = _gate(xf, wg)
            fe = idx.reshape(-1)
            oh = jax.nn.one_hot(fe, E, dtype=jnp.int32)
            pos = (jnp.cumsum(oh, axis=0) * oh).sum(-1) - 1
            keep = pos < cap
            dest = jnp.where(keep, fe * cap + pos, E * cap)
            tok = jnp.arange(N * K, dtype=jnp.int32) // K
            buf_tok = jnp.full((E * cap + 1,), N, jnp.int32).at[dest].set(tok)[:-1]
            buf_w = jnp.zeros((E * cap + 1,), x.dtype).at[dest].set(w.reshape(-1))[:-1]
            xp = jnp.concatenate([xf, jnp.zeros((1, DIM), x.dtype)], axis=0)
            xe = xp[buf_tok].reshape(E, cap, DIM)
            h = jax.nn.silu(jnp.einsum('ecd,edh->ech', xe, w1)) * jnp.einsum('ecd,edh->ech', xe, w3)
            out = jnp.einsum('ech,ehd->ecd', h, w2) * buf_w.reshape(E, cap, 1)
            y = jnp.zeros((N + 1, DIM), x.dtype).at[buf_tok].add(out.reshape(E * cap, DIM))[:N]
            z = jax.nn.silu(xf @ sw1) * (xf @ sw3) @ sw2
            return (y + z).reshape(shape)
        return _forward(x, wg, w1, w2, w3, sw1, sw2, sw3)
    x = x + jnp.tanh(g_xattn[0]) * _L0_xattn_ref(_layernorm(x, axis=-1), ctx_1024, ctx_1024, L0_xattn_w_q, L0_xattn_w_k, L0_xattn_w_v)
    x = x + jnp.tanh(g_ffn[0]) * _L0_ffn_ref(_layernorm(x, axis=-1), L0_ffn_Wr, L0_ffn_W1, L0_ffn_b1, L0_ffn_W2, L0_ffn_b2)
    x = x + jnp.tanh(g_xattn[1]) * _L1_xattn_ref(ctx_1024, _layernorm(x, axis=-1), mask_BxS2_bk0, L1_xattn_ln_x_g, L1_xattn_ln_x_b, L1_xattn_ln_l_g, L1_xattn_ln_l_b, L1_xattn_q_gamma, L1_xattn_k_gamma, L1_xattn_W_q, L1_xattn_W_kv, L1_xattn_W_out, L1_xattn_b_out)
    x = x + jnp.tanh(g_ffn[1]) * _L1_ffn_ref(_layernorm(x, axis=-1), L1_ffn_W1, L1_ffn_b1, L1_ffn_W3, L1_ffn_b3, L1_ffn_W2, L1_ffn_b2, L1_ffn_Wg, L1_ffn_bg, L1_ffn_Wf, L1_ffn_bf)
    x = x + jnp.tanh(g_xattn[2]) * _L2_xattn_ref(_layernorm(x, axis=-1), ctx_1024, L2_xattn_w_sim, L2_xattn_b_sim, L2_xattn_W_qv, L2_xattn_b_qv)
    x = x + jnp.tanh(g_ffn[2]) * _L2_ffn_ref(_layernorm(x, axis=-1), L2_ffn_gate_w, L2_ffn_gate_b, L2_ffn_rms_w, L2_ffn_w1, L2_ffn_b1, L2_ffn_w2, L2_ffn_b2)
    x = x + jnp.tanh(g_xattn[3]) * _L3_xattn_ref(_layernorm(x, axis=-1), ctx_1024, L3_xattn_ln_g, L3_xattn_ln_b, L3_xattn_Wq, L3_xattn_Wkv, L3_xattn_Wm, L3_xattn_Wo, L3_xattn_bo)
    x = x + jnp.tanh(g_ffn[3]) * _L3_ffn_ref(_layernorm(x, axis=-1), L3_ffn_wg, L3_ffn_w1, L3_ffn_w2, L3_ffn_w3, L3_ffn_sw1, L3_ffn_sw2, L3_ffn_sw3)
    return x

_drawn_inputs = setup_inputs


def setup_inputs(seed=0):
    import zlib

    import numpy as np

    out = dict(_drawn_inputs(seed))
    spreads = {'L0_ffn_b1': (0.0, 0.1),
     'L0_ffn_b2': (0.0, 0.1),
     'L1_xattn_ln_x_g': (1.0, 0.6),
     'L1_xattn_ln_x_b': (0.0, 0.419),
     'L1_xattn_ln_l_g': (1.0, 0.2),
     'L1_xattn_ln_l_b': (0.0, 0.1),
     'L1_xattn_q_gamma': (1.0, 0.2),
     'L1_xattn_k_gamma': (1.0, 0.544),
     'L1_xattn_b_out': (0.0, 0.1),
     'L1_ffn_b1': (0.0, 0.1),
     'L1_ffn_b3': (0.0, 0.1),
     'L1_ffn_b2': (0.0, 0.1),
     'L1_ffn_bg': (0.0, 0.1),
     'L1_ffn_bf': (0.0, 0.1),
     'L2_ffn_gate_b': (0.0, 0.8),
     'L2_ffn_rms_w': (1.0, 0.6),
     'L2_ffn_b1': (0.0, 0.1),
     'L2_ffn_b2': (0.0, 0.1),
     'L3_xattn_ln_g': (1.0, 0.2),
     'L3_xattn_ln_b': (0.0, 0.1),
     'L3_xattn_bo': (0.0, 0.1)}
    factors = {'L2_ffn_gate_w': 8.0}
    for name, (base, spread) in spreads.items():
        noise = np.random.default_rng([zlib.crc32(name.encode()), seed]).standard_normal(out[name].shape)
        drawn = base * np.exp(spread * noise) if base else spread * noise
        out[name] = jnp.asarray(drawn.astype(out[name].dtype))
    for name, factor in factors.items():
        out[name] = (out[name] * factor).astype(out[name].dtype)
    return out
```

```python
from contextlib import ExitStack, contextmanager

import concourse.bass as bass
from concourse import mybir

F32 = mybir.dt.float32
F32R = mybir.dt.float32r
I32 = mybir.dt.int32
U32 = mybir.dt.uint32
ALU = mybir.AluOpType
ACT = mybir.ActivationFunctionType
AX = mybir.AxisListType

P = 128
BATCH, SEQ, D = 2, 1024, 256
TOKENS = BATCH * SEQ
TILES = TOKENS // P
BATCH_TILES = SEQ // P
DC = D // P
CTX = 154
CTX_REST = CTX - P
CHUNKS = ((0, P), (P, CTX_REST))
EPS = 1e-5
SLOTS = 4
TURN_BANKS = 2


class Steps:

    def __init__(self, engine, sem, first=0):
        self.engine, self.sem, self.first, self.n = engine, sem, first, 0

    def __call__(self, instruction):
        instruction.then_inc(self.sem, 1)
        self.wait()

    def wait(self):
        self.n += 1
        self.engine.wait_ge(self.sem, self.first + self.n)


def tile_of(tensor, t):
    return tensor[:, bass.ds(t, 1), :].rearrange("p a d -> p (a d)")


def expert(weights, e):
    return weights[bass.ds(e, 1), :, :].rearrange("a r c -> (a r) c")


def column(tensor, c):
    return tensor[:, bass.ds(c, 1)]



ROOT_STEPS = 12
NORM_STEPS = TILES + 6 + ROOT_STEPS


def inverse_root(dve, step, out, value, scale, eps, scratch):
    v, half = scratch
    step(dve.tensor_scalar(v, value, scale, eps, ALU.mult, ALU.add))
    step(dve.tensor_scalar(half.bitcast(I32), v.bitcast(I32), 1, None, ALU.logical_shift_right))
    step(dve.tensor_scalar(out.bitcast(I32), half.bitcast(I32), -1.0, float(0x5F3759DF), ALU.mult, ALU.add))
    for _ in range(3):
        step(dve.tensor_tensor(half, out, out, ALU.mult))
        step(dve.scalar_tensor_tensor(half, half, -0.5, v, ALU.mult, ALU.mult))
        step(dve.scalar_tensor_tensor(out, half, 1.5, out, ALU.add, ALU.mult))


def row_statistics(dve, chip, sem, first, source):
    with dve.Fori(0, TILES // 4) as i:
        for u in range(4):
            dve.bn_stats(tile_of(chip.stats, i * 4 + u), tile_of(source, i * 4 + u)).then_inc(sem, 1)
    dve.wait_ge(sem, first + TILES)
    aggregate(dve, sem, first + TILES, chip.stats[:], chip.mean[:], chip.inv_std[:],
              (chip.small_a[:], chip.small_b[:], chip.small_c[:]))


AGGREGATE_STEPS = 6 + ROOT_STEPS


def aggregate(dve, sem, first, stats, mean, inv_std, small):
    mean_even, m2_even, mean_odd, m2_odd = (stats[:, :, k] for k in (1, 2, 4, 5))
    a, b, c = small
    dve.tensor_tensor(mean, mean_even, mean_odd, ALU.add).then_inc(sem, 1)
    dve.tensor_tensor(a, mean_even, mean_odd, ALU.subtract).then_inc(sem, 1)
    dve.tensor_tensor(b, m2_even, m2_odd, ALU.add).then_inc(sem, 1)
    dve.wait_ge(sem, first + 3)
    step = Steps(dve, sem, first + 3)
    step(dve.tensor_scalar(mean, mean, 0.5, None, ALU.mult))
    step(dve.tensor_tensor(a, a, a, ALU.mult))
    step(dve.scalar_tensor_tensor(a, a, D / 4.0, b, ALU.mult, ALU.add))
    inverse_root(dve, step, inv_std, a, 1.0 / D, EPS, (b, c))


def normalize_dve(dve, chip, s, source):
    with dve.Fori(0, TILES // SLOTS) as i:
        for u in range(SLOTS):
            t = i * SLOTS + u
            dve.wait_ge(s.turned, t + 1)
            if s.copied is not None:
                dve.wait_ge(s.copied, t + 1)
            dve.tensor_scalar(chip.stage[:, u, :], tile_of(source, t), column(chip.mean, t),
                              column(chip.inv_std, t), ALU.subtract, ALU.mult).then_inc(s.staged, 1)


def normalize_pool(pool, chip, s):
    pool.sem_inc(s.copied, SLOTS)
    with pool.Fori(0, TILES // SLOTS) as i:
        for u in range(SLOTS):
            t = i * SLOTS + u
            pool.wait_ge(s.staged, t + 1)
            pool.tensor_copy(tile_of(chip.xn, t), chip.stage[:, u, :]).then_inc(s.copied, 1)


def turn_pe(pe, chip, s, psum):
    pe.sem_inc(s.turned, SLOTS)
    with pe.Fori(0, TILES // SLOTS) as i:
        for u in range(SLOTS):
            t = i * SLOTS + u
            pe.wait_ge(s.staged, t + 1)
            pe.wait_ge(s.turned_read, t + 1)
            for c in range(DC):
                ins = pe.transpose(psum[:, u % TURN_BANKS, c * P:(c + 1) * P], chip.stage[:, u, c * P:(c + 1) * P], chip.ident[:])
            ins.then_inc(s.turned, 1)


def turn_act(act, chip, s, psum, scale=None, bias=None):
    act.sem_inc(s.turned_read, TURN_BANKS)
    with act.Fori(0, TILES // SLOTS) as i:
        for u in range(SLOTS):
            t = i * SLOTS + u
            act.wait_ge(s.turned, t + (SLOTS + 1))
            if scale is None:
                act.copy(chip.xt[:, :, bass.ds(t * P, P)],
                         psum[:, u % TURN_BANKS, 0:D].rearrange("p (c t) -> p c t", c=DC)).then_inc(s.turned_read, 1)
            else:
                for c in range(DC):
                    ins = act.activation(chip.xt[:, c, bass.ds(t * P, P)], psum[:, u % TURN_BANKS, c * P:(c + 1) * P],
                                         ACT.Identity, bias=bias[:, c:c + 1], scale=scale[:, c:c + 1])
                ins.then_inc(s.turned_read, 1)


class TurnSemaphores:
    def __init__(self, sem, stage, keep=False):
        self.staged, self.turned, self.turned_read = sem(f"{stage}_staged"), sem(f"{stage}_turned"), sem(f"{stage}_turned_read")
        self.copied = sem(f"{stage}_copied") if keep else None


def scope(nc, stack, stage, clear=True):
    def sb(name, shape, dtype=F32):
        return stack.enter_context(nc.sbuf_tensor(f"{stage}_{name}", shape, dtype))

    def psum(name, shape, dtype=F32):
        return stack.enter_context(nc.psum_tensor(f"{stage}_{name}", shape, dtype))

    semaphores = []

    def sem(name):
        semaphores.append(nc.alloc_semaphore(name=f"{stage}_{name}"))
        return semaphores[-1]

    def release():
        nc.all_engine_barrier()
        nc.clear_and_free_semaphores(semaphores)
        nc.all_engine_barrier()

    if clear:
        stack.callback(release)
    return sb, psum, sem



class Chip:
    def __init__(self, nc, stack):
        sb, _, _ = scope(nc, stack, "chip", clear=False)
        self.x = sb("x", [P, TILES, D])
        self.xt = sb("xt", [P, DC, TOKENS])
        self.stage = sb("stage", [P, SLOTS, D])
        self.stats = sb("stats", [P, TILES, 6])
        self.mean = sb("mean", [P, TILES])
        self.inv_std = sb("inv_std", [P, TILES])
        self.small_a = sb("small_a", [P, TILES])
        self.small_b = sb("small_b", [P, TILES])
        self.small_c = sb("small_c", [P, TILES])
        self.xn = sb("xn", [P, TILES, D])
        self.before = sb("before", [P, P])
        self.ident = sb("ident", [P, P])
        self.ones = sb("ones", [P, P])
        self.gates = sb("gates", [P, 8])
        self.ctx = sb("ctx", [P, BATCH, 2, D])
        self.ctxt = sb("ctxt", [P, DC, BATCH * CTX])


def setup(nc, chip, I):
    with ExitStack() as stack:
        sb, psum, sem = scope(nc, stack, "setup")
        turned = psum("turned", [P, 4, 512])
        loaded, made, ident_made, ctx_turned, ctx_kept, tanh_done = (
            sem(n) for n in ("loaded", "made", "ident_made", "ctx_turned", "ctx_kept", "tanh_done"))
        block = stack.enter_context(nc.Block())

        @block.sync
        def _(sp):
            for b in range(BATCH):
                for c, (row, rows) in enumerate(CHUNKS):
                    sp.dma_start(chip.ctx[0:rows, b, c, :], I["ctx_1024"][b, row:row + rows, :]).then_inc(loaded, 16)
            sp.dma_start(chip.x[:], I["x"].rearrange("b (t p) d -> p (b t) d", p=P)).then_inc(loaded, 16)
            sp.dma_start(chip.gates[:, 0:4], I["g_xattn"].partition_broadcast(P)).then_inc(loaded, 16)
            sp.dma_start(chip.gates[:, 4:8], I["g_ffn"].partition_broadcast(P)).then_inc(loaded, 16)

        @block.gpsimd
        def _(pool):
            pool.memset(chip.ones[:], 1.0).then_inc(made, 1)
            pool.wait_ge(made, 1)
            pool.affine_select(out=chip.ident[:], in_=chip.ones[:], compare_op=ALU.is_equal, fill=0.0,
                               base=0, pattern=[[-1, P]], channel_multiplier=1).then_inc(ident_made, 1)
            pool.affine_select(out=chip.before[:], in_=chip.ones[:], compare_op=ALU.is_gt, fill=0.0,
                               base=0, pattern=[[1, P]], channel_multiplier=-1).then_inc(ident_made, 1)

        @block.tensor
        def _(pe):
            pe.wait_ge(ident_made, 1)
            pe.wait_ge(loaded, 7 * 16)
            for b in range(BATCH):
                for c, (row, rows) in enumerate(CHUNKS):
                    for d in range(DC):
                        ins = pe.transpose(turned[:, b * 2 + c, d * P:d * P + rows],
                                           chip.ctx[0:rows, b, c, d * P:(d + 1) * P], chip.ident[0:rows, 0:rows])
            ins.then_inc(ctx_turned, 1)

        @block.vector
        def _(dve):
            dve.wait_ge(ctx_turned, 1)
            for b in range(BATCH):
                for c, (row, rows) in enumerate(CHUNKS):
                    at = b * CTX + row
                    dve.tensor_copy(chip.ctxt[:, :, at:at + rows],
                                    turned[:, b * 2 + c, 0:D].rearrange("p (d r) -> p d r", d=DC)[:, :, 0:rows]
                                    ).then_inc(ctx_kept, 1)

        @block.scalar
        def _(act):
            act.wait_ge(loaded, 7 * 16)
            act.activation(chip.gates[:], chip.gates[:], ACT.Tanh).then_inc(tanh_done, 1)



def l0_attention(nc, chip, I):
    with ExitStack() as stack:
        sb, psum, sem = scope(nc, stack, "l0a")
        wq, wk, wv = (sb(n, [P, DC, D]) for n in ("wq", "wk", "wv"))
        wvt, wqk_t = sb("wvt", [P, DC, D]), sb("wqk_t", [P, DC, D])
        keys = sb("keys", [P, DC, BATCH * CTX])
        values = sb("values", [P, BATCH, 2, D])
        xt = sb("xt", [P, 2, DC, P])
        probs = sb("probs", [P, 2, CTX])
        probs_t = sb("probs_t", [P, 2, 2, P])
        neg_max, total, factor = sb("neg_max", [P, 2]), sb("total", [P, 2]), sb("factor", [P, 2])
        pa = psum("pa", [P, 2, 512])
        pb = psum("pb", [P, 2, 512])
        pc = psum("pc", [P, 2, 512])
        pd = psum("pd", [P, 2, 512])
        w_loaded, wv_turned, wv_kept, wqk_done, wqk_kept, keys_done, keys_kept = (sem(n) for n in (
            "w_loaded", "wv_turned", "wv_kept", "wqk_done", "wqk_kept", "keys_done", "keys_kept"))
        values_done, values_kept, norm_steps, staged, turned, xt_kept = (sem(n) for n in (
            "values_done", "values_kept", "norm_steps", "staged", "turned", "xt_kept"))
        scored, maxed, exped, probs_turned, probs_kept, out_done, dve_steps = (sem(n) for n in (
            "scored", "maxed", "exped", "probs_turned", "probs_kept", "out_done", "dve_steps"))
        block = stack.enter_context(nc.Block())

        @block.sync
        def _(sp):
            for w, name in ((wv, "L0_xattn_w_v"), (wk, "L0_xattn_w_k"), (wq, "L0_xattn_w_q")):
                sp.dma_start(w[:], I[name].rearrange("(c p) d -> p c d", p=P)).then_inc(w_loaded, 16)

        @block.tensor
        def _(pe):
            pe.wait_ge(w_loaded, 48)
            for o in range(DC):
                for d in range(DC):
                    ins = pe.transpose(pa[:, d, o * P:(o + 1) * P], wv[:, o, d * P:(d + 1) * P], chip.ident[:])
            ins.then_inc(wv_turned, 1)
            for d in range(DC):
                for o in range(DC):
                    ins = pe.matmul(pb[:, d, 0:D], wk[:, o, d * P:(d + 1) * P], wq[:, o, :], start=o == 0, stop=o == DC - 1)
            ins.then_inc(wqk_done, 1)
            pe.wait_ge(wqk_kept, 1)
            for d in range(DC):
                for e in range(DC):
                    ins = pe.matmul(pc[:, d, 0:BATCH * CTX], wqk_t[:, e, d * P:(d + 1) * P], chip.ctxt[:, e, :],
                                    start=e == 0, stop=e == DC - 1)
            ins.then_inc(keys_done, 1)
            pe.wait_ge(wv_kept, 1)
            for b in range(BATCH):
                for c, (row, rows) in enumerate(CHUNKS):
                    at = b * CTX + row
                    for d in range(DC):
                        ins = pe.matmul(pd[0:rows, b, c * D:(c + 1) * D], chip.ctxt[:, d, at:at + rows], wvt[:, d, :],
                                        start=d == 0, stop=d == DC - 1)
            ins.then_inc(values_done, 1)
            pe.wait_ge(keys_kept, 1)
            pe.wait_ge(values_kept, 2 * BATCH)
            with pe.Fori(0, BATCH_TILES) as i:
                for u in range(BATCH):
                    pe.wait_ge(staged, i * 2 + (u + 1))
                    for c in range(DC):
                        ins = pe.transpose(pa[:, u, c * P:(c + 1) * P], chip.stage[:, u, c * P:(c + 1) * P], chip.ident[:])
                    ins.then_inc(turned, 1)
                for u in range(BATCH):
                    pe.wait_ge(xt_kept, i * 2 + (u + 1))
                    for c in range(DC):
                        ins = pe.matmul(pb[:, u, 0:CTX], xt[:, u, c, :], keys[:, c, u * CTX:(u + 1) * CTX],
                                        start=c == 0, stop=c == DC - 1)
                    ins.then_inc(scored, 1)
                for u in range(BATCH):
                    pe.wait_ge(exped, i * 2 + (u + 1))
                    for c, (row, rows) in enumerate(CHUNKS):
                        ins = pe.transpose(pc[0:rows, u, c * P:(c + 1) * P], probs[:, u, row:row + rows], chip.ident[:])
                    ins.then_inc(probs_turned, 1)
                for u in range(BATCH):
                    pe.wait_ge(probs_kept, i * 4 + (2 * u + 2))
                    for c, (row, rows) in enumerate(CHUNKS):
                        ins = pe.matmul(pd[:, u, 0:D], probs_t[0:rows, u, c, :], values[0:rows, u, c, :],
                                        start=c == 0, stop=c == 1)
                    ins.then_inc(out_done, 1)

        @block.scalar
        def _(act):
            act.wait_ge(wqk_done, 1)
            act.copy(wqk_t[:], pb[:, :, 0:D]).then_inc(wqk_kept, 1)
            act.wait_ge(keys_done, 1)
            act.mul(keys[:], pc[:, :, 0:BATCH * CTX], D ** -0.5).then_inc(keys_kept, 1)
            with act.Fori(0, BATCH_TILES) as i:
                for u in range(BATCH):
                    act.wait_ge(turned, i * 2 + (u + 1))
                    act.copy(xt[:, u, :, :], pa[:, u, 0:D].rearrange("p (c t) -> p c t", c=DC)).then_inc(xt_kept, 1)
                for u in range(BATCH):
                    act.wait_ge(maxed, i * 2 + (u + 1))
                    act.activation(probs[:, u, :], pb[:, u, 0:CTX], ACT.Exp, bias=neg_max[:, u:u + 1],
                                   accum_out=total[:, u:u + 1]).then_inc(exped, 1)

        @block.vector
        def _(dve):
            row_statistics(dve, chip, norm_steps, 0, chip.x)
            dve.wait_ge(wv_turned, 1)
            dve.tensor_copy(wvt[:], pa[:, :, 0:D]).then_inc(wv_kept, 1)
            dve.wait_ge(values_done, 1)
            for b in range(BATCH):
                for c, (row, rows) in enumerate(CHUNKS):
                    dve.tensor_copy(values[0:rows, b, c, :], pd[0:rows, b, c * D:(c + 1) * D]).then_inc(values_kept, 1)
            with dve.Fori(0, BATCH_TILES) as i:
                for u in range(BATCH):
                    t = i + u * BATCH_TILES
                    dve.tensor_scalar(chip.stage[:, u, :], tile_of(chip.x, t), column(chip.mean, t),
                                      column(chip.inv_std, t), ALU.subtract, ALU.mult).then_inc(staged, 1)
                for u in range(BATCH):
                    dve.wait_ge(scored, i * 2 + (u + 1))
                    dve.tensor_reduce(neg_max[:, u:u + 1], pb[:, u, 0:CTX], AX.X, ALU.max, negate=True).then_inc(maxed, 1)
                for u in range(BATCH):
                    dve.wait_ge(probs_turned, i * 2 + (u + 1))
                    for c, (row, rows) in enumerate(CHUNKS):
                        dve.tensor_copy(probs_t[0:rows, u, c, :], pc[0:rows, u, c * P:(c + 1) * P]).then_inc(probs_kept, 1)
                for u in range(BATCH):
                    t = i + u * BATCH_TILES
                    step = Steps(dve, dve_steps, i * 6 + 3 * u)
                    step(dve.reciprocal(factor[:, u:u + 1], total[:, u:u + 1]))
                    step(dve.tensor_scalar(factor[:, u:u + 1], factor[:, u:u + 1], chip.gates[:, 0:1], None, ALU.mult))
                    dve.wait_ge(out_done, i * 2 + (u + 1))
                    step(dve.scalar_tensor_tensor(tile_of(chip.x, t), pd[:, u, 0:D], factor[:, u:u + 1], tile_of(chip.x, t),
                                                  ALU.mult, ALU.add))



def spread(ap, n):
    return ap.unsqueeze(2).to_broadcast([ap.shape[0], ap.shape[1], n])


def choose(dve, step, scores, onehot, order, value, best, drop):
    n = scores.shape[2]
    step(dve.tensor_reduce(value, scores, AX.X, ALU.max))
    step(dve.tensor_tensor(onehot, scores, spread(value, n), ALU.is_equal))
    step(dve.tensor_tensor(onehot, onehot, order, ALU.mult))
    step(dve.tensor_reduce(best, onehot, AX.X, ALU.max))
    step(dve.tensor_tensor(onehot, onehot, spread(best, n), ALU.is_equal))
    if drop:
        step(dve.scalar_tensor_tensor(scores, onehot, -drop, scores, ALU.mult, ALU.add))


def rank_pe(pe, chip, chosen, within, total):
    rhs = chosen.rearrange("p t e -> p e t")
    pe.matmul(within, chip.before[:], rhs, start=True, stop=True)
    return pe.matmul(total, chip.ones[:], rhs, start=True, stop=True)


def ranks_dve(dve, step, rank, upto, within, total, restart):
    flat = "p e t -> p (e t)"
    step(dve.tensor_tensor_scan(upto.rearrange(flat), restart.rearrange(flat), total.rearrange(flat), 0.0, ALU.mult, ALU.add))
    step(dve.tensor_tensor(rank, within, upto, ALU.add))
    step(dve.tensor_tensor(rank, rank, total, ALU.subtract))


def slots_dve(dve, step, slot, onehot, product, place, index):
    step(dve.tensor_tensor(product, onehot, slot.rearrange("p e t -> p t e"), ALU.mult))
    step(dve.tensor_reduce(place, product, AX.X, ALU.add))
    step(dve.tensor_copy(index, place))


def expert_bases(dve, step, ones, rank, upto, compare, thresholds, tiles, ends, tile_counts):
    experts = tiles.shape[1]
    step(dve.tensor_tensor(compare, spread(upto[:, :, TILES - 1], TILES), thresholds, ALU.is_gt))
    step(dve.tensor_reduce(tiles, compare, AX.X, ALU.add))
    step(dve.tensor_scalar(tiles, tiles, 1.0, None, ALU.max))
    step(dve.tensor_copy(tile_counts, tiles))
    step(dve.tensor_tensor_scan(ends, ones[:, 0:experts], tiles, 0.0, ALU.mult, ALU.add))
    step(dve.tensor_tensor(ends, ends, tiles, ALU.subtract))
    step(dve.scalar_tensor_tensor(rank, spread(ends, TILES), float(P), rank, ALU.mult, ALU.add))


def routing_constants(pool, sem, order, restart, thresholds, ascending):
    experts = order.shape[2]
    step = 1 if ascending else -1
    pool.iota(order, [[0, TILES], [step, experts]], base=1 if ascending else experts, channel_multiplier=0,
              allow_small_or_imprecise_dtypes=True).then_inc(sem, 1)
    if thresholds is not None:
        pool.iota(thresholds, [[0, experts], [P, TILES]], base=0, channel_multiplier=0,
                  allow_small_or_imprecise_dtypes=True).then_inc(sem, 1)
    pool.iota(restart, [[0, experts], [1, TILES]], base=0, channel_multiplier=0,
              allow_small_or_imprecise_dtypes=True).then_inc(sem, 1)


@contextmanager
def tiles_of_expert(engine, tile_counts, e, g, max_tiles):
    n = engine.value_load(tile_counts[0:1, bass.ds(e, 1)], min_val=1, max_val=TILES)
    with engine.Fori(0, n):
        yield engine.snap(g, min_val=0, max_val=max_tiles - 1)
        engine.reg_add(g, g, 1)


def zero_register(engine, name):
    g = engine.alloc_register(name)
    engine.reg_mov(g, 0)
    return g



def l0_ffn(nc, chip, I):
    E, F = 8, 1024
    FC = F // P
    HB = 4
    CB = FC // HB
    MAX_TILES = TILES + E - 1
    slots_x = nc.dram_tensor("l0f_slots_x", [MAX_TILES * P, D], F32, kind="Internal").ap()
    slots_y = nc.dram_tensor("l0f_slots_y", [MAX_TILES * P, D], F32, kind="Internal").ap()
    with ExitStack() as stack:
        sb, psum, sem = scope(nc, stack, "l0f")
        wr = sb("wr", [P, DC, E])
        w1, w2 = sb("w1", [P, 2, DC, F]), sb("w2", [P, 2, FC, D])
        b1_rows, b1 = sb("b1_rows", [E * FC, P]), sb("b1", [P, E * FC])
        b2 = sb("b2", [P, E, D])
        zeros = sb("zeros", [P, 2048])
        logits, exps, chosen, product = (sb(n, [P, TILES, E]) for n in ("logits", "exps", "chosen", "product"))
        order = sb("order", [P, TILES, E])
        restart, thresholds, rank, upto, compare = (sb(n, [P, E, TILES]) for n in ("restart", "thresholds", "rank", "upto", "compare"))
        best, weight, place = (sb(n, [P, TILES]) for n in ("best", "weight", "place"))
        tiles, ends = sb("tiles", [P, E]), sb("ends", [P, E])
        tile_counts, index = sb("tile_counts", [P, E], I32), sb("index", [P, TILES], I32)
        x_tile, xt_tile = sb("x_tile", [P, D]), sb("xt_tile", [P, D])
        hidden, y_tile = sb("hidden", [P, FC, P]), sb("y_tile", [P, D])
        fetched = sb("fetched", [P, TILES, D])
        p_route = psum("p_route", [P, 512])
        p_xt = psum("p_xt", [P, 512])
        p_hidden = psum("p_hidden", [P, HB, 512])
        p_y = psum("p_y", [P, 512])
        turn = TurnSemaphores(sem, "t", keep=True)
        (loaded, b_loaded, b2_loaded, zeroed, cleared, constants, norm_steps, b1_turned, b1_kept, routed, exped, chose, ranked, route_steps,
         placed, scattered, x_loaded, x_turned, x_kept, h_done, h_kept, y_done, y_kept, y_stored, added, passed) = (sem(n) for n in (
            "loaded", "b_loaded", "b2_loaded", "zeroed", "cleared", "constants", "norm_steps", "b1_turned", "b1_kept", "routed", "exped", "chose", "ranked",
            "route_steps", "placed", "scattered", "x_loaded", "x_turned", "x_kept", "h_done", "h_kept", "y_done", "y_kept",
            "y_stored", "added", "passed"))
        gathered = [sem(f"gathered{q}") for q in range(TILES // 4)]
        w_loaded = [sem("w_loaded0"), sem("w_loaded1")]
        block = stack.enter_context(nc.Block())
        CLEARS = 2 * -(-MAX_TILES // 8)

        def load_expert(engine, e, u):
            engine.dma_start(w1[:, u, :, :], expert(I["L0_ffn_W1"], e).rearrange("(c p) f -> p c f", p=P)).then_inc(w_loaded[u], 16)
            engine.dma_start(w2[:, u, :, :], expert(I["L0_ffn_W2"], e).rearrange("(c p) d -> p c d", p=P)).then_inc(w_loaded[u], 16)

        @block.sync
        def _(sp):
            sp.dma_start(wr[:], I["L0_ffn_Wr"].rearrange("(c p) e -> p c e", p=P)).then_inc(loaded, 16)
            sp.dma_start(b1_rows[:], I["L0_ffn_b1"].rearrange("e (c p) -> (e c) p", p=P)).then_inc(b_loaded, 16)
            sp.wait_ge(zeroed, 1)
            for slots in (slots_x, slots_y):
                for t in range(0, MAX_TILES, 8):
                    n = min(8, MAX_TILES - t)
                    sp.dma_start(slots[t * P:(t + n) * P, :].rearrange("(p n) d -> p (n d)", p=P), zeros[:, 0:n * D]).then_inc(cleared, 16)
            for u in range(2):
                load_expert(sp, u, u)
            sp.dma_start(b2[:], I["L0_ffn_b2"].partition_broadcast(P)).then_inc(b2_loaded, 16)
            sp.wait_ge(placed, 1)
            sp.wait_ge(scattered, 16 * TILES)
            g = zero_register(sp, "l0f_sp_g")
            with sp.Fori(0, E) as e:
                with tiles_of_expert(sp, tile_counts, e, g, MAX_TILES) as at:
                    sp.wait_ge(x_turned, at)
                    sp.dma_start(x_tile[:], slots_x[bass.ds(at * P, P), :]).then_inc(x_loaded, 16)

        @block.gpsimd
        def _(pool):
            pool.memset(zeros[:], 0.0).then_inc(zeroed, 1)
            routing_constants(pool, constants, order[:], restart[:], thresholds[:], ascending=False)
            normalize_pool(pool, chip, turn)
            pool.wait_ge(placed, 1)
            pool.wait_ge(turn.copied, SLOTS + TILES)
            pool.wait_ge(cleared, 16 * CLEARS)
            for t in range(TILES):
                pool.indirect_dma_start(slots_x, bass.IndirectOffsetOnAxis(index[:, t:t + 1], 0), chip.xn[:, t, :], None
                                        ).then_inc(scattered, 16)
            g = zero_register(pool, "l0f_pool_g")
            with pool.Fori(0, E) as e:
                with tiles_of_expert(pool, tile_counts, e, g, MAX_TILES) as at:
                    pool.wait_ge(y_kept, at + 1)
                    pool.dma_start(slots_y[bass.ds(at * P, P), :], y_tile[:]).then_inc(y_stored, 16)
            last = pool.snap(g, min_val=0, max_val=MAX_TILES)
            pool.wait_ge(y_stored, last * 16)
            pool.sem_inc(passed, 1)
            for t in range(TILES):
                pool.indirect_dma_start(fetched[:, t, :], None, slots_y, bass.IndirectOffsetOnAxis(index[:, t:t + 1], 0)
                                        ).then_inc(gathered[t // 4], 16)

        @block.tensor
        def _(pe):
            pe.wait_ge(b_loaded, 16)
            pe.transpose(p_y[:, 0:E * FC], b1_rows[:], chip.ident[0:E * FC, 0:E * FC]).then_inc(b1_turned, 1)
            turn_pe(pe, chip, turn, p_hidden)
            pe.wait_ge(loaded, 16)
            for t in range(TILES):
                pe.wait_ge(turn.turned_read, TURN_BANKS + t + 1)
                for c in range(DC):
                    ins = pe.matmul(p_route[:, t * E:(t + 1) * E], chip.xt[:, c, t * P:(t + 1) * P], wr[:, c, :],
                                    start=c == 0, stop=c == DC - 1)
            ins.then_inc(routed, 1)
            pe.wait_ge(chose, 1)
            rank_pe(pe, chip, chosen[:], p_route[:, 128:256].rearrange("p (e t) -> p e t", e=E),
                    p_route[:, 256:384].rearrange("p (e t) -> p e t", e=E)).then_inc(ranked, 1)
            pe.wait_ge(placed, 1)
            g = zero_register(pe, "l0f_pe_g")
            with pe.Fori(0, E // 2) as i:
                for u in range(2):
                    pe.wait_ge(w_loaded[u], i * 32 + 32)
                    pe.sem_inc(passed, 1)
                    with tiles_of_expert(pe, tile_counts, i * 2 + u, g, MAX_TILES) as at:
                        pe.wait_ge(x_loaded, at * 16 + 16)
                        pe.wait_ge(x_kept, at)
                        for c in range(DC):
                            ins = pe.transpose(p_xt[:, c * P:(c + 1) * P], x_tile[:, c * P:(c + 1) * P], chip.ident[:])
                        ins.then_inc(x_turned, 1)
                        pe.wait_ge(x_kept, at + 1)
                        for f in range(FC):
                            pe.wait_ge(h_kept, at * FC)
                            for c in range(DC):
                                ins = pe.matmul(p_hidden[:, f // CB, (f % CB) * P:(f % CB + 1) * P], w1[:, u, c, f * P:(f + 1) * P], xt_tile[:, c * P:(c + 1) * P],
                                                start=c == 0, stop=c == DC - 1)
                            ins.then_inc(h_done, 1)
                        pe.wait_ge(y_kept, at)
                        for f in range(FC):
                            pe.wait_ge(h_kept, at * FC + (f + 1))
                            ins = pe.matmul(p_y[:, 0:D], hidden[:, f, :], w2[:, u, f, :], start=f == 0, stop=f == FC - 1)
                        ins.then_inc(y_done, 1)

        @block.scalar
        def _(act):
            turn_act(act, chip, turn, p_hidden)
            act.wait_ge(route_steps, 2)
            act.activation(exps[:], logits[:], ACT.Exp).then_inc(exped, 1)
            act.wait_ge(placed, 1)
            act.wait_ge(b1_kept, 1)
            g = zero_register(act, "l0f_act_g")

            def run_expert(e, u, reload):
                with tiles_of_expert(act, tile_counts, e, g, MAX_TILES) as at:
                    act.wait_ge(y_done, at)
                    for f in range(FC):
                        act.wait_ge(h_done, at * FC + (f // CB + 1) * CB)
                        act.activation(hidden[:, f, :], p_hidden[:, f // CB, (f % CB) * P:(f % CB + 1) * P], ACT.Gelu,
                                       bias=column(b1, e * FC + f)).then_inc(h_kept, 1)
                if reload:
                    done = act.snap(g, min_val=0, max_val=MAX_TILES)
                    act.wait_ge(y_done, done)
                    load_expert(act, e + 2, u)

            with act.Fori(0, E // 2 - 1) as i:
                for u in range(2):
                    run_expert(i * 2 + u, u, True)
            for u in range(2):
                run_expert(E - 2 + u, u, False)

        @block.vector
        def _(dve):
            row_statistics(dve, chip, norm_steps, 0, chip.x)
            normalize_dve(dve, chip, turn, chip.x)
            dve.wait_ge(b1_turned, 1)
            dve.tensor_copy(b1[:], p_y[:, 0:E * FC]).then_inc(b1_kept, 1)
            dve.wait_ge(routed, 1)
            step = Steps(dve, route_steps)
            p_logits = p_route[:, 0:TILES * E].rearrange("p (t e) -> p t e", e=E)
            step(dve.tensor_reduce(best[:], p_logits, AX.X, ALU.max))
            step(dve.tensor_tensor(logits[:], p_logits, spread(best[:], E), ALU.subtract))
            dve.wait_ge(exped, 1)
            step(dve.tensor_reduce(weight[:], exps[:], AX.X, ALU.add))
            step(dve.reciprocal(weight[:], weight[:]))
            step(dve.tensor_scalar(weight[:], weight[:], chip.gates[:, 4:5], None, ALU.mult))
            dve.wait_ge(constants, 3)
            step(dve.tensor_scalar(restart[:], restart[:], 0.0, None, ALU.is_gt))
            choose(dve, step, exps[:], chosen[:], order[:], place[:], best[:], 0)
            dve.sem_inc(chose, 1)
            dve.wait_ge(ranked, 1)
            within, total = (p_route[:, a:a + E * TILES].rearrange("p (e t) -> p e t", e=E) for a in (128, 256))
            ranks_dve(dve, step, rank[:], upto[:], within, total, restart[:])
            expert_bases(dve, step, chip.ones, rank[:], upto[:], compare[:], thresholds[:], tiles[:], ends[:], tile_counts[:])
            slots_dve(dve, step, rank[:], chosen[:], product[:], place[:], index[:])
            dve.sem_inc(placed, 1)
            dve.wait_ge(b2_loaded, 16)
            g = zero_register(dve, "l0f_dve_g")
            with dve.Fori(0, E) as e:
                with tiles_of_expert(dve, tile_counts, e, g, MAX_TILES) as at:
                    dve.wait_ge(x_turned, at + 1)
                    dve.wait_ge(h_done, at * FC)
                    dve.tensor_copy(xt_tile[:], p_xt[:, 0:D]).then_inc(x_kept, 1)
                    dve.wait_ge(y_done, at + 1)
                    dve.wait_ge(y_stored, at * 16)
                    dve.tensor_tensor(y_tile[:], p_y[:, 0:D], tile_of(b2, e), ALU.add).then_inc(y_kept, 1)
            for q in range(TILES // 4):
                dve.wait_ge(gathered[q], 64)
                for t in range(4 * q, 4 * q + 4):
                    dve.scalar_tensor_tensor(chip.x[:, t, :], fetched[:, t, :], weight[:, t:t + 1], chip.x[:, t, :],
                                             ALU.mult, ALU.add).then_inc(added, 1)



def l1_ffn(nc, chip, I):
    E, F, K = 8, 512, 2
    FC = F // P
    MAX_TILES = K * TILES + E - 1
    slots_x = nc.dram_tensor("l1f_slots_x", [MAX_TILES * P, D], F32, kind="Internal").ap()
    slots_y = nc.dram_tensor("l1f_slots_y", [MAX_TILES * P, D], F32, kind="Internal").ap()
    with ExitStack() as stack:
        sb, psum, sem = scope(nc, stack, "l1f")
        wg, wf = sb("wg", [P, DC, E]), sb("wf", [P, DC, D])
        w1, w3, w2 = sb("w1", [P, 2, DC, F]), sb("w3", [P, 2, DC, F]), sb("w2", [P, 2, FC, D])
        b13_rows, b13 = sb("b13_rows", [2 * E * FC, P]), sb("b13", [P, 2 * E * FC])
        b2, bg, bf = sb("b2", [P, E, D]), sb("bg", [P, E]), sb("bf", [1, D])
        zeros = sb("zeros", [P, 2048])
        logits, exps, chosen, product = (sb(n, [P, TILES, E]) for n in ("logits", "exps", "chosen", "product"))
        picked = [sb(f"picked{k}", [P, TILES, E]) for k in range(K)]
        order = sb("order", [P, TILES, E])
        restart, thresholds, rank, upto, compare = (sb(n, [P, E, TILES]) for n in ("restart", "thresholds", "rank", "upto", "compare"))
        best, total, place = (sb(n, [P, TILES]) for n in ("best", "total", "place"))
        weight = [sb(f"weight{k}", [P, TILES]) for k in range(K)]
        tiles, ends = sb("tiles", [P, E]), sb("ends", [P, E])
        tile_counts = sb("tile_counts", [P, E], I32)
        index = [sb(f"index{k}", [P, TILES], I32) for k in range(K)]
        x_tile, xt_tile = sb("x_tile", [P, D]), sb("xt_tile", [P, D])
        h3, h13, hidden, y_tile = sb("h3", [P, FC, P]), sb("h13", [P, FC, P]), sb("hidden", [P, FC, P]), sb("y_tile", [P, D])
        fetched = [sb(f"fetched{k}", [P, TILES, D]) for k in range(K)]
        mixed, mixed_t = sb("mixed", [P, 4, D]), sb("mixed_t", [P, 4, D])
        p_route = psum("p_route", [P, 512])
        p_xt = psum("p_xt", [P, 512])
        p_h = psum("p_h", [P, 4, 512])
        p_y = psum("p_y", [P, 512])
        turn = TurnSemaphores(sem, "t", keep=True)
        (loaded, b_loaded, b2_loaded, zeroed, cleared, constants, norm_steps, b_turned, b_kept, routed, exped, chose, ranked,
         route_steps, placed, scattered, x_loaded, x_turned, x_kept, h_done, h3_kept, h13_kept, h_kept, y_done, y_kept,
         y_stored, passed, mix_steps, mixed_turned, mixed_kept, out_done, added) = (sem(n) for n in (
            "loaded", "b_loaded", "b2_loaded", "zeroed", "cleared", "constants", "norm_steps", "b_turned", "b_kept", "routed", "exped",
            "chose", "ranked", "route_steps", "placed", "scattered", "x_loaded", "x_turned", "x_kept", "h_done",
            "h3_kept", "h13_kept", "h_kept", "y_done", "y_kept", "y_stored", "passed", "mix_steps", "mixed_turned",
            "mixed_kept", "out_done", "added"))
        w_loaded = [sem("w_loaded0"), sem("w_loaded1")]
        gathered = [sem(f"gathered{q}") for q in range(TILES // 4)]
        block = stack.enter_context(nc.Block())
        CLEARS = 2 * -(-MAX_TILES // 8)

        def add_output(dve, t):
            dve.wait_ge(out_done, t + 1)
            dve.scalar_tensor_tensor(chip.x[:, t, :], p_h[:, 2 + t % 2, 0:D], chip.gates[:, 5:6], chip.x[:, t, :],
                                     ALU.mult, ALU.add).then_inc(added, 1)

        def load_expert(engine, e, u):
            engine.dma_start(w1[:, u, :, :], expert(I["L1_ffn_W1"], e).rearrange("(c p) f -> p c f", p=P)).then_inc(w_loaded[u], 16)
            engine.dma_start(w3[:, u, :, :], expert(I["L1_ffn_W3"], e).rearrange("(c p) f -> p c f", p=P)).then_inc(w_loaded[u], 16)
            engine.dma_start(w2[:, u, :, :], expert(I["L1_ffn_W2"], e).rearrange("(c p) d -> p c d", p=P)).then_inc(w_loaded[u], 16)

        @block.sync
        def _(sp):
            sp.dma_start(wg[:], I["L1_ffn_Wg"].rearrange("(c p) e -> p c e", p=P)).then_inc(loaded, 16)
            sp.dma_start(bg[:], I["L1_ffn_bg"].partition_broadcast(P)).then_inc(loaded, 16)
            for n, b in enumerate(("L1_ffn_b1", "L1_ffn_b3")):
                sp.dma_start(b13_rows[n * E * FC:(n + 1) * E * FC, :], I[b].rearrange("e (c p) -> (e c) p", p=P)).then_inc(b_loaded, 16)
            sp.wait_ge(zeroed, 1)
            for slots in (slots_x, slots_y):
                for t in range(0, MAX_TILES, 8):
                    n = min(8, MAX_TILES - t)
                    sp.dma_start(slots[t * P:(t + n) * P, :].rearrange("(p n) d -> p (n d)", p=P), zeros[:, 0:n * D]).then_inc(cleared, 16)
            for u in range(2):
                load_expert(sp, u, u)
            sp.dma_start(b2[:], I["L1_ffn_b2"].partition_broadcast(P)).then_inc(b2_loaded, 16)
            sp.dma_start(bf[:], I["L1_ffn_bf"].rearrange("(a d) -> a d", a=1)).then_inc(b2_loaded, 16)
            sp.dma_start(wf[:], I["L1_ffn_Wf"].rearrange("(c p) d -> p c d", p=P)).then_inc(b2_loaded, 16)
            sp.wait_ge(placed, 1)
            sp.wait_ge(scattered, 16 * K * TILES)
            g = zero_register(sp, "l1f_sp_g")
            with sp.Fori(0, E) as e:
                with tiles_of_expert(sp, tile_counts, e, g, MAX_TILES) as at:
                    sp.wait_ge(x_turned, at)
                    sp.dma_start(x_tile[:], slots_x[bass.ds(at * P, P), :]).then_inc(x_loaded, 16)

        @block.gpsimd
        def _(pool):
            pool.memset(zeros[:], 0.0).then_inc(zeroed, 1)
            routing_constants(pool, constants, order[:], restart[:], thresholds[:], ascending=True)
            normalize_pool(pool, chip, turn)
            pool.wait_ge(placed, 1)
            pool.wait_ge(turn.copied, SLOTS + TILES)
            pool.wait_ge(cleared, 16 * CLEARS)
            for t in range(TILES):
                for k in range(K):
                    pool.indirect_dma_start(slots_x, bass.IndirectOffsetOnAxis(index[k][:, t:t + 1], 0), chip.xn[:, t, :], None
                                            ).then_inc(scattered, 16)
            g = zero_register(pool, "l1f_pool_g")
            with pool.Fori(0, E) as e:
                with tiles_of_expert(pool, tile_counts, e, g, MAX_TILES) as at:
                    pool.wait_ge(y_kept, at + 1)
                    pool.dma_start(slots_y[bass.ds(at * P, P), :], y_tile[:]).then_inc(y_stored, 16)
            last = pool.snap(g, min_val=0, max_val=MAX_TILES)
            pool.wait_ge(y_stored, last * 16)
            pool.sem_inc(passed, 1)
            for t in range(TILES):
                for k in range(K):
                    pool.indirect_dma_start(fetched[k][:, t, :], None, slots_y, bass.IndirectOffsetOnAxis(index[k][:, t:t + 1], 0)
                                            ).then_inc(gathered[t // 4], 16)

        @block.tensor
        def _(pe):
            pe.wait_ge(b_loaded, 32)
            pe.transpose(p_y[:, 0:2 * E * FC], b13_rows[:], chip.ident[0:2 * E * FC, 0:2 * E * FC]).then_inc(b_turned, 1)
            turn_pe(pe, chip, turn, p_h)
            pe.wait_ge(loaded, 32)
            for t in range(TILES):
                pe.wait_ge(turn.turned_read, TURN_BANKS + t + 1)
                for c in range(DC):
                    ins = pe.matmul(p_route[:, t * E:(t + 1) * E], chip.xt[:, c, t * P:(t + 1) * P], wg[:, c, :],
                                    start=c == 0, stop=c == DC - 1)
            ins.then_inc(routed, 1)
            pe.wait_ge(chose, 1)
            rank_pe(pe, chip, chosen[:], p_route[:, 128:256].rearrange("p (e t) -> p e t", e=E),
                    p_route[:, 256:384].rearrange("p (e t) -> p e t", e=E)).then_inc(ranked, 1)
            pe.wait_ge(placed, 1)
            g = zero_register(pe, "l1f_pe_g")
            with pe.Fori(0, E // 2) as i:
                for u in range(2):
                    pe.wait_ge(w_loaded[u], i * 48 + 48)
                    pe.sem_inc(passed, 1)
                    with tiles_of_expert(pe, tile_counts, i * 2 + u, g, MAX_TILES) as at:
                        pe.wait_ge(x_loaded, at * 16 + 16)
                        pe.wait_ge(x_kept, at)
                        for c in range(DC):
                            ins = pe.transpose(p_xt[:, c * P:(c + 1) * P], x_tile[:, c * P:(c + 1) * P], chip.ident[:])
                        ins.then_inc(x_turned, 1)
                        pe.wait_ge(x_kept, at + 1)
                        pe.wait_ge(h3_kept, at * 4)
                        pe.wait_ge(h13_kept, at * 4)
                        for half in range(2):
                            for bank, w in ((2 + half, w3), (half, w1)):
                                for f in (2 * half, 2 * half + 1):
                                    for c in range(DC):
                                        ins = pe.matmul(p_h[:, bank, (f % 2) * P:(f % 2 + 1) * P], w[:, u, c, f * P:(f + 1) * P],
                                                        xt_tile[:, c * P:(c + 1) * P], start=c == 0, stop=c == DC - 1)
                                ins.then_inc(h_done, 1)
                        pe.wait_ge(y_kept, at)
                        for f in range(FC):
                            pe.wait_ge(h_kept, at * 2 + (f // 2 + 1))
                            ins = pe.matmul(p_y[:, 0:D], hidden[:, f, :], w2[:, u, f, :], start=f == 0, stop=f == FC - 1)
                        ins.then_inc(y_done, 1)
            pe.wait_ge(b2_loaded, 48)
            for t in range(TILES):
                s = t % 4
                if t >= 2:
                    pe.wait_ge(mixed_kept, t - 1)
                pe.wait_ge(mix_steps, 2 * t + 2)
                for c in range(DC):
                    ins = pe.transpose(p_h[:, t % 2, c * P:(c + 1) * P], mixed[:, s, c * P:(c + 1) * P], chip.ident[:])
                ins.then_inc(mixed_turned, 1)
                pe.wait_ge(mixed_kept, t + 1)
                if t >= 2:
                    pe.wait_ge(added, t - 1)
                for c in range(DC):
                    pe.matmul(p_h[:, 2 + t % 2, 0:D], mixed_t[:, s, c * P:(c + 1) * P], wf[:, c, :], start=c == 0, stop=False)
                pe.matmul(p_h[:, 2 + t % 2, 0:D], chip.ones[0:1, :], bf[:], start=False, stop=True).then_inc(out_done, 1)

        @block.scalar
        def _(act):
            turn_act(act, chip, turn, p_h)
            act.wait_ge(route_steps, 3)
            act.activation(exps[:], logits[:], ACT.Exp).then_inc(exped, 1)
            act.wait_ge(placed, 1)
            act.wait_ge(b_kept, 1)
            g = zero_register(act, "l1f_act_g")

            def run_expert(e, u, reload):
                with tiles_of_expert(act, tile_counts, e, g, MAX_TILES) as at:
                    for half in range(2):
                        act.wait_ge(h_done, at * 4 + (2 * half + 1))
                        act.wait_ge(h13_kept, at * 4)
                        for f in (2 * half, 2 * half + 1):
                            act.activation(h3[:, f, :], p_h[:, 2 + half, (f % 2) * P:(f % 2 + 1) * P], ACT.Identity,
                                           bias=column(b13, e * FC + (E * FC + f))).then_inc(h3_kept, 1)
                    act.wait_ge(y_done, at)
                    for half in range(2):
                        act.wait_ge(h13_kept, at * 4 + (2 * half + 2))
                        act.activation(hidden[:, 2 * half:2 * half + 2, :], h13[:, 2 * half:2 * half + 2, :], ACT.Silu).then_inc(h_kept, 1)
                if reload:
                    done = act.snap(g, min_val=0, max_val=MAX_TILES)
                    act.wait_ge(y_done, done)
                    load_expert(act, e + 2, u)

            with act.Fori(0, E // 2 - 1) as i:
                for u in range(2):
                    run_expert(i * 2 + u, u, True)
            for u in range(2):
                run_expert(E - 2 + u, u, False)
            for t in range(TILES):
                act.wait_ge(mixed_turned, t + 1)
                if t >= 4:
                    act.wait_ge(out_done, t - 3)
                act.copy(mixed_t[:, t % 4, :], p_h[:, t % 2, 0:D]).then_inc(mixed_kept, 1)

        @block.vector
        def _(dve):
            row_statistics(dve, chip, norm_steps, 0, chip.x)
            normalize_dve(dve, chip, turn, chip.x)
            dve.wait_ge(b_turned, 1)
            dve.tensor_copy(b13[:], p_y[:, 0:2 * E * FC]).then_inc(b_kept, 1)
            dve.wait_ge(routed, 1)
            dve.wait_ge(loaded, 32)
            step = Steps(dve, route_steps)
            step(dve.tensor_tensor(logits[:], p_route[:, 0:TILES * E].rearrange("p (t e) -> p t e", e=E),
                                   bg[:].unsqueeze(1).to_broadcast([P, TILES, E]), ALU.add))
            step(dve.tensor_reduce(best[:], logits[:], AX.X, ALU.max))
            step(dve.tensor_tensor(logits[:], logits[:], spread(best[:], E), ALU.subtract))
            dve.wait_ge(exped, 1)
            step(dve.tensor_reduce(total[:], exps[:], AX.X, ALU.add))
            step(dve.reciprocal(total[:], total[:]))
            dve.wait_ge(constants, 3)
            step(dve.tensor_scalar(restart[:], restart[:], 0.0, None, ALU.is_gt))
            for k in range(K):
                choose(dve, step, exps[:], picked[k][:], order[:], weight[k][:], best[:], 2.0)
                step(dve.tensor_tensor(weight[k][:], weight[k][:], total[:], ALU.mult))
            step(dve.tensor_tensor(chosen[:], picked[0][:], picked[1][:], ALU.add))
            dve.sem_inc(chose, 1)
            dve.wait_ge(ranked, 1)
            within, tile_total = (p_route[:, a:a + E * TILES].rearrange("p (e t) -> p e t", e=E) for a in (128, 256))
            ranks_dve(dve, step, rank[:], upto[:], within, tile_total, restart[:])
            expert_bases(dve, step, chip.ones, rank[:], upto[:], compare[:], thresholds[:], tiles[:], ends[:], tile_counts[:])
            for k in range(K):
                slots_dve(dve, step, rank[:], picked[k][:], product[:], place[:], index[k][:])
            dve.sem_inc(placed, 1)
            dve.wait_ge(b2_loaded, 48)
            g = zero_register(dve, "l1f_dve_g")
            with dve.Fori(0, E) as e:
                with tiles_of_expert(dve, tile_counts, e, g, MAX_TILES) as at:
                    dve.wait_ge(x_turned, at + 1)
                    dve.wait_ge(h_done, at * 4)
                    dve.tensor_copy(xt_tile[:], p_xt[:, 0:D]).then_inc(x_kept, 1)
                    dve.wait_ge(h_kept, at * 2)
                    for half in range(2):
                        dve.wait_ge(h_done, at * 4 + (2 * half + 2))
                        for f in (2 * half, 2 * half + 1):
                            dve.wait_ge(h3_kept, at * 4 + (f + 1))
                            dve.scalar_tensor_tensor(h13[:, f, :], p_h[:, half, (f % 2) * P:(f % 2 + 1) * P],
                                                     column(b13, e * FC + f), h3[:, f, :], ALU.add, ALU.mult).then_inc(h13_kept, 1)
                    dve.wait_ge(y_done, at + 1)
                    dve.wait_ge(y_stored, at * 16)
                    dve.tensor_tensor(y_tile[:], p_y[:, 0:D], tile_of(b2, e), ALU.add).then_inc(y_kept, 1)
            for t in range(TILES):
                if t % 4 == 0:
                    dve.wait_ge(gathered[t // 4], 4 * K * 16)
                if t >= 4:
                    dve.wait_ge(mixed_turned, t - 3)
                step = Steps(dve, mix_steps, 2 * t)
                step(dve.tensor_scalar(mixed[:, t % 4, :], fetched[0][:, t, :], weight[0][:, t:t + 1], None, ALU.mult))
                step(dve.scalar_tensor_tensor(mixed[:, t % 4, :], fetched[1][:, t, :], weight[1][:, t:t + 1], mixed[:, t % 4, :],
                                              ALU.mult, ALU.add))
                if t >= 1:
                    add_output(dve, t - 1)
            add_output(dve, TILES - 1)



def l2_attention(nc, chip, I):
    with ExitStack() as stack:
        sb, psum, sem = scope(nc, stack, "l2a")
        w = sb("w", [P, 4, DC, D])
        w_hc = sb("w_hc", [P, BATCH, DC, D])
        wsim_rows, wsim = sb("wsim_rows", [6, P]), sb("wsim", [P, 6])
        b_sim, b_qv = sb("b_sim", [1, 1]), sb("b_qv", [1, D])
        keys, column_term = sb("keys", [P, DC, BATCH * CTX]), sb("column_term", [1, BATCH * CTX])
        xt, probs, probs_t = sb("xt", [P, 2, DC, P]), sb("probs", [P, 2, CTX]), sb("probs_t", [P, 2, 2, P])
        hq_t, xhq_t = sb("hq_t", [P, DC, TOKENS]), sb("xhq_t", [P, DC, TOKENS])
        neg_max, attended = sb("neg_max", [P, TILES]), sb("attended", [P, TILES])
        total, factor = sb("total", [P, 2]), sb("factor", [P, 2])
        tile_min, batch_min, shift, sums, inv_sums = sb("tile_min", [P, 2]), sb("batch_min", [1, 2]), sb("shift", [P, 2]), sb("sums", [P, 2]), sb("inv_sums", [P, 2])
        hc = sb("hc", [P, BATCH, DC])
        pa, pb = psum("pa", [P, 2, 512]), psum("pb", [P, 2, 512])
        pc, pd = psum("pc", [P, 2, 512]), psum("pd", [P, 2, 512])
        (loaded, w_loaded, wsim_turned, wsim_kept, term_done, keys_kept, norm_steps, staged, kept, turned, xt_kept, scored, maxed,
         exped, scaled, probs_turned, probs_kept, hq_done, hq_kept, xhq_kept, min_turned, min_steps, shift_done, exp_done, hc_done,
         hc_steps, out_done, added) = (sem(n) for n in (
            "loaded", "w_loaded", "wsim_turned", "wsim_kept", "term_done", "keys_kept", "norm_steps", "staged", "kept", "turned",
            "xt_kept", "scored", "maxed", "exped", "scaled", "probs_turned", "probs_kept", "hq_done", "hq_kept", "xhq_kept",
            "min_turned", "min_steps", "shift_done", "exp_done", "hc_done", "hc_steps", "out_done", "added"))
        block = stack.enter_context(nc.Block())

        @block.sync
        def _(sp):
            sp.dma_start(wsim_rows[:], I["L2_xattn_w_sim"].rearrange("(c p) -> c p", p=P)).then_inc(loaded, 16)
            sp.dma_start(b_sim[:], I["L2_xattn_b_sim"].rearrange("(a d) -> a d", a=1)).then_inc(loaded, 16)
            sp.dma_start(w[:], I["L2_xattn_W_qv"].rearrange("(k c p) d -> p k c d", k=4, p=P)).then_inc(w_loaded, 16)
            sp.dma_start(b_qv[:], I["L2_xattn_b_qv"].rearrange("(a d) -> a d", a=1)).then_inc(w_loaded, 16)

        @block.tensor
        def _(pe):
            pe.wait_ge(loaded, 32)
            pe.transpose(pa[:, 0, 0:6], wsim_rows[:], chip.ident[0:6, 0:6]).then_inc(wsim_turned, 1)
            pe.wait_ge(wsim_kept, 1)
            for c in range(DC):
                ins = pe.matmul(pb[0:1, 0, 0:BATCH * CTX], wsim[:, 2 + c:3 + c], chip.ctxt[:, c, :], start=c == 0, stop=c == DC - 1)
            ins.then_inc(term_done, 1)
            pe.wait_ge(keys_kept, DC + 1)
            with pe.Fori(0, BATCH_TILES) as i:
                for u in range(BATCH):
                    pe.wait_ge(staged, i * 2 + (u + 1))
                    for c in range(DC):
                        ins = pe.transpose(pa[:, u, c * P:(c + 1) * P], chip.stage[:, u, c * P:(c + 1) * P], chip.ident[:])
                    ins.then_inc(turned, 1)
                for u in range(BATCH):
                    pe.wait_ge(xt_kept, i * 2 + (u + 1))
                    for c in range(DC):
                        pe.matmul(pb[:, u, 0:CTX], xt[:, u, c, :], keys[:, c, u * CTX:(u + 1) * CTX], start=c == 0, stop=False)
                    pe.matmul(pb[:, u, 0:CTX], chip.ones[0:1, :], column_term[:, u * CTX:(u + 1) * CTX],
                              start=False, stop=True).then_inc(scored, 1)
                for u in range(BATCH):
                    pe.wait_ge(scaled, i * 4 + (2 * u + 2))
                    for c, (row, rows) in enumerate(CHUNKS):
                        ins = pe.transpose(pc[0:rows, u, c * P:(c + 1) * P], probs[:, u, row:row + rows], chip.ident[:])
                    ins.then_inc(probs_turned, 1)
                for u in range(BATCH):
                    pe.wait_ge(probs_kept, i * 4 + (2 * u + 2))
                    for d in range(DC):
                        for c, (row, rows) in enumerate(CHUNKS):
                            ins = pe.matmul(pd[:, u, d * P:(d + 1) * P], chip.ctx[0:rows, u, c, d * P:(d + 1) * P],
                                            probs_t[0:rows, u, c, :], start=c == 0, stop=c == 1)
                    ins.then_inc(hq_done, 1)
            pe.wait_ge(min_steps, 1)
            for b in range(BATCH):
                ins = pe.transpose(pa[0:1, 0, b * P:(b + 1) * P], tile_min[:, b:b + 1], chip.ident[:])
            ins.then_inc(min_turned, 1)
            pe.wait_ge(min_steps, 2)
            pe.matmul(pb[:, 0, 0:BATCH], chip.ones[0:1, :], batch_min[:], start=True, stop=True).then_inc(shift_done, 1)
            pe.wait_ge(exp_done, BATCH)
            pe.matmul(pc[:, 0, 0:BATCH], chip.ones[:], sums[:], start=True, stop=True)
            pe.wait_ge(kept, 2 + TILES)
            for b in range(BATCH):
                for c in range(DC):
                    for t in range(BATCH_TILES):
                        at = b * BATCH_TILES + t
                        ins = pe.matmul(pc[:, 1, b * DC + c:b * DC + c + 1], chip.xn[:, at, c * P:(c + 1) * P], attended[:, at:at + 1],
                                        start=t == 0, stop=t == BATCH_TILES - 1)
            ins.then_inc(hc_done, 1)
            pe.wait_ge(hc_steps, 2 + BATCH * DC)
            pe.wait_ge(w_loaded, 32)
            pe.wait_ge(xhq_kept, 2 * TILES)
            for t in range(TILES):
                tokens = slice(t * P, (t + 1) * P)
                if t >= 2:
                    pe.wait_ge(added, t - 1)
                for c in range(DC):
                    pe.matmul(pd[:, t % 2, 0:D], chip.xt[:, c, tokens], w_hc[:, t // BATCH_TILES, c, :], start=c == 0, stop=False)
                    pe.matmul(pd[:, t % 2, 0:D], hq_t[:, c, tokens], w[:, 1, c, :], start=False, stop=False)
                    pe.matmul(pd[:, t % 2, 0:D], xhq_t[:, c, tokens], w[:, 2, c, :], start=False, stop=False)
                pe.matmul(pd[:, t % 2, 0:D], chip.ones[0:1, :], b_qv[:], start=False, stop=True).then_inc(out_done, 1)

        @block.scalar
        def _(act):
            with act.Fori(0, BATCH_TILES) as i:
                for u in range(BATCH):
                    act.wait_ge(turned, i * 2 + (u + 1))
                    act.wait_ge(xhq_kept, i * 4)
                    act.copy(xt[:, u, :, :], pa[:, u, 0:D].rearrange("p (c t) -> p c t", c=DC)).then_inc(xt_kept, 1)
                for u in range(BATCH):
                    act.wait_ge(maxed, i * 2 + (u + 1))
                    act.activation(probs[:, u, :], pb[:, u, 0:CTX], ACT.Exp, bias=column(neg_max, i + u * BATCH_TILES),
                                   accum_out=total[:, u:u + 1]).then_inc(exped, 1)
                for u in range(BATCH):
                    act.wait_ge(hq_done, i * 2 + (u + 1))
                    act.copy(hq_t[:, :, bass.ds((i + u * BATCH_TILES) * P, P)],
                             pd[:, u, 0:D].rearrange("p (c t) -> p c t", c=DC)).then_inc(hq_kept, 1)
            act.wait_ge(min_steps, 3)
            for b in range(BATCH):
                rows = slice(b * BATCH_TILES, (b + 1) * BATCH_TILES)
                act.activation(attended[:, rows], neg_max[:, rows], ACT.Exp, bias=shift[:, b:b + 1], scale=-1.0,
                               accum_out=sums[:, b:b + 1]).then_inc(exp_done, 1)

        @block.gpsimd
        def _(pool):
            pool.sem_inc(kept, 2)
            with pool.Fori(0, BATCH_TILES) as i:
                for u in range(BATCH):
                    pool.wait_ge(staged, i * 2 + (u + 1))
                    pool.tensor_copy(tile_of(chip.xn, i + u * BATCH_TILES), chip.stage[:, u, :]).then_inc(kept, 1)
                for u in range(BATCH):
                    tokens = bass.ds((i + u * BATCH_TILES) * P, P)
                    pool.wait_ge(xt_kept, i * 2 + (u + 1))
                    pool.tensor_copy(chip.xt[:, :, tokens], xt[:, u, :, :]).then_inc(xhq_kept, 1)
                    pool.wait_ge(hq_kept, i * 2 + (u + 1))
                    pool.tensor_tensor(xhq_t[:, :, tokens], hq_t[:, :, tokens], xt[:, u, :, :], ALU.mult).then_inc(xhq_kept, 1)

        @block.vector
        def _(dve):
            dve.wait_ge(wsim_turned, 1)
            dve.tensor_copy(wsim[:], pa[:, 0, 0:6]).then_inc(wsim_kept, 1)
            dve.wait_ge(wsim_kept, 1)
            for c in range(DC):
                dve.tensor_scalar(keys[:, c, :], chip.ctxt[:, c, :], wsim[:, 4 + c:5 + c], wsim[:, c:c + 1],
                                  ALU.mult, ALU.add).then_inc(keys_kept, 1)
            row_statistics(dve, chip, norm_steps, 0, chip.x)
            dve.wait_ge(term_done, 1)
            dve.tensor_scalar(column_term[:], pb[0:1, 0, 0:BATCH * CTX], b_sim[:], None, ALU.add).then_inc(keys_kept, 1)
            with dve.Fori(0, BATCH_TILES) as i:
                for u in range(BATCH):
                    t = i + u * BATCH_TILES
                    dve.wait_ge(kept, i * 2 + (u + 1))
                    dve.tensor_scalar(chip.stage[:, u, :], tile_of(chip.x, t), column(chip.mean, t),
                                      column(chip.inv_std, t), ALU.subtract, ALU.mult).then_inc(staged, 1)
                for u in range(BATCH):
                    dve.wait_ge(scored, i * 2 + (u + 1))
                    dve.tensor_reduce(column(neg_max, i + u * BATCH_TILES), pb[:, u, 0:CTX], AX.X, ALU.max, negate=True).then_inc(maxed, 1)
                for u in range(BATCH):
                    dve.wait_ge(exped, i * 2 + (u + 1))
                    step = Steps(dve, scaled, i * 4 + 2 * u)
                    step(dve.reciprocal(factor[:, u:u + 1], total[:, u:u + 1]))
                    step(dve.tensor_scalar(probs[:, u, :], probs[:, u, :], factor[:, u:u + 1], None, ALU.mult))
                for u in range(BATCH):
                    dve.wait_ge(probs_turned, i * 2 + (u + 1))
                    for c, (row, rows) in enumerate(CHUNKS):
                        dve.tensor_copy(probs_t[0:rows, u, c, :], pc[0:rows, u, c * P:(c + 1) * P]).then_inc(probs_kept, 1)
            step = Steps(dve, min_steps)
            step(dve.tensor_reduce(tile_min[:], neg_max[:].rearrange("p (b t) -> p b t", b=BATCH), AX.X, ALU.min))
            dve.wait_ge(min_turned, 1)
            step(dve.tensor_reduce(batch_min[:], pa[0:1, 0, 0:BATCH * P].rearrange("p (b t) -> p b t", b=BATCH), AX.X, ALU.min))
            dve.wait_ge(shift_done, 1)
            step(dve.tensor_copy(shift[:], pb[:, 0, 0:BATCH]))
            dve.wait_ge(hc_done, 1)
            step = Steps(dve, hc_steps)
            step(dve.reciprocal(inv_sums[:], pc[:, 0, 0:BATCH]))
            step(dve.tensor_tensor(hc[:], pc[:, 1, 0:BATCH * DC].rearrange("p (b c) -> p b c", b=BATCH), spread(inv_sums[:], DC), ALU.mult))
            dve.wait_ge(w_loaded, 32)
            for b in range(BATCH):
                for c in range(DC):
                    step(dve.scalar_tensor_tensor(w_hc[:, b, c, :], w[:, 3, c, :], hc[:, b, c:c + 1], w[:, 0, c, :], ALU.mult, ALU.add))
            for t in range(TILES):
                dve.wait_ge(out_done, t + 1)
                dve.scalar_tensor_tensor(chip.x[:, t, :], pd[:, t % 2, 0:D], chip.gates[:, 2:3], chip.x[:, t, :],
                                         ALU.mult, ALU.add).then_inc(added, 1)



def l2_ffn(nc, chip, I):
    E, F = 8, 512
    FC = F // P
    BLOCK = 512
    BLOCKS = TOKENS // BLOCK
    with ExitStack() as stack:
        sb, psum, sem = scope(nc, stack, "l2f")
        gate_rows, gate_w = sb("gate_rows", [E, D]), sb("gate_w", [P, DC, E])
        gate_b, rms_w = sb("gate_b", [P, E]), sb("rms_w", [P, E])
        w1, w2 = sb("w1", [P, 2, DC, F]), sb("w2", [P, 2, FC, D])
        b1_rows, b1, b2 = sb("b1_rows", [E * FC, P]), sb("b1", [P, E * FC]), sb("b2", [E, D])
        b1_pair = sb("b1_pair", [P, 2 * FC])
        logits, squares = sb("logits", [P, TILES, E]), sb("squares", [P, TILES, E])
        best, root, weight, other = (sb(n, [P, TILES]) for n in ("best", "root", "weight", "other"))
        hidden = sb("hidden", [P, 2, FC, BLOCK])
        y = sb("y", [P, TILES, D])
        p_h, p_y, p_s = psum("p_h", [P, FC, 512]), psum("p_y", [P, 2, 512]), psum("p_s", [P, 2, 512])
        turn = TurnSemaphores(sem, "t")
        (loaded, gate_turned, gate_kept, norm_steps, routed, squared, exped, route_steps, h_done, h_kept, pair_kept, y_done, y_kept, added) = (
            sem(n) for n in ("loaded", "gate_turned", "gate_kept", "norm_steps", "routed", "squared", "exped", "route_steps",
                             "h_done", "h_kept", "pair_kept", "y_done", "y_kept", "added"))
        w_loaded = [sem("w_loaded0"), sem("w_loaded1")]
        block = stack.enter_context(nc.Block())

        def load_expert(engine, e, u):
            engine.dma_start(w1[:, u, :, :], expert(I["L2_ffn_w1"], e).rearrange("(c p) f -> p c f", p=P)).then_inc(w_loaded[u], 16)
            engine.dma_start(w2[:, u, :, :], expert(I["L2_ffn_w2"], e).rearrange("(c p) d -> p c d", p=P)).then_inc(w_loaded[u], 16)

        @block.sync
        def _(sp):
            sp.dma_start(gate_rows[:], I["L2_ffn_gate_w"]).then_inc(loaded, 16)
            sp.dma_start(b1_rows[:], I["L2_ffn_b1"].rearrange("e (c p) -> (e c) p", p=P)).then_inc(loaded, 16)
            sp.dma_start(b2[:], I["L2_ffn_b2"]).then_inc(loaded, 16)
            sp.dma_start(gate_b[:], I["L2_ffn_gate_b"].partition_broadcast(P)).then_inc(loaded, 16)
            sp.dma_start(rms_w[:], I["L2_ffn_rms_w"].partition_broadcast(P)).then_inc(loaded, 16)
            for u in range(2):
                load_expert(sp, u, u)
            with sp.Fori(1, E // 2) as i:
                for u in range(2):
                    sp.wait_ge(y_done, i * (4 * BLOCKS) + (u + 1 - 2) * 2 * BLOCKS)
                    load_expert(sp, i * 2 + u, u)

        @block.tensor
        def _(pe):
            pe.wait_ge(loaded, 80)
            for c in range(DC):
                pe.transpose(p_s[:, 0, c * E:(c + 1) * E], gate_rows[:, c * P:(c + 1) * P], chip.ident[0:E, 0:E])
            pe.transpose(p_s[:, 0, 32:32 + E * FC], b1_rows[:], chip.ident[0:E * FC, 0:E * FC])
            pe.matmul(p_s[:, 0, 128:128 + D], chip.ones[0:E, :], b2[:], start=True, stop=True).then_inc(gate_turned, 1)
            turn_pe(pe, chip, turn, p_h)
            pe.wait_ge(gate_kept, 3)
            for t in range(TILES):
                pe.wait_ge(turn.turned_read, TURN_BANKS + t + 1)
                for c in range(DC):
                    ins = pe.matmul(p_s[:, 1, t * E:(t + 1) * E], chip.xt[:, c, t * P:(t + 1) * P], gate_w[:, c, :],
                                    start=c == 0, stop=c == DC - 1)
            ins.then_inc(routed, 1)
            with pe.Fori(0, E // 2) as i:
                def make_hidden(n):
                    u, b = n // BLOCKS, n % BLOCKS
                    at = i * (2 * BLOCKS) + n
                    if b == 0:
                        pe.wait_ge(w_loaded[u], i * 32 + 32)
                    for f in range(FC):
                        pe.wait_ge(h_kept, at * FC + (f + 1))
                        for c in range(DC):
                            ins = pe.matmul(p_h[:, f, :], w1[:, u, c, f * P:(f + 1) * P], chip.xt[:, c, b * BLOCK:(b + 1) * BLOCK],
                                            start=c == 0, stop=c == DC - 1)
                        ins.then_inc(h_done, 1)

                def multiply_out(n):
                    u, b = n // BLOCKS, n % BLOCKS
                    at = i * (2 * BLOCKS) + n
                    pe.wait_ge(h_kept, at * FC + 2 * FC)
                    for bank in range(2):
                        pe.wait_ge(y_kept, at * 2 + (bank + 1))
                        for half in range(2):
                            j = 2 * bank + half
                            for f in range(FC):
                                ins = pe.matmul(p_y[:, bank, half * D:(half + 1) * D], hidden[:, n % 2, f, j * P:(j + 1) * P],
                                                w2[:, u, f, :], start=f == 0, stop=f == FC - 1)
                        ins.then_inc(y_done, 1)

                make_hidden(0)
                for n in range(2 * BLOCKS):
                    if n + 1 < 2 * BLOCKS:
                        make_hidden(n + 1)
                    multiply_out(n)

        @block.scalar
        def _(act):
            turn_act(act, chip, turn, p_h)
            act.wait_ge(gate_kept, 3)
            act.sem_inc(h_kept, FC)
            with act.Fori(0, E // 2) as i:
                act.wait_ge(h_kept, i * (2 * BLOCKS * FC) + FC)
                act.copy(b1_pair[:], b1[:, bass.ds(i * (2 * FC), 2 * FC)]).then_inc(pair_kept, 1)
                act.wait_ge(pair_kept, i + 1)
                for n in range(2 * BLOCKS):
                    at = i * (2 * BLOCKS) + n
                    act.wait_ge(y_done, i * (4 * BLOCKS) + max(2 * (n - 1), 0))
                    for f in range(FC):
                        act.wait_ge(h_done, at * FC + (f + 1))
                        act.activation(hidden[:, n % 2, f, :], p_h[:, f, :], ACT.Gelu,
                                       bias=column(b1_pair, (n // BLOCKS) * FC + f)).then_inc(h_kept, 1)
            act.wait_ge(route_steps, 20)
            act.activation(logits[:], logits[:], ACT.Exp, scale=2.0).then_inc(exped, 1)

        @block.vector
        def _(dve):
            row_statistics(dve, chip, norm_steps, 0, chip.x)
            dve.wait_ge(gate_turned, 1)
            dve.tensor_copy(gate_w[:], p_s[:, 0, 0:DC * E].rearrange("p (c e) -> p c e", c=DC)).then_inc(gate_kept, 1)
            dve.tensor_copy(b1[:], p_s[:, 0, 32:32 + E * FC]).then_inc(gate_kept, 1)
            dve.tensor_copy(y[:], p_s[:, 0, 128:128 + D].unsqueeze(1).to_broadcast([P, TILES, D])).then_inc(gate_kept, 1)
            normalize_dve(dve, chip, turn, chip.x)
            dve.wait_ge(routed, 1)
            step = Steps(dve, route_steps)
            step(dve.tensor_tensor(logits[:], p_s[:, 1, 0:TILES * E].rearrange("p (t e) -> p t e", e=E),
                                   gate_b[:].unsqueeze(1).to_broadcast([P, TILES, E]), ALU.add))
            step(dve.tensor_tensor(squares[:], logits[:], logits[:], ALU.mult))
            step(dve.tensor_reduce(best[:], squares[:], AX.X, ALU.add))
            inverse_root(dve, step, root[:], best[:], 1.0 / E, 1.1920929e-07, (weight[:], other[:]))
            step(dve.tensor_tensor(logits[:], logits[:], spread(root[:], E), ALU.mult))
            step(dve.tensor_tensor(logits[:], logits[:], rms_w[:].unsqueeze(1).to_broadcast([P, TILES, E]), ALU.mult))
            step(dve.tensor_reduce(best[:], logits[:], AX.X, ALU.max))
            step(dve.tensor_tensor(logits[:], logits[:], spread(best[:], E), ALU.subtract))
            dve.sem_inc(route_steps, 1)
            dve.sem_inc(y_kept, 2)
            with dve.Fori(0, E // 2) as i:
                for n in range(2 * BLOCKS):
                    b = n % BLOCKS
                    for bank in range(2):
                        dve.wait_ge(y_done, i * (4 * BLOCKS) + (2 * n + bank + 1))
                        part = y[:, b * 4 + 2 * bank:b * 4 + 2 * bank + 2, :].rearrange("p t d -> p (t d)")
                        dve.tensor_tensor(part, p_y[:, bank, :], part, ALU.add).then_inc(y_kept, 1)
            dve.wait_ge(exped, 1)
            step = Steps(dve, route_steps, 20)
            step(dve.tensor_reduce(weight[:], logits[:], AX.X, ALU.add))
            step(dve.reciprocal(weight[:], weight[:]))
            step(dve.tensor_scalar(other[:], weight[:], 1e-6, None, ALU.add))
            step(dve.reciprocal(other[:], other[:]))
            step(dve.tensor_tensor(weight[:], weight[:], other[:], ALU.mult))
            step(dve.tensor_scalar(weight[:], weight[:], chip.gates[:, 6:7], None, ALU.mult))
            with dve.Fori(0, TILES // 4) as i:
                for u in range(4):
                    t = i * 4 + u
                    dve.scalar_tensor_tensor(tile_of(chip.x, t), tile_of(y, t), column(weight, t), tile_of(chip.x, t),
                                             ALU.mult, ALU.add).then_inc(added, 1)



HEAD = 64
KEYS = SEQ + CTX
KEY_CHUNKS = 10
BLOCK = 512
BLOCKS_PER_BATCH = SEQ // BLOCK
SLOTS_OF_UNIT = 2 * BLOCKS_PER_BATCH * KEY_CHUNKS
PT_SLOTS = 4
LAG = 2
GROUPS = 4
Q_PARTS = ("q0", "q1", "k0", "k1", "kc")
V_PARTS = ("v0", "v1", "v2", "v3", "v4")
FIRST_OUT, LAST_OUT = ("o0", "o1", "o2", "o3"), ("o4", "o5", "o6", "o7")


def key_chunk(c):
    return c * P, min(P, KEYS - c * P)


def part_columns(part):
    if part == "kc":
        return slice(SEQ, KEYS)
    return slice(int(part[1]) * BLOCK, (int(part[1]) + 1) * BLOCK)


def head_rows(h):
    return (slice(0, HEAD), slice(HEAD, P)) if h == 0 else (slice(HEAD, P), slice(0, HEAD))


def extra_rows(h):
    return slice(HEAD, HEAD + 8) if h == 0 else slice(0, 8)


def second_rows(h):
    return slice(0, HEAD + 8) if h == 0 else slice(0, P)


class Uses:

    def __init__(self, names, done, read, maxima, groups):
        self.names, self.done, self.read, self.maxima, self.groups = names, done, read, maxima, groups

    def bank(self, name):
        return self.names.index(name) % 2

    def done_with(self, name):
        return self.done + (self.names.index(name) + 1)

    def read_before(self, name):
        return self.read + self.names.index(name) // 2

    def read_with(self, name):
        return self.read + (self.names.index(name) // 2 + 1)


class Attention:

    def __init__(self, sb, psum, sem, projected, gate, out_t=None):
        self.gate = gate
        self.q1 = sb("q1", [P, 2, 2, SEQ], F32R)
        self.q2 = sb("q2", [P, 2, 2, SEQ], F32R)
        self.k1 = sb("k1", [P, 2, 2, KEYS], F32R)
        self.k2 = sb("k2", [P, 2, 2, KEYS], F32R)
        self.v = sb("v", [P, 2, KEY_CHUNKS, 2, HEAD + 1])
        self.pt = sb("pt", [P, PT_SLOTS, BLOCK])
        self.maxima = sb("maxima", [P, 16])
        self.minus = sb("minus", [8, 8])
        self.out = sb("out", [P, 2, BLOCK])
        self.inverse = sb("inverse", [P, 2, BLOCK])
        self.shared = sb("shared", [P, 2, BLOCK])
        self.out_t = sb("out_t", [P, 2, SEQ]) if out_t is None else out_t
        self.s_bank, self.st_bank = psum("s_bank", [P, 3, 512]), psum("st_bank", [P, 2, 512])
        self.o_bank, self.side = psum("o_bank", [P, 512]), psum("side", [P, 2, 512])
        self.side_read = [sem("side_read0"), sem("side_read1")]
        self.prepared, self.side_done, self.hi_kept, self.dup_kept = sem("prepared"), sem("side_done"), sem("hi_kept"), sem("dup_kept")
        self.scored, self.maxed, self.st_done, self.exped = sem("scored"), sem("maxed"), sem("st_done"), sem("exped")
        self.pv_done, self.o_kept, self.inverted = sem("pv_done"), sem("o_kept"), sem("inverted")
        self.spread_done, self.ot_done, self.passed = sem("spread_done"), sem("ot_done"), sem("passed")
        self.parts = Q_PARTS + V_PARTS if projected else ()
        self.first_order = list(self.parts + ("nA", "nB"))
        if projected:
            self.order = list(Q_PARTS + ("v0",) + LAST_OUT + V_PARTS[1:] + ("nA", "nB") + FIRST_OUT)
        else:
            self.order = list(LAST_OUT + ("nA", "nB") + FIRST_OUT)
        self.prologue = Uses(self.first_order, 0, 0, 0, 0)

    def uses_before(self, unit):
        first, each = len(self.first_order), len(self.order)
        return unit * each + first, unit * (each // 2) + first // 2

    def cycle(self, unit):
        done, read = self.uses_before(unit)
        return Uses(self.order, done, read, unit * 16 + 16, unit * GROUPS)

    def last(self, unit):
        done, read = self.uses_before(unit)
        return Uses(list(LAST_OUT + FIRST_OUT), done, read, 0, unit * GROUPS)

    def epilogue(self, unit):
        done, read = self.uses_before(unit)
        return Uses(list(LAST_OUT), done + 8, read + 4, 0, (unit + 1) * GROUPS)


class Projection:

    def __init__(self, pe, act, dve, kept, w_out_ready, w_out):
        self.pe, self.act, self.dve, self.kept, self.w_out_ready, self.w_out = pe, act, dve, kept, w_out_ready, w_out


class Mask:
    def __init__(self, row, ones, columns):
        self.row, self.ones, self.columns = row, ones, columns


PREPARED = 7


def attention_prepare(pool, chip, a):
    ones = lambda ap: pool.memset(ap.bitcast(F32), 1.0).then_inc(a.prepared, 1)
    zeros = lambda ap: pool.memset(ap.bitcast(F32), 0.0).then_inc(a.prepared, 1)
    ones(a.k2[HEAD:HEAD + 8, :, 0, :])
    zeros(a.k2[0:HEAD, :, 1, :])
    zeros(a.q2[0:HEAD, :, 1, :])
    pool.wait_ge(a.prepared, 2)
    ones(a.k2[0:8, :, 1, :])
    ones(a.v[:, :, :, :, HEAD:HEAD + 1])
    zeros(a.out_t[:, 1, :])
    pool.tensor_scalar(a.minus[:], chip.ident[0:8, 0:8], -1.0, None, ALU.mult).then_inc(a.prepared, 1)


def side_pe(pe, chip, a, uses, name, unit, u, project):
    bank = a.side[:, uses.bank(name), :]
    pe.wait_ge(a.side_read[uses.bank(name)], uses.read_before(name))
    if name[0] == "n":
        h = "AB".index(name[1])
        pe.wait_ge(a.maxed, uses.maxima + 8 * (h + 1))
        ins = pe.transpose(bank[0:8, 0:P], a.maxima[:, h * 8:h * 8 + 8], chip.ident[:])
    elif name[0] == "o":
        t = int(name[1])
        if t == 0:
            pe.wait_ge(a.ot_done, unit * GROUPS + 2)
            project.w_out_ready(pe, unit, u)
        if t == 4:
            pe.wait_ge(a.ot_done, uses.groups)
        ins = pe.matmul(bank[:, 0:D], a.out_t[:, u, t * P:(t + 1) * P], project.w_out(unit, u, t), start=True, stop=True)
    else:
        ins = project.pe(pe, bank, name, unit, u)
    ins.then_inc(a.side_done, 1)


def scores_pe(pe, a, unit, u, n, mask):
    h, t = n // 8, n % 8
    hi, _ = head_rows(h)
    if n == 0:
        pe.wait_ge(a.hi_kept, unit * 10 + 10)
    pe.wait_ge(a.maxed, unit * 16 + n)
    lhs = a.q1[hi, u, h, t * P:(t + 1) * P]
    for c in range(3):
        at, end = c * BLOCK, min((c + 1) * BLOCK, KEYS)
        masked = mask is not None and c == 2
        ins = pe.matmul(a.s_bank[:, c, 0:end - at], lhs, a.k1[hi, u, h, at:end], start=True, stop=not masked)
        if masked:
            ins = pe.matmul(a.s_bank[:, c, 0:end - at], mask.ones[0:1, :], mask.row[0:1, u * CTX:(u + 1) * CTX], start=False, stop=True)
    ins.then_inc(a.scored, 1)


def score_slot(n):
    return 14 + n + n // 8


def side_slots(projected):
    at = {}
    if projected:
        for j, name in enumerate(Q_PARTS + ("v0",)):
            at[name] = 2 + j
        for j, name in enumerate(LAST_OUT):
            at[name] = 8 + j
        for j, name in enumerate(V_PARTS[1:]):
            at[name] = 12 + j
    else:
        for j, name in enumerate(LAST_OUT):
            at[name] = 8 + j
    at["nA"], at["nB"] = 24, 34
    for j, name in enumerate(FIRST_OUT):
        at[name] = 35 + j
    return at


def attention_pe(pe, chip, a, unit, u, uses, project, mask=None, following=True):
    slots = side_slots(bool(a.parts))
    pe.wait_ge(a.dup_kept, unit * 10 + 10)
    before = uses.read
    for bank in range(2):
        pe.wait_ge(a.side_read[bank], before)
    if project.kept is not None:
        project.kept(pe, unit)

    def multiply_values(n):
        b, h, c = n // 20, (n // 10) % 2, n % 10
        row, rows = key_chunk(c)
        pe.wait_ge(a.exped, unit * SLOTS_OF_UNIT + (n + 1 + 2))
        if c == 0:
            pe.wait_ge(a.o_kept, unit * GROUPS + n // 10)
        ins = pe.matmul(a.o_bank[0:HEAD + 1, :], a.v[0:rows, u, c, h, :], a.pt[0:rows, n % PT_SLOTS, :],
                        start=c == 0, stop=c == KEY_CHUNKS - 1)
        ins.then_inc(a.pv_done, 1)

    for n in range(SLOTS_OF_UNIT):
        b, h, c = n // 20, (n // 10) % 2, n % 10
        row, rows = key_chunk(c)
        pe.wait_ge(a.exped, unit * SLOTS_OF_UNIT + (n + 1))
        queries = slice(b * BLOCK, (b + 1) * BLOCK)
        second = second_rows(h)
        pe.matmul(a.st_bank[0:rows, n % 2, :], a.k1[:, u, h, row:row + rows], a.q1[:, u, h, queries], start=True, stop=False)
        pe.matmul(a.st_bank[0:rows, n % 2, :], a.k2[second, u, h, row:row + rows], a.q2[second, u, h, queries],
                  start=False, stop=True).then_inc(a.st_done, 1)
        if n >= LAG:
            multiply_values(n - LAG)
        for name, slot in slots.items():
            if slot == n and name in uses.names:
                side_pe(pe, chip, a, uses, name, unit, u if name in FIRST_OUT else 1 - u, project)
        if following:
            for m in range(16):
                if score_slot(m) == n:
                    scores_pe(pe, a, unit + 1, 1 - u, m, mask)
    for n in range(SLOTS_OF_UNIT - LAG, SLOTS_OF_UNIT):
        multiply_values(n)


def attention_act(act, a, unit, u, uses, scale, project, mask=None, following=True):
    slots = side_slots(bool(a.parts))
    for n in range(SLOTS_OF_UNIT):
        b, h, c = n // 20, (n // 10) % 2, n % 10
        row, rows = key_chunk(c)
        act.wait_ge(a.pv_done, unit * SLOTS_OF_UNIT + (n + 1))
        act.wait_ge(a.st_done, unit * SLOTS_OF_UNIT + (n + 1))
        if n % 10 == LAG and n > 10:
            keep_group(act, a, unit, n // 10 - 1)
        bias = mask.columns[0:rows, u * 2 + c - 8:u * 2 + c - 7] if mask is not None and c >= 8 else 0.0
        act.activation(a.pt[0:rows, n % PT_SLOTS, :], a.st_bank[0:rows, n % 2, :], ACT.Exp, bias=bias, scale=scale).then_inc(a.exped, 1)
        if following:
            for name, slot in slots.items():
                if slot == n and name in uses.names:
                    keep_part_act(act, a, uses, name, unit + 1, 1 - u)
            if project.act is not None:
                project.act(act, unit + 1, 1 - u, n)
    keep_group(act, a, unit, GROUPS - 1)


def keep_group(act, a, unit, g):
    act.wait_ge(a.pv_done, unit * SLOTS_OF_UNIT + (10 * (g + 1) + PT_SLOTS))
    act.wait_ge(a.ot_done, unit * GROUPS + max(g - 1, 0))
    act.copy(a.out[0:HEAD + 1, g % 2, :], a.o_bank[0:HEAD + 1, :]).then_inc(a.o_kept, 1)


def keep_part_act(act, a, uses, name, unit, u):
    if name[0] in "no":
        return
    bank = a.side[:, uses.bank(name), :]
    act.wait_ge(a.side_done, uses.done_with(name))
    if name[0] == "v":
        j = int(name[1])
        for c in (2 * j, 2 * j + 1):
            _, rows = key_chunk(c)
            ins = act.copy(a.v[0:rows, u, c, :, 0:HEAD],
                           bank[0:rows, (c % 2) * P:(c % 2 + 1) * P].rearrange("p (h d) -> p h d", h=2))
        ins.then_inc(a.side_read[uses.bank(name)], 1)
        return
    to, columns = (a.q1 if name[0] == "q" else a.k1), part_columns(name)
    for h in range(2):
        hi, _ = head_rows(h)
        act.copy(to[hi, u, h, columns], bank[hi, 0:columns.stop - columns.start]).then_inc(a.hi_kept, 1)


def keep_part_dve(dve, a, uses, name, unit, u):
    bank = a.side[:, uses.bank(name), :]
    if name[0] == "n":
        h = "AB".index(name[1])
        dve.wait_ge(a.side_done, uses.done_with(name))
        dve.tensor_tensor(a.q2[extra_rows(h), u, h, :].rearrange("p (t q) -> p t q", q=P),
                          bank[0:8, 0:P].unsqueeze(1).to_broadcast([8, 8, P]), spread(a.minus[:], P), ALU.mult
                          ).then_inc(a.side_read[uses.bank(name)], 1)
        return
    if name not in Q_PARTS:
        return
    columns = part_columns(name)
    dve.wait_ge(a.hi_kept, unit * 10 + 2 * (Q_PARTS.index(name) + 1))
    for h in range(2):
        hi, other = head_rows(h)
        source = a.q1 if name[0] == "q" else a.k1
        out = a.q2[hi, u, h, columns] if name[0] == "q" else a.k1[other, u, h, columns]
        ins = dve.tensor_tensor(out, bank[hi, 0:columns.stop - columns.start], source[hi, u, h, columns].bitcast(F32), ALU.subtract)
    ins.then_inc(a.side_read[uses.bank(name)], 1)


def add_output(dve, chip, a, uses, name, u):
    t = int(name[1]) + u * BATCH_TILES
    dve.wait_ge(a.side_done, uses.done_with(name))
    dve.scalar_tensor_tensor(chip.x[:, t, :], a.side[:, uses.bank(name), 0:D], a.gate, chip.x[:, t, :],
                             ALU.mult, ALU.add).then_inc(a.side_read[uses.bank(name)], 1)


def largest(dve, a, unit, n):
    dve.wait_ge(a.scored, unit * 16 + (n + 1))
    dve.tensor_reduce(a.maxima[:, n:n + 1], a.s_bank[:].rearrange("p a b -> p (a b)")[:, 0:KEYS], AX.X, ALU.max).then_inc(a.maxed, 1)


def attention_dve(dve, chip, a, unit, u, uses, project, following=True):
    slots = side_slots(bool(a.parts))
    for n in range(SLOTS_OF_UNIT):
        if n % 10 == LAG + 3 and n > 10:
            invert_group(dve, a, unit, n // 10 - 1)
        if n % 10 == LAG + 6 and n > 10:
            scale_group(dve, a, unit, u, n // 10 - 1)
        for name, slot in slots.items():
            if slot == n and name in uses.names:
                if name in LAST_OUT:
                    add_output(dve, chip, a, uses, name, 1 - u)
                elif name in FIRST_OUT:
                    add_output(dve, chip, a, uses, name, u)
                else:
                    keep_part_dve(dve, a, uses, name, unit + 1, 1 - u)
        if following:
            if project.dve is not None:
                project.dve(dve, unit + 1, 1 - u, n)
            for m in range(16):
                if score_slot(m) == n:
                    largest(dve, a, unit + 1, m)
    invert_group(dve, a, unit, GROUPS - 1)
    scale_group(dve, a, unit, u, GROUPS - 1)


def invert_group(dve, a, unit, g):
    dve.wait_ge(a.o_kept, unit * GROUPS + (g + 1))
    dve.wait_ge(a.spread_done, unit * GROUPS + max(g - 1, 0))
    dve.reciprocal(a.inverse[HEAD:HEAD + 1, g % 2, :], a.out[HEAD:HEAD + 1, g % 2, :]).then_inc(a.inverted, 1)


def scale_group(dve, a, unit, u, g):
    b, h = g // 2, g % 2
    dve.wait_ge(a.spread_done, unit * GROUPS + (g + 1))
    hi, _ = head_rows(h)
    dve.tensor_tensor(a.out_t[hi, u, b * BLOCK:(b + 1) * BLOCK], a.out[0:HEAD, g % 2, :], a.shared[0:HEAD, g % 2, :],
                      ALU.mult).then_inc(a.ot_done, 1)


def attention_pool(pool, a, unit, u, following=True):
    def spread_group(g):
        pool.wait_ge(a.dup_kept, unit * 10 + (20 if following else 10))
        pool.wait_ge(a.spread_done, unit * GROUPS + g)
        pool.wait_ge(a.ot_done, unit * GROUPS + max(g - 1, 0))
        pool.wait_ge(a.inverted, unit * GROUPS + (g + 1))
        pool.sem_inc(a.passed, 1)
        pool.partition_broadcast(a.shared[0:HEAD, g % 2, :], a.inverse[HEAD:HEAD + 1, g % 2, :], channels=HEAD).then_inc(a.spread_done, 1)

    if following:
        pool.wait_ge(a.spread_done, unit * GROUPS)
        double_parts(pool, a, unit + 1, 1 - u)
    for g in range(GROUPS - 1):
        spread_group(g)
    spread_group(GROUPS - 1)


def double_parts(pool, a, unit, u):
    for j, name in enumerate(Q_PARTS):
        pool.wait_ge(a.hi_kept, unit * 10 + 2 * (j + 1))
        pool.sem_inc(a.passed, 1)
        columns = part_columns(name)
        for h in range(2):
            hi, other = head_rows(h)
            if name[0] == "q":
                out, source = a.q1[other, u, h, columns], a.q1[hi, u, h, columns]
            else:
                out, source = a.k2[hi, u, h, columns], a.k1[hi, u, h, columns]
            pool.tensor_copy(out, source.bitcast(F32)).then_inc(a.dup_kept, 1)


def first_maxima_pe(pe, chip, a, project, mask=None):
    pe.wait_ge(a.prepared, PREPARED)
    for name in a.parts:
        side_pe(pe, chip, a, a.prologue, name, 0, 0, project)
    for h in range(2):
        for m in range(8):
            scores_pe(pe, a, 0, 0, 8 * h + m, mask)
        side_pe(pe, chip, a, a.prologue, "n" + "AB"[h], 0, 0, project)


def first_maxima_dve(dve, a):
    for h in range(2):
        for m in range(8):
            largest(dve, a, 0, 8 * h + m)
        keep_part_dve(dve, a, a.prologue, "n" + "AB"[h], 0, 0)


def attention_units(engine, pairs, cycle):
    if pairs > 2:
        with engine.Fori(0, pairs - 1) as i:
            for u in range(BATCH):
                cycle(i * BATCH + u, u, True)
    else:
        for u in range(BATCH):
            cycle(u, u, True)
    cycle(BATCH * (pairs - 1), 0, True)
    cycle(BATCH * (pairs - 1) + 1, 1, False)


def normalize_twice_dve(dve, chip, sem, add_sem, gb):
    row_statistics(dve, chip, sem, 0, chip.x)
    with dve.Fori(0, TILES // 4) as i:
        for v in range(4):
            t = i * 4 + v
            dve.tensor_scalar(tile_of(chip.xn, t), tile_of(chip.x, t), column(chip.mean, t), column(chip.inv_std, t),
                              ALU.subtract, ALU.mult).then_inc(sem, 1)
    dve.wait_ge(sem, NORM_STEPS + TILES)
    row_statistics(dve, chip, sem, NORM_STEPS + TILES, chip.xn)
    dve.tensor_tensor(chip.x[:], chip.x[:], gb.unsqueeze(1).to_broadcast([P, TILES, D]), ALU.add).then_inc(add_sem, 1)



def l1_attention(nc, chip, I):
    PAIRS = 2
    INNER = 2 * HEAD * PAIRS
    HEADS = 2 * PAIRS
    CT = 2 * BATCH
    SCALE = HEAD ** -0.5
    OFF = 1e30
    with ExitStack() as kept_stack:
        sb, _, sem = scope(nc, kept_stack, "l1a")
        k_t = sb("k_t", [P, PAIRS, BATCH * KEYS])
        v_all = sb("v_all", [P, TILES + CT, INNER])
        wo = sb("wo", [P, PAIRS, D])
        mask_bytes, mask_flat = sb("mask_bytes", [1, BATCH * CTX], mybir.dt.uint8), sb("mask_flat", [1, BATCH * CTX])
        mask_row, mask_ones = sb("mask_row", [1, BATCH * CTX], F32R), sb("mask_ones", [1, P], F32R)
        mask_columns = sb("mask_columns", [P, CT])
        q_t = chip.xt
        wo_loaded = sem("wo_loaded")

        with ExitStack() as stack:
            sb, psum, sem = scope(nc, stack, "l1p")
            w = sb("w", [P, DC, 3 * INNER])
            rows_in, columns = sb("rows_in", [10, P]), sb("columns", [P, 10])
            gb = sb("gb", [P, D])
            c_stats, c_stage, ctxn_t = sb("c_stats", [P, CT, 6]), sb("c_stage", [P, CT, D]), sb("ctxn_t", [P, DC, BATCH * CTX])
            c_mean, c_inv, c_a, c_b, c_c = (sb(n, [P, CT]) for n in ("c_mean", "c_inv", "c_a", "c_b", "c_c"))
            qk = sb("qk", [P, TILES + CT, 2 * INNER])
            squares = sb("squares", [P, 2, 2 * INNER])
            sums, inv, half, value = (sb(n, [P, TILES + CT, 2 * HEADS]) for n in ("sums", "inv", "half", "value"))
            pq, pv, pt, pc = psum("pq", [P, 2, 512]), psum("pv", [P, 2, 512]), psum("pt", [P, 2, 512]), psum("pc", [P, 2, 512])
            turn = TurnSemaphores(sem, "t")
            (loaded, w_loaded, made, gb_made, x_biased, norm_steps, c_steps, c_staged, rows_turned, rows_kept, c_turned, c_kept,
             projected, qk_kept, squared, v_kept, root_steps, scaled, qk_turned, q_kept, kk_kept, mask_steps, mask_done, mask_kept) = (
                sem(n) for n in (
                    "loaded", "w_loaded", "made", "gb_made", "x_biased", "norm_steps", "c_steps", "c_staged", "rows_turned",
                    "rows_kept", "c_turned", "c_kept", "projected", "qk_kept", "squared", "v_kept", "root_steps", "scaled",
                    "qk_turned", "q_kept", "kk_kept", "mask_steps", "mask_done", "mask_kept"))
            block = stack.enter_context(nc.Block())

            def tile_rows(t):
                return P if t < TILES or t % 2 == 0 else CTX_REST

            @block.sync
            def _(sp):
                for k, name in enumerate(("ln_x_g", "ln_x_b", "ln_l_g", "ln_l_b")):
                    sp.dma_start(rows_in[2 * k:2 * k + 2, :], I["L1_xattn_" + name].rearrange("(c p) -> c p", p=P)).then_inc(loaded, 16)
                for k, name in enumerate(("q_gamma", "k_gamma")):
                    for h in range(2):
                        sp.dma_start(rows_in[8 + k:9 + k, h * HEAD:(h + 1) * HEAD],
                                     I["L1_xattn_" + name].rearrange("(a d) -> a d", a=1)).then_inc(loaded, 16)
                sp.dma_start(mask_bytes[:], I["mask_BxS2_bk0"].rearrange("b c -> (b c)").rearrange("(a d) -> a d", a=1)).then_inc(loaded, 16)
                sp.dma_start(gb[:], I["L1_xattn_b_out"].partition_broadcast(P)).then_inc(loaded, 16)
                sp.dma_start(w[:, :, 0:INNER], I["L1_xattn_W_q"].rearrange("(c p) n -> p c n", p=P)).then_inc(w_loaded, 16)
                sp.dma_start(w[:, :, INNER:3 * INNER], I["L1_xattn_W_kv"].rearrange("(c p) n -> p c n", p=P)).then_inc(w_loaded, 16)
                sp.dma_start(wo[:], I["L1_xattn_W_out"].rearrange("(c p) n -> p c n", p=P)).then_inc(wo_loaded, 16)

            LOADED = 10 * 16

            @block.gpsimd
            def _(pool):
                pool.memset(c_stats[:], 0.0).then_inc(made, 1)
                pool.memset(sums[:], 1.0).then_inc(made, 1)
                pool.memset(mask_ones[:].bitcast(F32), 1.0).then_inc(made, 1)

            @block.tensor
            def _(pe):
                pe.wait_ge(loaded, LOADED)
                pe.transpose(pt[:, 0, 0:10], rows_in[:], chip.ident[0:10, 0:10]).then_inc(rows_turned, 1)
                pe.wait_ge(mask_steps, 2)
                for b in range(BATCH):
                    for c, (row, rows) in enumerate(CHUNKS):
                        at = b * CTX + row
                        ins = pe.matmul(pc[0:rows, 0, 2 * b + c:2 * b + c + 1], mask_flat[0:1, at:at + rows], chip.ones[0:1, 0:1],
                                        start=True, stop=True)
                ins.then_inc(mask_done, 1)
                turn_pe(pe, chip, turn, pq)
                for k in range(CT):
                    rows = tile_rows(TILES + k)
                    pe.wait_ge(c_staged, k + 1)
                    if k == 0:
                        pe.wait_ge(rows_kept, 1)
                    if k >= 2:
                        pe.wait_ge(c_kept, k - 1)
                    for c in range(DC):
                        ins = pe.transpose(pt[:, k % 2, c * P:c * P + rows], c_stage[0:rows, k, c * P:(c + 1) * P], chip.ident[0:rows, 0:rows])
                    ins.then_inc(c_turned, 1)
                pe.wait_ge(w_loaded, 32)
                pe.wait_ge(turn.turned_read, TURN_BANKS + TILES)
                pe.wait_ge(c_kept, CT)
                for t in range(TILES + CT):
                    rows, bank = tile_rows(t), t % 2
                    if t >= 2:
                        pe.wait_ge(squared, t - 1)
                        pe.wait_ge(v_kept, t - 1)
                    if t < TILES:
                        source, at, first = chip.xt, t * P, 0
                    else:
                        source, at, first = ctxn_t, (t - TILES) // 2 * CTX + CHUNKS[t % 2][0], INNER
                    for c in range(DC):
                        pe.matmul(pq[0:rows, bank, first:2 * INNER], source[:, c, at:at + rows], w[:, c, first:2 * INNER],
                                  start=c == 0, stop=c == DC - 1)
                    for c in range(DC):
                        ins = pe.matmul(pv[0:rows, bank, 0:INNER], source[:, c, at:at + rows], w[:, c, 2 * INNER:3 * INNER],
                                        start=c == 0, stop=c == DC - 1)
                    ins.then_inc(projected, 1)
                for t in range(TILES + CT):
                    rows, bank = tile_rows(t), t % 2
                    pe.wait_ge(scaled, t + 1)
                    if t >= 2:
                        pe.wait_ge(kk_kept, t - 1)
                    for j in range(0 if t < TILES else PAIRS, 2 * PAIRS):
                        ins = pe.transpose(pt[:, bank, j * P:j * P + rows], qk[0:rows, t, j * P:(j + 1) * P], chip.ident[0:rows, 0:rows])
                    ins.then_inc(qk_turned, 1)

            @block.scalar
            def _(act):
                act.wait_ge(rows_turned, 1)
                act.copy(columns[:], pt[:, 0, 0:10]).then_inc(rows_kept, 1)
                act.wait_ge(rows_kept, 1)
                act.wait_ge(mask_done, 1)
                for b in range(BATCH):
                    for c, (row, rows) in enumerate(CHUNKS):
                        act.copy(mask_columns[0:rows, 2 * b + c:2 * b + c + 1], pc[0:rows, 0, 2 * b + c:2 * b + c + 1]).then_inc(mask_kept, 1)
                turn_act(act, chip, turn, pq, scale=columns[:, 4:6], bias=columns[:, 6:8])
                for k in range(CT):
                    rows = tile_rows(TILES + k)
                    act.wait_ge(c_turned, k + 1)
                    at = k // 2 * CTX + CHUNKS[k % 2][0]
                    for c in range(DC):
                        ins = act.activation(ctxn_t[:, c, at:at + rows], pt[:, k % 2, c * P:c * P + rows], ACT.Identity,
                                             bias=columns[:, 2 + c:3 + c], scale=columns[:, c:c + 1])
                    ins.then_inc(c_kept, 1)
                for t in range(TILES + CT):
                    rows, bank, first = tile_rows(t), t % 2, 0 if t < TILES else INNER
                    act.wait_ge(projected, t + 1)
                    act.copy(qk[0:rows, t, first:2 * INNER], pq[0:rows, bank, first:2 * INNER]).then_inc(qk_kept, 1)
                    if t >= 2:
                        act.wait_ge(root_steps, t - 1)
                    act.activation(squares[0:rows, bank, first:2 * INNER], pq[0:rows, bank, first:2 * INNER], ACT.Square).then_inc(squared, 1)
                    act.copy(v_all[0:rows, t, :], pv[0:rows, bank, 0:INNER]).then_inc(v_kept, 1)
                for t in range(TILES + CT):
                    rows, bank = tile_rows(t), t % 2
                    act.wait_ge(qk_turned, t + 1)
                    if t < TILES:
                        b, at = t // BATCH_TILES, t % BATCH_TILES * P
                        act.mul(q_t[:, :, t * P:(t + 1) * P], pt[:, bank, 0:INNER].rearrange("p (j q) -> p j q", j=PAIRS),
                                columns[:, 8:9]).then_inc(q_kept, 1)
                    else:
                        b, at = (t - TILES) // 2, SEQ + CHUNKS[t % 2][0]
                    act.mul(k_t[:, :, b * KEYS + at:b * KEYS + at + rows],
                            pt[:, bank, INNER:2 * INNER].rearrange("p (j q) -> p j q", j=PAIRS)[:, :, 0:rows], columns[:, 9:10]
                            ).then_inc(kk_kept, 1)

            @block.vector
            def _(dve):
                dve.wait_ge(loaded, LOADED)
                dve.tensor_scalar(gb[:], gb[:], chip.gates[:, 1:2], None, ALU.mult).then_inc(gb_made, 1)
                step = Steps(dve, mask_steps)
                step(dve.tensor_copy(mask_flat[:], mask_bytes[:]))
                step(dve.tensor_scalar(mask_flat[:], mask_flat[:], 1.0, OFF, ALU.subtract, ALU.mult))
                step(dve.tensor_copy(mask_row[:], mask_flat[:]))
                dve.wait_ge(made, 3)
                for k in range(CT):
                    rows = tile_rows(TILES + k)
                    dve.bn_stats(c_stats[0:rows, k, :], chip.ctx[0:rows, k // 2, k % 2, :]).then_inc(c_steps, 1)
                dve.wait_ge(c_steps, CT)
                aggregate(dve, c_steps, CT, c_stats[:], c_mean[:], c_inv[:], (c_a[:], c_b[:], c_c[:]))
                for k in range(CT):
                    rows = tile_rows(TILES + k)
                    dve.tensor_scalar(c_stage[0:rows, k, :], chip.ctx[0:rows, k // 2, k % 2, :], c_mean[0:rows, k:k + 1],
                                      c_inv[0:rows, k:k + 1], ALU.subtract, ALU.mult).then_inc(c_staged, 1)
                normalize_twice_dve(dve, chip, norm_steps, x_biased, gb[:])
                normalize_dve(dve, chip, turn, chip.xn)
                for t in range(TILES + CT):
                    rows, first = tile_rows(t), 0 if t < TILES else INNER
                    dve.wait_ge(squared, t + 1)
                    dve.tensor_reduce(sums[0:rows, t, first // HEAD:2 * HEADS],
                                      squares[0:rows, t % 2, first:2 * INNER].rearrange("p (h d) -> p h d", d=HEAD), AX.X, ALU.add
                                      ).then_inc(root_steps, 1)
                dve.wait_ge(root_steps, TILES + CT)
                step = Steps(dve, root_steps, TILES + CT)
                flat = lambda tensor: tensor[:].rearrange("p t h -> p (t h)")
                step(dve.tensor_scalar(sums[:], sums[:], HEAD * 1e-16, None, ALU.max))
                inverse_root(dve, step, flat(inv), flat(sums), 1.0 / HEAD, 0.0, (flat(value), flat(half)))
                dve.wait_ge(qk_kept, TILES + CT)
                for t in range(TILES + CT):
                    rows, first = tile_rows(t), 0 if t < TILES else INNER
                    part = qk[0:rows, t, first:2 * INNER].rearrange("p (h d) -> p h d", d=HEAD)
                    dve.tensor_tensor(part, part, spread(inv[0:rows, t, first // HEAD:2 * HEADS], HEAD), ALU.mult).then_inc(scaled, 1)

        with ExitStack() as stack:
            sb, psum, sem = scope(nc, stack, "l1a2")
            a = Attention(sb, psum, sem, projected=False, gate=chip.gates[:, 1:2],
                                  out_t=chip.xn[:, 0:8, :].rearrange("p (u t) d -> p u (t d)", u=2))
            lo_kept = sem("lo_kept")
            mask = Mask(row=mask_row, ones=mask_ones, columns=mask_columns)
            block = stack.enter_context(nc.Block())

            def source_of(name, pair, b):
                columns = part_columns(name)
                if name[0] == "q":
                    return q_t[:, pair, b * SEQ + columns.start:b * SEQ + columns.stop]
                return k_t[:, pair, b * KEYS + columns.start:b * KEYS + columns.stop]

            def keep_hi_act(act, unit, u, n):
                if 2 <= n < 7:
                    name = Q_PARTS[n - 2]
                    to = a.q1 if name[0] == "q" else a.k1
                    for h in range(2):
                        hi, _ = head_rows(h)
                        act.copy(to[hi, u, h, part_columns(name)], source_of(name, unit // 2, u)[hi]).then_inc(a.hi_kept, 1)
                if n == 7:
                    for h in range(2):
                        at = unit // 2 * P + h * HEAD
                        act.copy(a.v[:, u, 0:8, h, 0:HEAD], v_all[:, u * 8:u * 8 + 8, at:at + HEAD])
                        for c in range(2):
                            rows = CHUNKS[c][1]
                            act.copy(a.v[0:rows, u, 8 + c, h, 0:HEAD], v_all[0:rows, TILES + 2 * u + c, at:at + HEAD])

            def keep_lo_dve(dve, unit, u, n):
                if not 2 <= n < 7:
                    return
                name = Q_PARTS[n - 2]
                dve.wait_ge(a.hi_kept, unit * 10 + 2 * (n - 1))
                for h in range(2):
                    hi, other = head_rows(h)
                    columns = part_columns(name)
                    hi_values = (a.q1 if name[0] == "q" else a.k1)[hi, u, h, columns].bitcast(F32)
                    out = a.q2[hi, u, h, columns] if name[0] == "q" else a.k1[other, u, h, columns]
                    ins = dve.tensor_tensor(out, source_of(name, unit // 2, u)[hi], hi_values, ALU.subtract)
                ins.then_inc(lo_kept, 1)

            project = Projection(
                pe=None, act=keep_hi_act, dve=keep_lo_dve, kept=lambda pe, unit: pe.wait_ge(lo_kept, unit * 5 + 5),
                w_out_ready=lambda pe, unit, u: None,
                w_out=lambda unit, u, t: wo[:, (unit if t < 4 else max(unit - 1, 0)) // 2, :])
            uses_of = lambda unit, following: (a.cycle if following else a.last)(unit)

            @block.tensor
            def _(pe):
                pe.sem_inc(a.pv_done, PT_SLOTS)
                pe.wait_ge(wo_loaded, 16)
                first_maxima_pe(pe, chip, a, project, mask)
                attention_units(pe, PAIRS, lambda unit, u, following: attention_pe(
                    pe, chip, a, unit, u, uses_of(unit, following), project, mask, following))
                last = BATCH * PAIRS - 1
                for name in LAST_OUT:
                    side_pe(pe, chip, a, a.epilogue(last), name, last, 1, project)

            @block.scalar
            def _(act):
                act.sem_inc(a.exped, 2)
                act.wait_ge(a.prepared, PREPARED)
                for n in range(8):
                    keep_hi_act(act, 0, 0, n)
                attention_units(act, PAIRS, lambda unit, u, following: attention_act(
                    act, a, unit, u, uses_of(unit, following), SCALE, project, mask, following))

            @block.vector
            def _(dve):
                dve.wait_ge(a.prepared, PREPARED)
                for n in range(8):
                    keep_lo_dve(dve, 0, 0, n)
                first_maxima_dve(dve, a)
                attention_units(dve, PAIRS, lambda unit, u, following: attention_dve(
                    dve, chip, a, unit, u, uses_of(unit, following), project, following))
                for name in LAST_OUT:
                    add_output(dve, chip, a, a.epilogue(BATCH * PAIRS - 1), name, 1)

            @block.gpsimd
            def _(pool):
                attention_prepare(pool, chip, a)
                pool.wait_ge(a.prepared, PREPARED)
                double_parts(pool, a, 0, 0)
                attention_units(pool, PAIRS, lambda unit, u, following: attention_pool(pool, a, unit, u, following))



def l3_attention(nc, chip, I):
    PAIRS = 8
    INNER = 2 * HEAD * PAIRS
    SCALE = HEAD ** -0.5
    with ExitStack() as stack:
        sb, psum, sem = scope(nc, stack, "l3a")
        w = sb("w", [P, 4, DC, P])
        wo = sb("wo", [P, D])
        ln_rows, ln = sb("ln_rows", [2 * DC, P]), sb("ln", [P, 2 * DC])
        gb = sb("gb", [P, D])
        a = Attention(sb, psum, sem, projected=True, gate=chip.gates[:, 3:4])
        turn = TurnSemaphores(sem, "t")
        loaded, norm_steps, x_biased, gb_made, ln_turned, ln_kept, w_loaded, wo_loaded = (sem(n) for n in (
            "loaded", "norm_steps", "x_biased", "gb_made", "ln_turned", "ln_kept", "w_loaded", "wo_loaded"))
        block = stack.enter_context(nc.Block())

        def load_weights(sp, pair):
            for k, (name, at) in enumerate((("L3_xattn_Wq", 0), ("L3_xattn_Wkv", 0), ("L3_xattn_Wkv", INNER), ("L3_xattn_Wm", 0))):
                sp.dma_start(w[:, k, :, :], I[name].rearrange("(c p) n -> p c n", p=P)[:, :, bass.ds(pair * P + at, P)]).then_inc(w_loaded, 16)

        def load_w_out(sp, pair):
            sp.dma_start(wo[:], I["L3_xattn_Wo"][bass.ds(pair * P, P), :]).then_inc(wo_loaded, 16)

        def project_pe(pe, bank, name, unit, u):
            if name == "q0" and u == 0:
                first = isinstance(unit, int) and unit == 0
                pe.wait_ge(w_loaded, 64 if first else unit * 32 + 96)
            base = u * SEQ
            if name[0] == "v":
                for chunk in (2 * int(name[1]), 2 * int(name[1]) + 1):
                    at, rows = key_chunk(chunk)
                    out = bank[0:rows, (chunk % 2) * P:(chunk % 2 + 1) * P]
                    for c in range(DC):
                        tokens = chip.xt[:, c, base + at:base + at + rows] if at < SEQ else \
                            chip.ctxt[:, c, u * CTX + at - SEQ:u * CTX + at - SEQ + rows]
                        ins = pe.matmul(out, tokens, w[:, 2 if at < SEQ else 3, c, :], start=c == 0, stop=c == DC - 1)
                return ins
            k = {"q": 0, "k": 1}[name[0]]
            if name == "kc":
                out, source, at, k = bank[:, 0:CTX], chip.ctxt, u * CTX, 3
            else:
                out, source, at = bank[:, 0:BLOCK], chip.xt, base + int(name[1]) * BLOCK
            for c in range(DC):
                ins = pe.matmul(out, w[:, k, c, :], source[:, c, at:at + out.shape[1]], start=c == 0, stop=c == DC - 1)
            return ins

        def w_out_ready(pe, unit, u):
            pe.wait_ge(wo_loaded, unit * 8 + (16 - 8 * u))

        project = Projection(pe=project_pe, act=None, dve=None, kept=None, w_out_ready=w_out_ready,
                                  w_out=lambda unit, u, t: wo[:])

        @block.sync
        def _(sp):
            sp.dma_start(ln_rows[0:DC, :], I["L3_xattn_ln_g"].rearrange("(c p) -> c p", p=P)).then_inc(loaded, 16)
            sp.dma_start(ln_rows[DC:2 * DC, :], I["L3_xattn_ln_b"].rearrange("(c p) -> c p", p=P)).then_inc(loaded, 16)
            sp.dma_start(gb[:], I["L3_xattn_bo"].partition_broadcast(P)).then_inc(loaded, 16)
            load_weights(sp, 0)
            load_w_out(sp, 0)
            with sp.Fori(0, PAIRS - 1) as i:
                uses = a.cycle(i * BATCH)
                sp.wait_ge(a.side_done, uses.done_with("v4"))
                load_weights(sp, i + 1)
                sp.wait_ge(a.side_done, a.cycle(i * BATCH + 2).done_with("o7"))
                load_w_out(sp, i + 1)

        @block.tensor
        def _(pe):
            pe.sem_inc(a.pv_done, PT_SLOTS)
            pe.wait_ge(loaded, 48)
            pe.transpose(a.side[:, 0, 0:2 * DC], ln_rows[:], chip.ident[0:2 * DC, 0:2 * DC]).then_inc(ln_turned, 1)
            turn_pe(pe, chip, turn, a.st_bank)
            pe.wait_ge(turn.turned_read, TURN_BANKS + TILES)
            pe.wait_ge(wo_loaded, 16)
            first_maxima_pe(pe, chip, a, project)
            attention_units(pe, PAIRS, lambda unit, u, following: attention_pe(
                pe, chip, a, unit, u, (a.cycle if following else a.last)(unit), project, following=following))
            last = BATCH * PAIRS - 1
            for name in LAST_OUT:
                side_pe(pe, chip, a, a.epilogue(last), name, last, 1, project)

        @block.scalar
        def _(act):
            act.sem_inc(a.exped, 2)
            act.wait_ge(ln_turned, 1)
            act.copy(ln[:], a.side[:, 0, 0:2 * DC]).then_inc(ln_kept, 1)
            act.wait_ge(ln_kept, 1)
            turn_act(act, chip, turn, a.st_bank, scale=ln[:, 0:DC], bias=ln[:, DC:2 * DC])
            for name in a.parts:
                keep_part_act(act, a, a.prologue, name, 0, 0)
            attention_units(act, PAIRS, lambda unit, u, following: attention_act(
                act, a, unit, u, (a.cycle if following else a.last)(unit), SCALE, project, following=following))

        @block.vector
        def _(dve):
            dve.wait_ge(loaded, 48)
            dve.tensor_scalar(gb[:], gb[:], a.gate, None, ALU.mult).then_inc(gb_made, 1)
            dve.wait_ge(gb_made, 1)
            normalize_twice_dve(dve, chip, norm_steps, x_biased, gb[:])
            normalize_dve(dve, chip, turn, chip.xn)
            for name in Q_PARTS:
                keep_part_dve(dve, a, a.prologue, name, 0, 0)
            first_maxima_dve(dve, a)
            attention_units(dve, PAIRS, lambda unit, u, following: attention_dve(
                dve, chip, a, unit, u, (a.cycle if following else a.last)(unit), project, following=following))
            for name in LAST_OUT:
                add_output(dve, chip, a, a.epilogue(BATCH * PAIRS - 1), name, 1)

        @block.gpsimd
        def _(pool):
            attention_prepare(pool, chip, a)
            pool.wait_ge(a.prepared, PREPARED)
            double_parts(pool, a, 0, 0)
            attention_units(pool, PAIRS, lambda unit, u, following: attention_pool(pool, a, unit, u, following=following))



def l3_ffn(nc, chip, I):
    E, F, K = 32, 256, 4
    G, KEPT_GROUPS = 8, 4
    FC = F // P
    CAP = TOKENS * K * 5 // (E * 4)
    SLOTS_USED = E * CAP
    PIECES = ((0, P), (P, P), (2 * P, CAP - 2 * P))
    FAR = 65536.0
    CLEAR = 8
    CLEARS = SLOTS_USED // (P * CLEAR)
    slots_x = nc.dram_tensor("l3f_slots_x", [SLOTS_USED + K * TOKENS, D], F32, kind="Internal").ap()
    slots_y = nc.dram_tensor("l3f_slots_y", [SLOTS_USED, D], F32, kind="Internal").ap()
    with ExitStack() as stack:
        sb, psum, sem = scope(nc, stack, "l3f")
        wg_rows, wg = sb("wg_rows", [E, D]), sb("wg", [P, DC, E])
        sw1, sw3, sw2 = sb("sw1", [P, DC, F]), sb("sw3", [P, DC, F]), sb("sw2", [P, FC, D])
        w1, w3, w2 = sb("w1", [P, 2, DC, F]), sb("w3", [P, 2, DC, F]), sb("w2", [P, 2, FC, D])
        zeros = sb("zeros", [P, CLEAR * D])
        scores, chosen, product = (sb(n, [P, TILES, E]) for n in ("scores", "chosen", "product"))
        picked = [sb(f"picked{k}", [P, TILES, E]) for k in range(K)]
        groups, group_pick, group_kept, group_order = (sb(n, [P, TILES, G]) for n in ("groups", "group_pick", "group_kept", "group_order"))
        order = sb("order", [P, TILES, E])
        restart, bases, rank, upto = (sb(n, [P, E, TILES]) for n in ("restart", "bases", "rank", "upto"))
        best, total = sb("best", [P, TILES]), sb("total", [P, TILES])
        weight, place, fits, spare = (sb(n, [P, K, TILES]) for n in ("weight", "place", "fits", "spare"))
        scatter_index, gather_index = sb("scatter_index", [P, K, TILES], I32), sb("gather_index", [P, K, TILES], I32)
        z_silu, z_hidden = sb("z_silu", [P, FC, 512]), sb("z_hidden", [P, FC, 512])
        x_rows, xt = sb("x_rows", [P, 2, 3, D]), sb("xt", [P, 2, DC, CAP])
        silu, hidden, y_rows = sb("silu", [P, FC, CAP]), sb("hidden", [P, FC, CAP]), sb("y_rows", [P, 2, 3, D])
        fetched = [chip.xt[:].rearrange("p c (t d) -> p (c t) d", d=D)] + [sb(f"fetched{k}", [P, TILES, D]) for k in range(1, K)]
        p_xt, p_h, p_y = psum("p_xt", [P, DC, 512]), psum("p_h", [P, 4, 512]), psum("p_y", [P, 2, 512])
        turn = TurnSemaphores(sem, "t", keep=True)
        (loaded, s_loaded, zeroed, cleared, constants, norm_steps, wg_turned, wg_kept, routed, exped, chose, ranked, route_steps,
         placed, scattered, z_done, z_silu_kept, z_kept, z_out, z_added, x_turned, xt_kept, h_done, silu_kept, h_kept, y_done,
         y_kept, passed, added) = (sem(n) for n in (
            "loaded", "s_loaded", "zeroed", "cleared", "constants", "norm_steps", "wg_turned", "wg_kept", "routed", "exped", "chose",
            "ranked", "route_steps", "placed", "scattered", "z_done", "z_silu_kept", "z_kept", "z_out", "z_added", "x_turned",
            "xt_kept", "h_done", "silu_kept", "h_kept", "y_done", "y_kept", "passed", "added"))
        w_loaded = [sem("w_loaded0"), sem("w_loaded1")]
        x_loaded = [sem("x_loaded0"), sem("x_loaded1")]
        y_stored = [sem("y_stored0"), sem("y_stored1")]
        gathered = [sem(f"gathered{q}") for q in range(TILES // 2)]
        block = stack.enter_context(nc.Block())

        def load_expert(sp, e, u):
            for w, name, inner in ((w1, "L3_ffn_w1", DC), (w3, "L3_ffn_w3", DC), (w2, "L3_ffn_w2", FC)):
                sp.dma_start(w[:, u, :, :], expert(I[name], e).rearrange("(c p) f -> p c f", p=P)).then_inc(w_loaded[u], 16)

        def slot_rows(slots, rows, e, u):
            last, n = PIECES[2]
            return ((slots[bass.ds(e * CAP, 2 * P), :].rearrange("(t p) d -> p t d", p=P), rows[:, u, 0:2, :]),
                    (slots[bass.ds(e * CAP + last, n), :], rows[0:n, u, 2, :]))

        def load_rows(sp, e, u):
            for dram, rows in slot_rows(slots_x, x_rows, e, u):
                sp.dma_start(rows, dram).then_inc(x_loaded[u], 16)

        def experts(engine, run):
            with engine.Fori(0, E // 2 - 1) as i:
                for u in range(2):
                    run(i * 2 + u, u, i, True)
            for u in range(2):
                run(E - 2 + u, u, E // 2 - 1, False)

        @block.sync
        def _(sp):
            sp.dma_start(wg_rows[:], I["L3_ffn_wg"]).then_inc(loaded, 16)
            for w, name in ((sw1, "L3_ffn_sw1"), (sw3, "L3_ffn_sw3"), (sw2, "L3_ffn_sw2")):
                sp.dma_start(w[:], I[name].rearrange("(c p) f -> p c f", p=P)).then_inc(s_loaded, 16)
            sp.wait_ge(zeroed, 1)
            for n in range(CLEARS):
                rows = slots_x[n * P * CLEAR:(n + 1) * P * CLEAR, :].rearrange("(p n) d -> p (n d)", p=P)
                sp.dma_start(rows, zeros[:]).then_inc(cleared, 16)
            for u in range(2):
                load_expert(sp, u, u)
            sp.wait_ge(placed, 1)
            sp.wait_ge(scattered, 16 * K * TILES)
            for u in range(2):
                load_rows(sp, u, u)

            def run(e, u, i, more):
                if more:
                    sp.wait_ge(x_turned, e + 1)
                    load_rows(sp, e + 2, u)
                    sp.wait_ge(y_done, e * 3 + 3)
                    load_expert(sp, e + 2, u)
            experts(sp, run)

        @block.gpsimd
        def _(pool):
            pool.memset(zeros[:], 0.0).then_inc(zeroed, 1)
            routing_constants(pool, constants, order[:], restart[:], None, ascending=False)
            iota = dict(allow_small_or_imprecise_dtypes=True)
            pool.iota(group_order[:], [[0, TILES], [-1, G]], base=G, channel_multiplier=0, **iota).then_inc(constants, 1)
            pool.iota(bases[:], [[CAP, E], [0, TILES]], base=0, channel_multiplier=0, **iota).then_inc(constants, 1)
            pool.iota(spare[:], [[TOKENS, K], [P, TILES]], base=SLOTS_USED, channel_multiplier=1, **iota).then_inc(constants, 1)
            normalize_pool(pool, chip, turn)
            pool.wait_ge(placed, 1)
            pool.wait_ge(turn.copied, SLOTS + TILES)
            pool.wait_ge(cleared, 16 * CLEARS)
            for t in range(TILES):
                for k in range(K):
                    pool.indirect_dma_start(slots_x, bass.IndirectOffsetOnAxis(scatter_index[:, k, t:t + 1], 0), chip.xn[:, t, :], None
                                            ).then_inc(scattered, 16)

            def run(e, u, i, more):
                pool.wait_ge(y_kept, e * 3 + 3)
                for dram, rows in slot_rows(slots_y, y_rows, e, u):
                    pool.dma_start(dram, rows).then_inc(y_stored[u], 16)
            experts(pool, run)
            for u in range(2):
                pool.wait_ge(y_stored[u], 32 * (E // 2))
            for t in range(TILES):
                for k in range(K):
                    pool.indirect_dma_start(fetched[k][:, t, :], None, slots_y, bass.IndirectOffsetOnAxis(gather_index[:, k, t:t + 1], 0)
                                            ).then_inc(gathered[t // 2], 16)

        @block.tensor
        def _(pe):
            pe.wait_ge(loaded, 16)
            for c in range(DC):
                ins = pe.transpose(p_y[:, 0, c * E:(c + 1) * E], wg_rows[:, c * P:(c + 1) * P], chip.ident[0:E, 0:E])
            ins.then_inc(wg_turned, 1)
            turn_pe(pe, chip, turn, p_xt)
            pe.wait_ge(wg_kept, 1)
            for t in range(TILES):
                pe.wait_ge(turn.turned_read, TURN_BANKS + t + 1)
                for c in range(DC):
                    ins = pe.matmul(p_y[:, 1, t * E:(t + 1) * E], chip.xt[:, c, t * P:(t + 1) * P], wg[:, c, :],
                                    start=c == 0, stop=c == DC - 1)
            ins.then_inc(routed, 1)

            def shared_block(b):
                pe.wait_ge(z_kept, b * FC)
                for f in range(FC):
                    for k, w in ((0, sw1), (2, sw3)):
                        for c in range(DC):
                            ins = pe.matmul(p_h[:, k + f, :], w[:, c, f * P:(f + 1) * P], chip.xt[:, c, b * 512:(b + 1) * 512],
                                            start=c == 0, stop=c == DC - 1)
                    ins.then_inc(z_done, 1)
                for t in range(4):
                    at = 4 * b + t
                    pe.wait_ge(z_kept, (b + 1) * FC)
                    if at >= 2:
                        pe.wait_ge(z_added, at - 1)
                    for f in range(FC):
                        ins = pe.matmul(p_xt[:, t % 2, 0:D], z_hidden[:, f, t * P:(t + 1) * P], sw2[:, f, :],
                                        start=f == 0, stop=f == FC - 1)
                    ins.then_inc(z_out, 1)

            pe.wait_ge(chose, 1)
            rhs = chosen[:].rearrange("p t e -> p e t")
            pe.matmul(p_y[:, 0, :].rearrange("p (e t) -> p e t", e=E), chip.before[:], rhs, start=True, stop=True)
            pe.matmul(p_y[:, 1, :].rearrange("p (e t) -> p e t", e=E), chip.ones[:], rhs, start=True, stop=True).then_inc(ranked, 1)
            pe.wait_ge(s_loaded, 48)
            for b in range(4):
                shared_block(b)

            def turn_rows(e, u, i):
                pe.wait_ge(x_loaded[u], i * 32 + 32)
                pe.wait_ge(xt_kept, e * DC)
                for c in range(DC):
                    for j, (at, n) in enumerate(PIECES):
                        ins = pe.transpose(p_xt[:, c, at:at + n], x_rows[0:n, u, j, c * P:(c + 1) * P], chip.ident[0:n, 0:n])
                ins.then_inc(x_turned, 1)

            def run(e, u, i, more):
                pe.wait_ge(w_loaded[u], i * 48 + 48)
                pe.wait_ge(xt_kept, e * DC + DC)
                for f in range(FC):
                    pe.wait_ge(h_kept, e * FC + f)
                    for k, w in ((0, w1), (2, w3)):
                        for c in range(DC):
                            ins = pe.matmul(p_h[:, k + f, 0:CAP], w[:, u, c, f * P:(f + 1) * P], xt[:, u, c, :],
                                            start=c == 0, stop=c == DC - 1)
                    ins.then_inc(h_done, 1)
                if more or u == 0:
                    turn_rows(e + 1, 1 - u, i + u)
                pe.wait_ge(h_kept, e * FC + FC)
                pe.wait_ge(y_kept, e * 3)
                for j, (at, n) in enumerate(PIECES):
                    for f in range(FC):
                        ins = pe.matmul(p_y[0:n, j // 2, j % 2 * D:j % 2 * D + D], hidden[:, f, at:at + n], w2[:, u, f, :],
                                        start=f == 0, stop=f == FC - 1)
                    ins.then_inc(y_done, 1)

            pe.wait_ge(z_added, TILES)
            turn_rows(0, 0, 0)
            experts(pe, run)

        @block.scalar
        def _(act):
            turn_act(act, chip, turn, p_xt)
            act.wait_ge(route_steps, 2)
            act.activation(scores[:], scores[:], ACT.Exp).then_inc(exped, 1)
            for b in range(4):
                for f in range(FC):
                    act.wait_ge(z_done, b * FC + f + 1)
                    if b >= 1:
                        act.wait_ge(z_kept, (b - 1) * FC + f + 1)
                    act.activation(z_silu[:, f, :], p_h[:, f, :], ACT.Silu).then_inc(z_silu_kept, 1)

            def run(e, u, i, more):
                for f in range(FC):
                    act.wait_ge(h_done, e * FC + (f + 1))
                    act.wait_ge(h_kept, e * FC + f)
                    act.activation(silu[:, f, :], p_h[:, f, 0:CAP], ACT.Silu).then_inc(silu_kept, 1)
            experts(act, run)

        @block.vector
        def _(dve):
            row_statistics(dve, chip, norm_steps, 0, chip.x)
            dve.wait_ge(wg_turned, 1)
            dve.tensor_copy(wg[:], p_y[:, 0, 0:DC * E].rearrange("p (c e) -> p c e", c=DC)).then_inc(wg_kept, 1)
            normalize_dve(dve, chip, turn, chip.x)
            dve.wait_ge(routed, 1)
            step = Steps(dve, route_steps)
            p_logits = p_y[:, 1, :].rearrange("p (t e) -> p t e", e=E)
            step(dve.tensor_reduce(best[:], p_logits, AX.X, ALU.max))
            step(dve.tensor_tensor(scores[:], p_logits, spread(best[:], E), ALU.subtract))
            dve.wait_ge(exped, 1)
            step(dve.tensor_reduce(total[:], scores[:], AX.X, ALU.add))
            step(dve.reciprocal(total[:], total[:]))
            step(dve.tensor_tensor(scores[:], scores[:], spread(total[:], E), ALU.mult))
            dve.wait_ge(constants, 5)
            step(dve.tensor_scalar(restart[:], restart[:], 0.0, None, ALU.is_gt))
            step(dve.tensor_reduce(groups[:].rearrange("p t g -> p (t g)"), scores[:].rearrange("p t (g n) -> p (t g) n", g=G), AX.X, ALU.max))
            for k in range(KEPT_GROUPS):
                choose(dve, step, groups[:], group_pick[:], group_order[:], total[:], best[:], 2.0)
            step(dve.tensor_scalar(group_kept[:], groups[:], 0.0, 2.0, ALU.is_ge, ALU.mult))
            step(dve.tensor_tensor(scores[:].rearrange("p t (g n) -> p (t g) n", g=G), scores[:].rearrange("p t (g n) -> p (t g) n", g=G),
                                   spread(group_kept[:].rearrange("p t g -> p (t g)"), E // G), ALU.subtract))
            for k in range(K):
                choose(dve, step, scores[:], picked[k][:], order[:], weight[:, k, :], best[:], 2.0)
            step(dve.tensor_tensor(chosen[:], picked[0][:], picked[1][:], ALU.add))
            for k in range(2, K):
                step(dve.tensor_tensor(chosen[:], chosen[:], picked[k][:], ALU.add))
            dve.sem_inc(chose, 1)
            step(dve.tensor_reduce(total[:], weight[:].rearrange("p k t -> p t k"), AX.X, ALU.add))
            step(dve.tensor_scalar(total[:], total[:], 1e-9, None, ALU.add))
            step(dve.reciprocal(total[:], total[:]))
            step(dve.tensor_scalar(total[:], total[:], chip.gates[:, 7:8], None, ALU.mult))
            step(dve.tensor_tensor(weight[:], weight[:], total[:].unsqueeze(1).to_broadcast([P, K, TILES]), ALU.mult))
            dve.wait_ge(ranked, 1)
            within, tile_total = (p_y[:, n, :].rearrange("p (e t) -> p e t", e=E) for n in range(2))
            ranks_dve(dve, step, rank[:], upto[:], within, tile_total, restart[:])
            step(dve.tensor_scalar(upto[:], rank[:], float(CAP), FAR, ALU.is_ge, ALU.mult))
            step(dve.tensor_tensor(rank[:], rank[:], upto[:], ALU.add))
            step(dve.tensor_tensor(rank[:], rank[:], bases[:], ALU.add))
            for k in range(K):
                step(dve.tensor_tensor(product[:], picked[k][:], rank[:].rearrange("p e t -> p t e"), ALU.mult))
                step(dve.tensor_reduce(place[:, k, :], product[:], AX.X, ALU.add))
            step(dve.tensor_scalar(fits[:], place[:], FAR, None, ALU.is_lt))
            step(dve.tensor_tensor(place[:], place[:], fits[:], ALU.mult))
            step(dve.tensor_copy(gather_index[:], place[:]))
            step(dve.tensor_tensor(weight[:], weight[:], fits[:], ALU.mult))
            step(dve.tensor_scalar(fits[:], fits[:], -1.0, 1.0, ALU.mult, ALU.add))
            step(dve.tensor_tensor(fits[:], fits[:], spare[:], ALU.mult))
            step(dve.tensor_tensor(place[:], place[:], fits[:], ALU.add))
            step(dve.tensor_copy(scatter_index[:], place[:]))
            dve.sem_inc(placed, 1)
            for b in range(4):
                for f in range(FC):
                    dve.wait_ge(z_silu_kept, b * FC + f + 1)
                    if b >= 1:
                        dve.wait_ge(z_out, 4 * b)
                    dve.tensor_tensor(z_hidden[:, f, :], z_silu[:, f, :], p_h[:, 2 + f, :], ALU.mult).then_inc(z_kept, 1)
                for t in range(4 * b, 4 * b + 4):
                    dve.wait_ge(z_out, t + 1)
                    dve.scalar_tensor_tensor(chip.x[:, t, :], p_xt[:, t % 2, 0:D], chip.gates[:, 7:8], chip.x[:, t, :],
                                             ALU.mult, ALU.add).then_inc(z_added, 1)

            def keep_xt(e, u):
                dve.wait_ge(x_turned, e + 1)
                for c in range(DC):
                    dve.tensor_copy(xt[:, u, c, :], p_xt[:, c, 0:CAP]).then_inc(xt_kept, 1)

            def run(e, u, i, more):
                for f in range(FC):
                    dve.wait_ge(silu_kept, e * FC + (f + 1))
                    dve.wait_ge(y_done, e * 3)
                    dve.tensor_tensor(hidden[:, f, :], silu[:, f, :], p_h[:, 2 + f, 0:CAP], ALU.mult).then_inc(h_kept, 1)
                if more or u == 0:
                    keep_xt(e + 1, 1 - u)
                dve.wait_ge(y_stored[u], i * 32)
                dve.wait_ge(y_done, e * 3 + 2)
                dve.tensor_copy(y_rows[:, u, 0:2, :].rearrange("p j d -> p (j d)"), p_y[:, 0, :]).then_inc(y_kept, 2)
                dve.wait_ge(y_done, e * 3 + 3)
                rows = PIECES[2][1]
                dve.tensor_copy(y_rows[0:rows, u, 2, :], p_y[0:rows, 1, 0:D]).then_inc(y_kept, 1)

            keep_xt(0, 0)
            experts(dve, run)
            for t in range(TILES):
                if t % 2 == 0:
                    dve.wait_ge(gathered[t // 2], 2 * K * 16)
                step = Steps(dve, added, K * t)
                for k in range(K):
                    step(dve.scalar_tensor_tensor(chip.x[:, t, :], fetched[k][:, t, :], weight[:, k, t:t + 1], chip.x[:, t, :],
                                                  ALU.mult, ALU.add))


def store(nc, chip, out):
    with ExitStack() as stack:
        _, _, sem = scope(nc, stack, "store")
        stored = sem("stored")
        block = stack.enter_context(nc.Block())

        @block.sync
        def _(sp):
            sp.dma_start(out.rearrange("b (t p) d -> p (b t) d", p=P), chip.x[:]).then_inc(stored, 16)
            sp.wait_ge(stored, 16)


def build(nc, I, out):
    with ExitStack() as stack:
        chip = Chip(nc, stack)
        setup(nc, chip, I)
        l0_attention(nc, chip, I)
        l0_ffn(nc, chip, I)
        l1_attention(nc, chip, I)
        l1_ffn(nc, chip, I)
        l2_attention(nc, chip, I)
        l2_ffn(nc, chip, I)
        l3_attention(nc, chip, I)
        l3_ffn(nc, chip, I)
        store(nc, chip, out)


def kernel(**inputs):
    import numpy as np
    import concourse.bacc as bacc
    from concourse.bass_utils import run_bass_kernel_spmd

    nc = bacc.Bacc("TRN2", target_bir_lowering=False, num_devices=1)
    arrays, I = {}, {}
    for name in inputs:
        a = np.ascontiguousarray(inputs[name])
        arrays[f"in_{name}"] = a
        I[name] = nc.dram_tensor(f"in_{name}", a.shape, mybir.dt.from_np(a.dtype), kind="ExternalInput").ap()
    out = nc.dram_tensor("out_0_dram", (BATCH, SEQ, D), F32, kind="ExternalOutput").ap()
    build(nc, I, out)
    r = run_bass_kernel_spmd(nc, [arrays], core_ids=[0])
    return r.results[0]["out_0_dram"]
```

```python
from contextlib import ExitStack, contextmanager

import concourse.bass as bass
from concourse import mybir

F32 = mybir.dt.float32
F32R = mybir.dt.float32r
I32 = mybir.dt.int32
U32 = mybir.dt.uint32
ALU = mybir.AluOpType
ACT = mybir.ActivationFunctionType
AX = mybir.AxisListType

P = 128
BATCH, SEQ, D = 2, 1024, 256
TOKENS = BATCH * SEQ
TILES = TOKENS // P
BATCH_TILES = SEQ // P
DC = D // P
CTX = 154
CTX_REST = CTX - P
CHUNKS = ((0, P), (P, CTX_REST))
EPS = 1e-5
TURN_BANKS = 4


class Steps:

    def __init__(self, engine, sem, first=0):
        self.engine, self.sem, self.first, self.n = engine, sem, first, 0

    def __call__(self, instruction):
        instruction.then_inc(self.sem, 1)
        self.wait()

    def wait(self):
        self.n += 1
        self.engine.wait_ge(self.sem, self.first + self.n)


def tile_of(tensor, t):
    return tensor[:, bass.ds(t, 1), :].rearrange("p a d -> p (a d)")


def expert(weights, e):
    return weights[bass.ds(e, 1), :, :].rearrange("a r c -> (a r) c")


def column(tensor, c):
    return tensor[:, bass.ds(c, 1)]



ROOT_STEPS = 12
NORM_STEPS = TILES + 6 + ROOT_STEPS


def inverse_root(dve, step, out, value, scale, eps, scratch):
    v, half = scratch
    step(dve.tensor_scalar(v, value, scale, eps, ALU.mult, ALU.add))
    step(dve.tensor_scalar(half.bitcast(I32), v.bitcast(I32), 1, None, ALU.logical_shift_right))
    step(dve.tensor_scalar(out.bitcast(I32), half.bitcast(I32), -1.0, float(0x5F3759DF), ALU.mult, ALU.add))
    for _ in range(3):
        step(dve.tensor_tensor(half, out, out, ALU.mult))
        step(dve.scalar_tensor_tensor(half, half, -0.5, v, ALU.mult, ALU.mult))
        step(dve.scalar_tensor_tensor(out, half, 1.5, out, ALU.add, ALU.mult))


def row_statistics(dve, chip, sem, first, source):
    with dve.Fori(0, TILES // 4) as i:
        for u in range(4):
            dve.bn_stats(tile_of(chip.stats, i * 4 + u), tile_of(source, i * 4 + u)).then_inc(sem, 1)
    dve.wait_ge(sem, first + TILES)
    aggregate(dve, sem, first + TILES, chip.stats[:], chip.mean[:], chip.inv_std[:],
              (chip.small_a[:], chip.small_b[:], chip.small_c[:]))


AGGREGATE_STEPS = 6 + ROOT_STEPS


def aggregate(dve, sem, first, stats, mean, inv_std, small):
    mean_even, m2_even, mean_odd, m2_odd = (stats[:, :, k] for k in (1, 2, 4, 5))
    a, b, c = small
    dve.tensor_tensor(mean, mean_even, mean_odd, ALU.add).then_inc(sem, 1)
    dve.tensor_tensor(a, mean_even, mean_odd, ALU.subtract).then_inc(sem, 1)
    dve.tensor_tensor(b, m2_even, m2_odd, ALU.add).then_inc(sem, 1)
    dve.wait_ge(sem, first + 3)
    step = Steps(dve, sem, first + 3)
    step(dve.tensor_scalar(mean, mean, 0.5, None, ALU.mult))
    step(dve.tensor_tensor(a, a, a, ALU.mult))
    step(dve.scalar_tensor_tensor(a, a, D / 4.0, b, ALU.mult, ALU.add))
    inverse_root(dve, step, inv_std, a, 1.0 / D, EPS, (b, c))


def normalize_dve(dve, chip, s, source):
    for t in range(TILES):
        dve.tensor_scalar(chip.xn[:, t, :], source[:, t, :], chip.mean[:, t:t + 1], chip.inv_std[:, t:t + 1],
                          ALU.subtract, ALU.mult).then_inc(s.staged, 1)


def turn_pe(pe, chip, s, psum):
    for t in range(TILES):
        pe.wait_ge(s.staged, t + 1)
        if t >= TURN_BANKS:
            pe.wait_ge(s.turned_read, t + 1 - TURN_BANKS)
        for c in range(DC):
            ins = pe.transpose(psum[:, t % TURN_BANKS, c * P:(c + 1) * P], chip.xn[:, t, c * P:(c + 1) * P], chip.ident[:])
        ins.then_inc(s.turned, 1)


def turn_act(act, chip, s, psum, scale=None, bias=None):
    for t in range(TILES):
        act.wait_ge(s.turned, t + 1)
        tokens = slice(t * P, (t + 1) * P)
        if scale is None:
            act.copy(chip.xt[:, :, tokens],
                     psum[:, t % TURN_BANKS, 0:D].rearrange("p (c t) -> p c t", c=DC)).then_inc(s.turned_read, 1)
        else:
            for c in range(DC):
                ins = act.activation(chip.xt[:, c, tokens], psum[:, t % TURN_BANKS, c * P:(c + 1) * P],
                                     ACT.Identity, bias=bias[:, c:c + 1], scale=scale[:, c:c + 1])
            ins.then_inc(s.turned_read, 1)


class TurnSemaphores:
    def __init__(self, sem, stage):
        self.staged, self.turned, self.turned_read = sem(f"{stage}_staged"), sem(f"{stage}_turned"), sem(f"{stage}_turned_read")


def scope(nc, stack, stage, clear=True):
    def sb(name, shape, dtype=F32):
        return stack.enter_context(nc.sbuf_tensor(f"{stage}_{name}", shape, dtype))

    def psum(name, shape, dtype=F32):
        return stack.enter_context(nc.psum_tensor(f"{stage}_{name}", shape, dtype))

    semaphores = []

    def sem(name):
        semaphores.append(nc.alloc_semaphore(name=f"{stage}_{name}"))
        return semaphores[-1]

    def release():
        nc.all_engine_barrier()
        nc.clear_and_free_semaphores(semaphores)
        nc.all_engine_barrier()

    if clear:
        stack.callback(release)
    return sb, psum, sem



class Chip:
    def __init__(self, nc, stack):
        sb, _, _ = scope(nc, stack, "chip", clear=False)
        self.x = sb("x", [P, TILES, D])
        self.xt = sb("xt", [P, DC, TOKENS])
        self.stage = sb("stage", [P, 2, D])
        self.stats = sb("stats", [P, TILES, 6])
        self.mean = sb("mean", [P, TILES])
        self.inv_std = sb("inv_std", [P, TILES])
        self.small_a = sb("small_a", [P, TILES])
        self.small_b = sb("small_b", [P, TILES])
        self.small_c = sb("small_c", [P, TILES])
        self.xn = sb("xn", [P, TILES, D])
        self.before = sb("before", [P, P])
        self.ident = sb("ident", [P, P])
        self.ones = sb("ones", [P, P])
        self.gates = sb("gates", [P, 8])
        self.ctx = sb("ctx", [P, BATCH, 2, D])
        self.ctxt = sb("ctxt", [P, DC, BATCH * CTX])


def setup(nc, chip, I):
    with ExitStack() as stack:
        sb, psum, sem = scope(nc, stack, "setup")
        turned = psum("turned", [P, 4, 512])
        loaded, made, ident_made, ctx_turned, ctx_kept, tanh_done = (
            sem(n) for n in ("loaded", "made", "ident_made", "ctx_turned", "ctx_kept", "tanh_done"))
        block = stack.enter_context(nc.Block())

        @block.sync
        def _(sp):
            for b in range(BATCH):
                for c, (row, rows) in enumerate(CHUNKS):
                    sp.dma_start(chip.ctx[0:rows, b, c, :], I["ctx_1024"][b, row:row + rows, :]).then_inc(loaded, 16)
            sp.dma_start(chip.x[:], I["x"].rearrange("b (t p) d -> p (b t) d", p=P)).then_inc(loaded, 16)
            sp.dma_start(chip.gates[:, 0:4], I["g_xattn"].partition_broadcast(P)).then_inc(loaded, 16)
            sp.dma_start(chip.gates[:, 4:8], I["g_ffn"].partition_broadcast(P)).then_inc(loaded, 16)

        @block.gpsimd
        def _(pool):
            pool.memset(chip.ones[:], 1.0).then_inc(made, 1)
            pool.wait_ge(made, 1)
            pool.affine_select(out=chip.ident[:], in_=chip.ones[:], compare_op=ALU.is_equal, fill=0.0,
                               base=0, pattern=[[-1, P]], channel_multiplier=1).then_inc(ident_made, 1)
            pool.affine_select(out=chip.before[:], in_=chip.ones[:], compare_op=ALU.is_gt, fill=0.0,
                               base=0, pattern=[[1, P]], channel_multiplier=-1).then_inc(ident_made, 1)

        @block.tensor
        def _(pe):
            pe.wait_ge(ident_made, 1)
            pe.wait_ge(loaded, 7 * 16)
            for b in range(BATCH):
                for c, (row, rows) in enumerate(CHUNKS):
                    for d in range(DC):
                        ins = pe.transpose(turned[:, b * 2 + c, d * P:d * P + rows],
                                           chip.ctx[0:rows, b, c, d * P:(d + 1) * P], chip.ident[0:rows, 0:rows])
            ins.then_inc(ctx_turned, 1)

        @block.vector
        def _(dve):
            dve.wait_ge(ctx_turned, 1)
            for b in range(BATCH):
                for c, (row, rows) in enumerate(CHUNKS):
                    at = b * CTX + row
                    dve.tensor_copy(chip.ctxt[:, :, at:at + rows],
                                    turned[:, b * 2 + c, 0:D].rearrange("p (d r) -> p d r", d=DC)[:, :, 0:rows]
                                    ).then_inc(ctx_kept, 1)

        @block.scalar
        def _(act):
            act.wait_ge(loaded, 7 * 16)
            act.activation(chip.gates[:], chip.gates[:], ACT.Tanh).then_inc(tanh_done, 1)



def l0_attention(nc, chip, I):
    with ExitStack() as stack:
        sb, psum, sem = scope(nc, stack, "l0a")
        wq, wk, wv = (sb(n, [P, DC, D]) for n in ("wq", "wk", "wv"))
        wvt, wqk_t = sb("wvt", [P, DC, D]), sb("wqk_t", [P, DC, D])
        keys = sb("keys", [P, DC, BATCH * CTX])
        values = sb("values", [P, BATCH, 2, D])
        xt = sb("xt", [P, 2, DC, P])
        probs = sb("probs", [P, 2, CTX])
        probs_t = sb("probs_t", [P, 2, 2, P])
        neg_max, total, factor = sb("neg_max", [P, 2]), sb("total", [P, 2]), sb("factor", [P, 2])
        pa = psum("pa", [P, 2, 512])
        pb = psum("pb", [P, 2, 512])
        pc = psum("pc", [P, 2, 512])
        pd = psum("pd", [P, 2, 512])
        w_loaded, wv_turned, wv_kept, wqk_done, wqk_kept, keys_done, keys_kept = (sem(n) for n in (
            "w_loaded", "wv_turned", "wv_kept", "wqk_done", "wqk_kept", "keys_done", "keys_kept"))
        values_done, values_kept, norm_steps, staged, turned, xt_kept = (sem(n) for n in (
            "values_done", "values_kept", "norm_steps", "staged", "turned", "xt_kept"))
        scored, maxed, exped, probs_turned, probs_kept, out_done, dve_steps = (sem(n) for n in (
            "scored", "maxed", "exped", "probs_turned", "probs_kept", "out_done", "dve_steps"))
        block = stack.enter_context(nc.Block())

        @block.sync
        def _(sp):
            for w, name in ((wv, "L0_xattn_w_v"), (wk, "L0_xattn_w_k"), (wq, "L0_xattn_w_q")):
                sp.dma_start(w[:], I[name].rearrange("(c p) d -> p c d", p=P)).then_inc(w_loaded, 16)

        @block.tensor
        def _(pe):
            pe.wait_ge(w_loaded, 48)
            for o in range(DC):
                for d in range(DC):
                    ins = pe.transpose(pa[:, d, o * P:(o + 1) * P], wv[:, o, d * P:(d + 1) * P], chip.ident[:])
            ins.then_inc(wv_turned, 1)
            for d in range(DC):
                for o in range(DC):
                    ins = pe.matmul(pb[:, d, 0:D], wk[:, o, d * P:(d + 1) * P], wq[:, o, :], start=o == 0, stop=o == DC - 1)
            ins.then_inc(wqk_done, 1)
            pe.wait_ge(wqk_kept, 1)
            for d in range(DC):
                for e in range(DC):
                    ins = pe.matmul(pc[:, d, 0:BATCH * CTX], wqk_t[:, e, d * P:(d + 1) * P], chip.ctxt[:, e, :],
                                    start=e == 0, stop=e == DC - 1)
            ins.then_inc(keys_done, 1)
            pe.wait_ge(wv_kept, 1)
            for b in range(BATCH):
                for c, (row, rows) in enumerate(CHUNKS):
                    at = b * CTX + row
                    for d in range(DC):
                        ins = pe.matmul(pd[0:rows, b, c * D:(c + 1) * D], chip.ctxt[:, d, at:at + rows], wvt[:, d, :],
                                        start=d == 0, stop=d == DC - 1)
            ins.then_inc(values_done, 1)
            pe.wait_ge(keys_kept, 1)
            pe.wait_ge(values_kept, 2 * BATCH)
            with pe.Fori(0, BATCH_TILES) as i:
                for u in range(BATCH):
                    pe.wait_ge(staged, i * 2 + (u + 1))
                    for c in range(DC):
                        ins = pe.transpose(pa[:, u, c * P:(c + 1) * P], chip.stage[:, u, c * P:(c + 1) * P], chip.ident[:])
                    ins.then_inc(turned, 1)
                for u in range(BATCH):
                    pe.wait_ge(xt_kept, i * 2 + (u + 1))
                    for c in range(DC):
                        ins = pe.matmul(pb[:, u, 0:CTX], xt[:, u, c, :], keys[:, c, u * CTX:(u + 1) * CTX],
                                        start=c == 0, stop=c == DC - 1)
                    ins.then_inc(scored, 1)
                for u in range(BATCH):
                    pe.wait_ge(exped, i * 2 + (u + 1))
                    for c, (row, rows) in enumerate(CHUNKS):
                        ins = pe.transpose(pc[0:rows, u, c * P:(c + 1) * P], probs[:, u, row:row + rows], chip.ident[:])
                    ins.then_inc(probs_turned, 1)
                for u in range(BATCH):
                    pe.wait_ge(probs_kept, i * 4 + (2 * u + 2))
                    for c, (row, rows) in enumerate(CHUNKS):
                        ins = pe.matmul(pd[:, u, 0:D], probs_t[0:rows, u, c, :], values[0:rows, u, c, :],
                                        start=c == 0, stop=c == 1)
                    ins.then_inc(out_done, 1)

        @block.scalar
        def _(act):
            act.wait_ge(wqk_done, 1)
            act.copy(wqk_t[:], pb[:, :, 0:D]).then_inc(wqk_kept, 1)
            act.wait_ge(keys_done, 1)
            act.mul(keys[:], pc[:, :, 0:BATCH * CTX], D ** -0.5).then_inc(keys_kept, 1)
            with act.Fori(0, BATCH_TILES) as i:
                for u in range(BATCH):
                    act.wait_ge(turned, i * 2 + (u + 1))
                    act.copy(xt[:, u, :, :], pa[:, u, 0:D].rearrange("p (c t) -> p c t", c=DC)).then_inc(xt_kept, 1)
                for u in range(BATCH):
                    act.wait_ge(maxed, i * 2 + (u + 1))
                    act.activation(probs[:, u, :], pb[:, u, 0:CTX], ACT.Exp, bias=neg_max[:, u:u + 1],
                                   accum_out=total[:, u:u + 1]).then_inc(exped, 1)

        @block.vector
        def _(dve):
            row_statistics(dve, chip, norm_steps, 0, chip.x)
            dve.wait_ge(wv_turned, 1)
            dve.tensor_copy(wvt[:], pa[:, :, 0:D]).then_inc(wv_kept, 1)
            dve.wait_ge(values_done, 1)
            for b in range(BATCH):
                for c, (row, rows) in enumerate(CHUNKS):
                    dve.tensor_copy(values[0:rows, b, c, :], pd[0:rows, b, c * D:(c + 1) * D]).then_inc(values_kept, 1)
            with dve.Fori(0, BATCH_TILES) as i:
                for u in range(BATCH):
                    t = i + u * BATCH_TILES
                    dve.tensor_scalar(chip.stage[:, u, :], tile_of(chip.x, t), column(chip.mean, t),
                                      column(chip.inv_std, t), ALU.subtract, ALU.mult).then_inc(staged, 1)
                for u in range(BATCH):
                    dve.wait_ge(scored, i * 2 + (u + 1))
                    dve.tensor_reduce(neg_max[:, u:u + 1], pb[:, u, 0:CTX], AX.X, ALU.max, negate=True).then_inc(maxed, 1)
                for u in range(BATCH):
                    dve.wait_ge(probs_turned, i * 2 + (u + 1))
                    for c, (row, rows) in enumerate(CHUNKS):
                        dve.tensor_copy(probs_t[0:rows, u, c, :], pc[0:rows, u, c * P:(c + 1) * P]).then_inc(probs_kept, 1)
                for u in range(BATCH):
                    t = i + u * BATCH_TILES
                    step = Steps(dve, dve_steps, i * 6 + 3 * u)
                    step(dve.reciprocal(factor[:, u:u + 1], total[:, u:u + 1]))
                    step(dve.tensor_scalar(factor[:, u:u + 1], factor[:, u:u + 1], chip.gates[:, 0:1], None, ALU.mult))
                    dve.wait_ge(out_done, i * 2 + (u + 1))
                    step(dve.scalar_tensor_tensor(tile_of(chip.x, t), pd[:, u, 0:D], factor[:, u:u + 1], tile_of(chip.x, t),
                                                  ALU.mult, ALU.add))



def spread(ap, n):
    return ap.unsqueeze(2).to_broadcast([ap.shape[0], ap.shape[1], n])


def choose(dve, step, scores, onehot, order, value, best, drop):
    n = scores.shape[2]
    step(dve.tensor_reduce(value, scores, AX.X, ALU.max))
    step(dve.tensor_tensor(onehot, scores, spread(value, n), ALU.is_equal))
    step(dve.tensor_tensor(onehot, onehot, order, ALU.mult))
    step(dve.tensor_reduce(best, onehot, AX.X, ALU.max))
    step(dve.tensor_tensor(onehot, onehot, spread(best, n), ALU.is_equal))
    if drop:
        step(dve.scalar_tensor_tensor(scores, onehot, -drop, scores, ALU.mult, ALU.add))


def rank_pe(pe, chip, chosen, within, total):
    rhs = chosen.rearrange("p t e -> p e t")
    pe.matmul(within, chip.before[:], rhs, start=True, stop=True)
    return pe.matmul(total, chip.ones[:], rhs, start=True, stop=True)


def ranks_dve(dve, step, rank, upto, within, total, restart):
    flat = "p e t -> p (e t)"
    step(dve.tensor_tensor_scan(upto.rearrange(flat), restart.rearrange(flat), total.rearrange(flat), 0.0, ALU.mult, ALU.add))
    step(dve.tensor_tensor(rank, within, upto, ALU.add))
    step(dve.tensor_tensor(rank, rank, total, ALU.subtract))


def slots_dve(dve, step, slot, onehot, product, place, index):
    step(dve.tensor_tensor(product, onehot, slot.rearrange("p e t -> p t e"), ALU.mult))
    step(dve.tensor_reduce(place, product, AX.X, ALU.add))
    step(dve.tensor_copy(index, place))


def expert_bases(dve, step, ones, rank, upto, compare, thresholds, tiles, ends, tile_counts):
    experts = tiles.shape[1]
    step(dve.tensor_tensor(compare, spread(upto[:, :, TILES - 1], TILES), thresholds, ALU.is_gt))
    step(dve.tensor_reduce(tiles, compare, AX.X, ALU.add))
    step(dve.tensor_scalar(tiles, tiles, 1.0, None, ALU.max))
    step(dve.tensor_copy(tile_counts, tiles))
    step(dve.tensor_tensor_scan(ends, ones[:, 0:experts], tiles, 0.0, ALU.mult, ALU.add))
    step(dve.tensor_tensor(ends, ends, tiles, ALU.subtract))
    step(dve.scalar_tensor_tensor(rank, spread(ends, TILES), float(P), rank, ALU.mult, ALU.add))


def routing_constants(pool, sem, order, restart, thresholds, ascending):
    experts = order.shape[2]
    step = 1 if ascending else -1
    pool.iota(order, [[0, TILES], [step, experts]], base=1 if ascending else experts, channel_multiplier=0,
              allow_small_or_imprecise_dtypes=True).then_inc(sem, 1)
    if thresholds is not None:
        pool.iota(thresholds, [[0, experts], [P, TILES]], base=0, channel_multiplier=0,
                  allow_small_or_imprecise_dtypes=True).then_inc(sem, 1)
    pool.iota(restart, [[0, experts], [1, TILES]], base=0, channel_multiplier=0,
              allow_small_or_imprecise_dtypes=True).then_inc(sem, 1)


@contextmanager
def tiles_of_expert(engine, tile_counts, e, g, max_tiles):
    n = engine.value_load(tile_counts[0:1, bass.ds(e, 1)], min_val=1, max_val=TILES)
    with engine.Fori(0, n):
        yield engine.snap(g, min_val=1, max_val=max_tiles)
        engine.reg_add(g, g, 1)


def one_register(engine, name):
    g = engine.alloc_register(name)
    engine.reg_mov(g, 1)
    return g



def l0_ffn(nc, chip, I):
    E, F = 8, 1024
    FC = F // P
    HB = 4
    CB = FC // HB
    MAX_TILES = TILES + E - 1
    SLOT_TILES = MAX_TILES + 1
    slots_x = nc.dram_tensor("l0f_slots_x", [SLOT_TILES * P, D], F32, kind="Internal").ap()
    slots_y = nc.dram_tensor("l0f_slots_y", [SLOT_TILES * P, D], F32, kind="Internal").ap()
    with ExitStack() as stack:
        sb, psum, sem = scope(nc, stack, "l0f")
        wr = sb("wr", [P, DC, E])
        w1, w2 = sb("w1", [P, 2, DC, F]), sb("w2", [P, 2, FC, D])
        b1_rows, b1 = sb("b1_rows", [E * FC, P]), sb("b1", [P, E * FC])
        b2 = sb("b2", [P, E, D])
        zeros = sb("zeros", [P, 2048])
        logits, exps, chosen, product = (sb(n, [P, TILES, E]) for n in ("logits", "exps", "chosen", "product"))
        order = sb("order", [P, TILES, E])
        restart, thresholds, rank, upto, compare = (sb(n, [P, E, TILES]) for n in ("restart", "thresholds", "rank", "upto", "compare"))
        best, weight, place = (sb(n, [P, TILES]) for n in ("best", "weight", "place"))
        tiles, ends = sb("tiles", [P, E]), sb("ends", [P, E])
        tile_counts, index = sb("tile_counts", [P, E], I32), sb("index", [P, TILES], I32)
        x_tile, xt_tile = sb("x_tile", [P, D]), sb("xt_tile", [P, D])
        hidden, y_tile = sb("hidden", [P, FC, P]), sb("y_tile", [P, D])
        fetched = sb("fetched", [P, TILES, D])
        p_route = psum("p_route", [P, 512])
        p_xt = psum("p_xt", [P, 512])
        p_hidden = psum("p_hidden", [P, HB, 512])
        p_y = psum("p_y", [P, 512])
        turn = TurnSemaphores(sem, "t")
        (loaded, b_loaded, b2_loaded, zeroed, cleared, constants, norm_steps, b1_turned, b1_kept, routed, exped, chose, ranked, route_steps,
         placed, scattered, x_loaded, x_turned, x_kept, h_done, h_kept, y_done, y_kept, y_stored, added, y_free, passed) = (sem(n) for n in (
            "loaded", "b_loaded", "b2_loaded", "zeroed", "cleared", "constants", "norm_steps", "b1_turned", "b1_kept", "routed", "exped", "chose", "ranked",
            "route_steps", "placed", "scattered", "x_loaded", "x_turned", "x_kept", "h_done", "h_kept", "y_done", "y_kept",
            "y_stored", "added", "y_free", "passed"))
        gathered = [sem(f"gathered{q}") for q in range(TILES // 4)]
        w_loaded = [sem("w_loaded0"), sem("w_loaded1")]
        block = stack.enter_context(nc.Block())
        CLEARS = 2 * -(-SLOT_TILES // 8)

        def load_expert(engine, e, u):
            engine.dma_start(w1[:, u, :, :], expert(I["L0_ffn_W1"], e).rearrange("(c p) f -> p c f", p=P)).then_inc(w_loaded[u], 16)
            engine.dma_start(w2[:, u, :, :], expert(I["L0_ffn_W2"], e).rearrange("(c p) d -> p c d", p=P)).then_inc(w_loaded[u], 16)

        @block.sync
        def _(sp):
            sp.dma_start(wr[:], I["L0_ffn_Wr"].rearrange("(c p) e -> p c e", p=P)).then_inc(loaded, 16)
            sp.dma_start(b1_rows[:], I["L0_ffn_b1"].rearrange("e (c p) -> (e c) p", p=P)).then_inc(b_loaded, 16)
            sp.wait_ge(zeroed, 1)
            for slots in (slots_x, slots_y):
                for t in range(0, SLOT_TILES, 8):
                    n = min(8, SLOT_TILES - t)
                    sp.dma_start(slots[t * P:(t + n) * P, :].rearrange("(p n) d -> p (n d)", p=P), zeros[:, 0:n * D]).then_inc(cleared, 16)
            for u in range(2):
                load_expert(sp, u, u)
            sp.dma_start(b2[:], I["L0_ffn_b2"].partition_broadcast(P)).then_inc(b2_loaded, 16)
            sp.wait_ge(placed, 1)
            sp.wait_ge(scattered, 16 * TILES)
            sp.dma_start(x_tile[:], slots_x[0:P, :]).then_inc(x_loaded, 16)
            g = one_register(sp, "l0f_sp_g")
            with sp.Fori(0, E) as e:
                with tiles_of_expert(sp, tile_counts, e, g, MAX_TILES) as at:
                    sp.wait_ge(x_turned, at)
                    sp.dma_start(x_tile[:], slots_x[bass.ds(at * P, P), :]).then_inc(x_loaded, 16)

        @block.gpsimd
        def _(pool):
            pool.sem_inc(y_free, 1)
            pool.memset(zeros[:], 0.0).then_inc(zeroed, 1)
            routing_constants(pool, constants, order[:], restart[:], thresholds[:], ascending=False)
            pool.wait_ge(placed, 1)
            pool.wait_ge(turn.staged, TILES)
            pool.wait_ge(cleared, 16 * CLEARS)
            for t in range(TILES):
                pool.indirect_dma_start(slots_x, bass.IndirectOffsetOnAxis(index[:, t:t + 1], 0), chip.xn[:, t, :], None
                                        ).then_inc(scattered, 16)
            g = one_register(pool, "l0f_pool_g")
            with pool.Fori(0, E) as e:
                with tiles_of_expert(pool, tile_counts, e, g, MAX_TILES) as at:
                    pool.wait_ge(y_kept, at + 1)
                    pool.dma_start(slots_y[bass.ds(at * P - P, P), :], y_tile[:]).then_inc(y_stored, 16)
                    pool.wait_ge(y_stored, at * 16)
                    pool.sem_inc(y_free, 1)
            for t in range(TILES):
                pool.indirect_dma_start(fetched[:, t, :], None, slots_y, bass.IndirectOffsetOnAxis(index[:, t:t + 1], 0)
                                        ).then_inc(gathered[t // 4], 16)

        @block.tensor
        def _(pe):
            pe.wait_ge(b_loaded, 16)
            pe.transpose(p_y[:, 0:E * FC], b1_rows[:], chip.ident[0:E * FC, 0:E * FC]).then_inc(b1_turned, 1)
            turn_pe(pe, chip, turn, p_hidden)
            pe.wait_ge(loaded, 16)
            for t in range(TILES):
                pe.wait_ge(turn.turned_read, t + 1)
                for c in range(DC):
                    ins = pe.matmul(p_route[:, t * E:(t + 1) * E], chip.xt[:, c, t * P:(t + 1) * P], wr[:, c, :],
                                    start=c == 0, stop=c == DC - 1)
            ins.then_inc(routed, 1)
            pe.wait_ge(chose, 1)
            rank_pe(pe, chip, chosen[:], p_route[:, 128:256].rearrange("p (e t) -> p e t", e=E),
                    p_route[:, 256:384].rearrange("p (e t) -> p e t", e=E)).then_inc(ranked, 1)
            pe.wait_ge(placed, 1)
            pe.sem_inc(h_done, FC)
            pe.sem_inc(y_done, 1)

            def turn_rows(loads):
                pe.wait_ge(x_loaded, loads)
                for c in range(DC):
                    ins = pe.transpose(p_xt[:, c * P:(c + 1) * P], x_tile[:, c * P:(c + 1) * P], chip.ident[:])
                ins.then_inc(x_turned, 1)

            turn_rows(16)
            g = one_register(pe, "l0f_pe_g")
            with pe.Fori(0, E // 2) as i:
                for u in range(2):
                    pe.wait_ge(w_loaded[u], i * 32 + 32)
                    pe.sem_inc(passed, 1)
                    with tiles_of_expert(pe, tile_counts, i * 2 + u, g, MAX_TILES) as at:
                        pe.wait_ge(x_kept, at)
                        for f in range(FC):
                            for c in range(DC):
                                ins = pe.matmul(p_hidden[:, f // CB, (f % CB) * P:(f % CB + 1) * P], w1[:, u, c, f * P:(f + 1) * P], xt_tile[:, c * P:(c + 1) * P],
                                                start=c == 0, stop=c == DC - 1)
                            ins.then_inc(h_done, 1)
                        turn_rows(at * 16 + 16)
                        pe.wait_ge(y_kept, at)
                        for f in range(FC):
                            pe.wait_ge(h_kept, at * FC + (f + 1))
                            ins = pe.matmul(p_y[:, 0:D], hidden[:, f, :], w2[:, u, f, :], start=f == 0, stop=f == FC - 1)
                        ins.then_inc(y_done, 1)

        @block.scalar
        def _(act):
            turn_act(act, chip, turn, p_hidden)
            act.wait_ge(route_steps, 2)
            act.activation(exps[:], logits[:], ACT.Exp).then_inc(exped, 1)
            act.wait_ge(placed, 1)
            act.wait_ge(b1_kept, 1)
            act.sem_inc(h_kept, FC)
            g = one_register(act, "l0f_act_g")

            def run_expert(e, u, reload):
                with tiles_of_expert(act, tile_counts, e, g, MAX_TILES) as at:
                    act.wait_ge(y_done, at)
                    for f in range(FC):
                        act.wait_ge(h_done, at * FC + (f // CB + 1) * CB)
                        act.activation(hidden[:, f, :], p_hidden[:, f // CB, (f % CB) * P:(f % CB + 1) * P], ACT.Gelu,
                                       bias=column(b1, e * FC + f)).then_inc(h_kept, 1)
                if reload:
                    done = act.snap(g, min_val=1, max_val=MAX_TILES + 1)
                    act.wait_ge(y_done, done)
                    load_expert(act, e + 2, u)

            with act.Fori(0, E // 2 - 1) as i:
                for u in range(2):
                    run_expert(i * 2 + u, u, True)
            for u in range(2):
                run_expert(E - 2 + u, u, False)

        @block.vector
        def _(dve):
            row_statistics(dve, chip, norm_steps, 0, chip.x)
            normalize_dve(dve, chip, turn, chip.x)
            dve.wait_ge(b1_turned, 1)
            dve.tensor_copy(b1[:], p_y[:, 0:E * FC]).then_inc(b1_kept, 1)
            dve.wait_ge(routed, 1)
            step = Steps(dve, route_steps)
            p_logits = p_route[:, 0:TILES * E].rearrange("p (t e) -> p t e", e=E)
            step(dve.tensor_reduce(best[:], p_logits, AX.X, ALU.max))
            step(dve.tensor_tensor(logits[:], p_logits, spread(best[:], E), ALU.subtract))
            dve.wait_ge(exped, 1)
            step(dve.tensor_reduce(weight[:], exps[:], AX.X, ALU.add))
            step(dve.reciprocal(weight[:], weight[:]))
            step(dve.tensor_scalar(weight[:], weight[:], chip.gates[:, 4:5], None, ALU.mult))
            dve.wait_ge(constants, 3)
            step(dve.tensor_scalar(restart[:], restart[:], 0.0, None, ALU.is_gt))
            choose(dve, step, exps[:], chosen[:], order[:], place[:], best[:], 0)
            dve.sem_inc(chose, 1)
            dve.wait_ge(ranked, 1)
            within, total = (p_route[:, a:a + E * TILES].rearrange("p (e t) -> p e t", e=E) for a in (128, 256))
            ranks_dve(dve, step, rank[:], upto[:], within, total, restart[:])
            expert_bases(dve, step, chip.ones, rank[:], upto[:], compare[:], thresholds[:], tiles[:], ends[:], tile_counts[:])
            slots_dve(dve, step, rank[:], chosen[:], product[:], place[:], index[:])
            dve.sem_inc(placed, 1)
            dve.wait_ge(b2_loaded, 16)
            dve.sem_inc(y_kept, 1)

            def keep_turned(turnings):
                dve.wait_ge(x_turned, turnings)
                dve.tensor_copy(xt_tile[:], p_xt[:, 0:D]).then_inc(x_kept, 1)

            keep_turned(1)
            g = one_register(dve, "l0f_dve_g")
            with dve.Fori(0, E) as e:
                with tiles_of_expert(dve, tile_counts, e, g, MAX_TILES) as at:
                    keep_turned(at + 1)
                    dve.wait_ge(y_done, at + 1)
                    dve.wait_ge(y_free, at)
                    dve.tensor_tensor(y_tile[:], p_y[:, 0:D], tile_of(b2, e), ALU.add).then_inc(y_kept, 1)
            for q in range(TILES // 4):
                dve.wait_ge(gathered[q], 64)
                for t in range(4 * q, 4 * q + 4):
                    dve.scalar_tensor_tensor(chip.x[:, t, :], fetched[:, t, :], weight[:, t:t + 1], chip.x[:, t, :],
                                             ALU.mult, ALU.add).then_inc(added, 1)



def l1_ffn(nc, chip, I):
    E, F, K = 8, 512, 2
    FC = F // P
    MAX_TILES = K * TILES + E - 1
    SLOT_TILES = MAX_TILES + 1
    slots_x = nc.dram_tensor("l1f_slots_x", [SLOT_TILES * P, D], F32, kind="Internal").ap()
    slots_y = nc.dram_tensor("l1f_slots_y", [SLOT_TILES * P, D], F32, kind="Internal").ap()
    with ExitStack() as stack:
        sb, psum, sem = scope(nc, stack, "l1f")
        wg, wf = sb("wg", [P, DC, E]), sb("wf", [P, DC, D])
        w1, w3, w2 = sb("w1", [P, 2, DC, F]), sb("w3", [P, 2, DC, F]), sb("w2", [P, 2, FC, D])
        b13_rows, b13 = sb("b13_rows", [2 * E * FC, P]), sb("b13", [P, 2 * E * FC])
        b2, bg, bf = sb("b2", [P, E, D]), sb("bg", [P, E]), sb("bf", [1, D])
        zeros = sb("zeros", [P, 2048])
        logits, exps, chosen, product = (sb(n, [P, TILES, E]) for n in ("logits", "exps", "chosen", "product"))
        picked = [sb(f"picked{k}", [P, TILES, E]) for k in range(K)]
        order = sb("order", [P, TILES, E])
        restart, thresholds, rank, upto, compare = (sb(n, [P, E, TILES]) for n in ("restart", "thresholds", "rank", "upto", "compare"))
        best, total, place = (sb(n, [P, TILES]) for n in ("best", "total", "place"))
        weight = [sb(f"weight{k}", [P, TILES]) for k in range(K)]
        tiles, ends = sb("tiles", [P, E]), sb("ends", [P, E])
        tile_counts = sb("tile_counts", [P, E], I32)
        index = [sb(f"index{k}", [P, TILES], I32) for k in range(K)]
        x_tile, xt_tile = sb("x_tile", [P, D]), sb("xt_tile", [P, D])
        h3, h13, hidden, y_tile = sb("h3", [P, FC, P]), sb("h13", [P, FC, P]), sb("hidden", [P, FC, P]), sb("y_tile", [P, D])
        fetched = [sb(f"fetched{k}", [P, TILES, D]) for k in range(K)]
        mixed, mixed_t = sb("mixed", [P, 4, D]), sb("mixed_t", [P, 4, D])
        p_route = psum("p_route", [P, 512])
        p_xt = psum("p_xt", [P, 512])
        p_h = psum("p_h", [P, 4, 512])
        p_y = psum("p_y", [P, 512])
        turn = TurnSemaphores(sem, "t")
        (loaded, b_loaded, b2_loaded, zeroed, cleared, constants, norm_steps, b_turned, b_kept, routed, exped, chose, ranked,
         route_steps, placed, scattered, x_loaded, x_turned, x_kept, h_done, h3_kept, h13_kept, h_kept, y_done, y_kept,
         y_stored, y_free, passed, mix_steps, mixed_turned, mixed_kept, out_done, added) = (sem(n) for n in (
            "loaded", "b_loaded", "b2_loaded", "zeroed", "cleared", "constants", "norm_steps", "b_turned", "b_kept", "routed", "exped",
            "chose", "ranked", "route_steps", "placed", "scattered", "x_loaded", "x_turned", "x_kept", "h_done",
            "h3_kept", "h13_kept", "h_kept", "y_done", "y_kept", "y_stored", "y_free", "passed", "mix_steps", "mixed_turned",
            "mixed_kept", "out_done", "added"))
        w_loaded = [sem("w_loaded0"), sem("w_loaded1")]
        gathered = [sem(f"gathered{q}") for q in range(TILES // 4)]
        block = stack.enter_context(nc.Block())
        CLEARS = 2 * -(-SLOT_TILES // 8)

        def add_output(dve, t):
            dve.wait_ge(out_done, t + 1)
            dve.scalar_tensor_tensor(chip.x[:, t, :], p_h[:, 2 + t % 2, 0:D], chip.gates[:, 5:6], chip.x[:, t, :],
                                     ALU.mult, ALU.add).then_inc(added, 1)

        def load_expert(engine, e, u):
            engine.dma_start(w1[:, u, :, :], expert(I["L1_ffn_W1"], e).rearrange("(c p) f -> p c f", p=P)).then_inc(w_loaded[u], 16)
            engine.dma_start(w3[:, u, :, :], expert(I["L1_ffn_W3"], e).rearrange("(c p) f -> p c f", p=P)).then_inc(w_loaded[u], 16)
            engine.dma_start(w2[:, u, :, :], expert(I["L1_ffn_W2"], e).rearrange("(c p) d -> p c d", p=P)).then_inc(w_loaded[u], 16)

        @block.sync
        def _(sp):
            sp.dma_start(wg[:], I["L1_ffn_Wg"].rearrange("(c p) e -> p c e", p=P)).then_inc(loaded, 16)
            sp.dma_start(bg[:], I["L1_ffn_bg"].partition_broadcast(P)).then_inc(loaded, 16)
            for n, b in enumerate(("L1_ffn_b1", "L1_ffn_b3")):
                sp.dma_start(b13_rows[n * E * FC:(n + 1) * E * FC, :], I[b].rearrange("e (c p) -> (e c) p", p=P)).then_inc(b_loaded, 16)
            sp.wait_ge(zeroed, 1)
            for slots in (slots_x, slots_y):
                for t in range(0, SLOT_TILES, 8):
                    n = min(8, SLOT_TILES - t)
                    sp.dma_start(slots[t * P:(t + n) * P, :].rearrange("(p n) d -> p (n d)", p=P), zeros[:, 0:n * D]).then_inc(cleared, 16)
            for u in range(2):
                load_expert(sp, u, u)
            sp.dma_start(b2[:], I["L1_ffn_b2"].partition_broadcast(P)).then_inc(b2_loaded, 16)
            sp.dma_start(bf[:], I["L1_ffn_bf"].rearrange("(a d) -> a d", a=1)).then_inc(b2_loaded, 16)
            sp.dma_start(wf[:], I["L1_ffn_Wf"].rearrange("(c p) d -> p c d", p=P)).then_inc(b2_loaded, 16)
            sp.wait_ge(placed, 1)
            sp.wait_ge(scattered, 16 * K * TILES)
            sp.dma_start(x_tile[:], slots_x[0:P, :]).then_inc(x_loaded, 16)
            g = one_register(sp, "l1f_sp_g")
            with sp.Fori(0, E) as e:
                with tiles_of_expert(sp, tile_counts, e, g, MAX_TILES) as at:
                    sp.wait_ge(x_turned, at)
                    sp.dma_start(x_tile[:], slots_x[bass.ds(at * P, P), :]).then_inc(x_loaded, 16)

        @block.gpsimd
        def _(pool):
            pool.sem_inc(y_free, 1)
            pool.memset(zeros[:], 0.0).then_inc(zeroed, 1)
            routing_constants(pool, constants, order[:], restart[:], thresholds[:], ascending=True)
            pool.wait_ge(placed, 1)
            pool.wait_ge(turn.staged, TILES)
            pool.wait_ge(cleared, 16 * CLEARS)
            for t in range(TILES):
                for k in range(K):
                    pool.indirect_dma_start(slots_x, bass.IndirectOffsetOnAxis(index[k][:, t:t + 1], 0), chip.xn[:, t, :], None
                                            ).then_inc(scattered, 16)
            g = one_register(pool, "l1f_pool_g")
            with pool.Fori(0, E) as e:
                with tiles_of_expert(pool, tile_counts, e, g, MAX_TILES) as at:
                    pool.wait_ge(y_kept, at + 1)
                    pool.dma_start(slots_y[bass.ds(at * P - P, P), :], y_tile[:]).then_inc(y_stored, 16)
                    pool.wait_ge(y_stored, at * 16)
                    pool.sem_inc(y_free, 1)
            for t in range(TILES):
                for k in range(K):
                    pool.indirect_dma_start(fetched[k][:, t, :], None, slots_y, bass.IndirectOffsetOnAxis(index[k][:, t:t + 1], 0)
                                            ).then_inc(gathered[t // 4], 16)

        @block.tensor
        def _(pe):
            pe.wait_ge(b_loaded, 32)
            pe.transpose(p_y[:, 0:2 * E * FC], b13_rows[:], chip.ident[0:2 * E * FC, 0:2 * E * FC]).then_inc(b_turned, 1)
            turn_pe(pe, chip, turn, p_h)
            pe.wait_ge(loaded, 32)
            for t in range(TILES):
                pe.wait_ge(turn.turned_read, t + 1)
                for c in range(DC):
                    ins = pe.matmul(p_route[:, t * E:(t + 1) * E], chip.xt[:, c, t * P:(t + 1) * P], wg[:, c, :],
                                    start=c == 0, stop=c == DC - 1)
            ins.then_inc(routed, 1)
            pe.wait_ge(chose, 1)
            rank_pe(pe, chip, chosen[:], p_route[:, 128:256].rearrange("p (e t) -> p e t", e=E),
                    p_route[:, 256:384].rearrange("p (e t) -> p e t", e=E)).then_inc(ranked, 1)
            pe.wait_ge(placed, 1)
            pe.sem_inc(h_done, 4)
            pe.sem_inc(y_done, 1)

            def turn_rows(loads):
                pe.wait_ge(x_loaded, loads)
                for c in range(DC):
                    ins = pe.transpose(p_xt[:, c * P:(c + 1) * P], x_tile[:, c * P:(c + 1) * P], chip.ident[:])
                ins.then_inc(x_turned, 1)

            turn_rows(16)
            g = one_register(pe, "l1f_pe_g")
            with pe.Fori(0, E // 2) as i:
                for u in range(2):
                    pe.wait_ge(w_loaded[u], i * 48 + 48)
                    pe.sem_inc(passed, 1)
                    with tiles_of_expert(pe, tile_counts, i * 2 + u, g, MAX_TILES) as at:
                        pe.wait_ge(x_kept, at)
                        pe.wait_ge(h3_kept, at * 4)
                        pe.wait_ge(h13_kept, at * 4)
                        for half in range(2):
                            for bank, w in ((2 + half, w3), (half, w1)):
                                for f in (2 * half, 2 * half + 1):
                                    for c in range(DC):
                                        ins = pe.matmul(p_h[:, bank, (f % 2) * P:(f % 2 + 1) * P], w[:, u, c, f * P:(f + 1) * P],
                                                        xt_tile[:, c * P:(c + 1) * P], start=c == 0, stop=c == DC - 1)
                                ins.then_inc(h_done, 1)
                        turn_rows(at * 16 + 16)
                        pe.wait_ge(y_kept, at)
                        for f in range(FC):
                            pe.wait_ge(h_kept, at * 2 + (f // 2 + 1))
                            ins = pe.matmul(p_y[:, 0:D], hidden[:, f, :], w2[:, u, f, :], start=f == 0, stop=f == FC - 1)
                        ins.then_inc(y_done, 1)
            pe.wait_ge(b2_loaded, 48)
            for t in range(TILES):
                s = t % 4
                if t >= 2:
                    pe.wait_ge(mixed_kept, t - 1)
                pe.wait_ge(mix_steps, 2 * t + 2)
                for c in range(DC):
                    ins = pe.transpose(p_h[:, t % 2, c * P:(c + 1) * P], mixed[:, s, c * P:(c + 1) * P], chip.ident[:])
                ins.then_inc(mixed_turned, 1)
                pe.wait_ge(mixed_kept, t + 1)
                if t >= 2:
                    pe.wait_ge(added, t - 1)
                for c in range(DC):
                    pe.matmul(p_h[:, 2 + t % 2, 0:D], mixed_t[:, s, c * P:(c + 1) * P], wf[:, c, :], start=c == 0, stop=False)
                pe.matmul(p_h[:, 2 + t % 2, 0:D], chip.ones[0:1, :], bf[:], start=False, stop=True).then_inc(out_done, 1)

        @block.scalar
        def _(act):
            turn_act(act, chip, turn, p_h)
            act.wait_ge(route_steps, 3)
            act.activation(exps[:], logits[:], ACT.Exp).then_inc(exped, 1)
            act.wait_ge(placed, 1)
            act.wait_ge(b_kept, 1)
            act.sem_inc(h_kept, 2)
            g = one_register(act, "l1f_act_g")

            def run_expert(e, u, reload):
                with tiles_of_expert(act, tile_counts, e, g, MAX_TILES) as at:
                    act.wait_ge(y_done, at)
                    for half in range(2):
                        act.wait_ge(h13_kept, at * 4 + (2 * half + 2))
                        act.activation(hidden[:, 2 * half:2 * half + 2, :], h13[:, 2 * half:2 * half + 2, :], ACT.Silu).then_inc(h_kept, 1)
                if reload:
                    done = act.snap(g, min_val=1, max_val=MAX_TILES + 1)
                    act.wait_ge(y_done, done)
                    load_expert(act, e + 2, u)

            with act.Fori(0, E // 2 - 1) as i:
                for u in range(2):
                    run_expert(i * 2 + u, u, True)
            for u in range(2):
                run_expert(E - 2 + u, u, False)
            for t in range(TILES):
                act.wait_ge(mixed_turned, t + 1)
                if t >= 4:
                    act.wait_ge(out_done, t - 3)
                act.copy(mixed_t[:, t % 4, :], p_h[:, t % 2, 0:D]).then_inc(mixed_kept, 1)

        @block.vector
        def _(dve):
            row_statistics(dve, chip, norm_steps, 0, chip.x)
            normalize_dve(dve, chip, turn, chip.x)
            dve.wait_ge(b_turned, 1)
            dve.tensor_copy(b13[:], p_y[:, 0:2 * E * FC]).then_inc(b_kept, 1)
            dve.wait_ge(routed, 1)
            dve.wait_ge(loaded, 32)
            step = Steps(dve, route_steps)
            step(dve.tensor_tensor(logits[:], p_route[:, 0:TILES * E].rearrange("p (t e) -> p t e", e=E),
                                   bg[:].unsqueeze(1).to_broadcast([P, TILES, E]), ALU.add))
            step(dve.tensor_reduce(best[:], logits[:], AX.X, ALU.max))
            step(dve.tensor_tensor(logits[:], logits[:], spread(best[:], E), ALU.subtract))
            dve.wait_ge(exped, 1)
            step(dve.tensor_reduce(total[:], exps[:], AX.X, ALU.add))
            step(dve.reciprocal(total[:], total[:]))
            dve.wait_ge(constants, 3)
            step(dve.tensor_scalar(restart[:], restart[:], 0.0, None, ALU.is_gt))
            for k in range(K):
                choose(dve, step, exps[:], picked[k][:], order[:], weight[k][:], best[:], 2.0)
                step(dve.tensor_tensor(weight[k][:], weight[k][:], total[:], ALU.mult))
            step(dve.tensor_tensor(chosen[:], picked[0][:], picked[1][:], ALU.add))
            dve.sem_inc(chose, 1)
            dve.wait_ge(ranked, 1)
            within, tile_total = (p_route[:, a:a + E * TILES].rearrange("p (e t) -> p e t", e=E) for a in (128, 256))
            ranks_dve(dve, step, rank[:], upto[:], within, tile_total, restart[:])
            expert_bases(dve, step, chip.ones, rank[:], upto[:], compare[:], thresholds[:], tiles[:], ends[:], tile_counts[:])
            for k in range(K):
                slots_dve(dve, step, rank[:], picked[k][:], product[:], place[:], index[k][:])
            dve.sem_inc(placed, 1)
            dve.wait_ge(b2_loaded, 48)
            dve.sem_inc(y_kept, 1)
            dve.sem_inc(h3_kept, 4)
            dve.sem_inc(h13_kept, 4)

            def keep_turned(turnings):
                dve.wait_ge(x_turned, turnings)
                dve.tensor_copy(xt_tile[:], p_xt[:, 0:D]).then_inc(x_kept, 1)

            keep_turned(1)
            g = one_register(dve, "l1f_dve_g")
            with dve.Fori(0, E) as e:
                with tiles_of_expert(dve, tile_counts, e, g, MAX_TILES) as at:
                    dve.wait_ge(h_kept, at * 2)
                    for half in range(2):
                        dve.wait_ge(h_done, at * 4 + (2 * half + 1))
                        for f in (2 * half, 2 * half + 1):
                            dve.tensor_scalar(h3[:, f, :], p_h[:, 2 + half, (f % 2) * P:(f % 2 + 1) * P],
                                              column(b13, e * FC + (E * FC + f)), None, ALU.add).then_inc(h3_kept, 1)
                        dve.wait_ge(h_done, at * 4 + (2 * half + 2))
                        for f in (2 * half, 2 * half + 1):
                            dve.wait_ge(h3_kept, at * 4 + (f + 1))
                            dve.scalar_tensor_tensor(h13[:, f, :], p_h[:, half, (f % 2) * P:(f % 2 + 1) * P],
                                                     column(b13, e * FC + f), h3[:, f, :], ALU.add, ALU.mult).then_inc(h13_kept, 1)
                    keep_turned(at + 1)
                    dve.wait_ge(y_done, at + 1)
                    dve.wait_ge(y_free, at)
                    dve.tensor_tensor(y_tile[:], p_y[:, 0:D], tile_of(b2, e), ALU.add).then_inc(y_kept, 1)
            for t in range(TILES):
                if t % 4 == 0:
                    dve.wait_ge(gathered[t // 4], 4 * K * 16)
                if t >= 4:
                    dve.wait_ge(mixed_turned, t - 3)
                step = Steps(dve, mix_steps, 2 * t)
                step(dve.tensor_scalar(mixed[:, t % 4, :], fetched[0][:, t, :], weight[0][:, t:t + 1], None, ALU.mult))
                step(dve.scalar_tensor_tensor(mixed[:, t % 4, :], fetched[1][:, t, :], weight[1][:, t:t + 1], mixed[:, t % 4, :],
                                              ALU.mult, ALU.add))
                if t >= 1:
                    add_output(dve, t - 1)
            add_output(dve, TILES - 1)



def l2_attention(nc, chip, I):
    with ExitStack() as stack:
        sb, psum, sem = scope(nc, stack, "l2a")
        w = sb("w", [P, 4, DC, D])
        w_hc = sb("w_hc", [P, BATCH, DC, D])
        wsim_rows, wsim = sb("wsim_rows", [6, P]), sb("wsim", [P, 6])
        b_sim, b_qv = sb("b_sim", [1, 1]), sb("b_qv", [1, D])
        keys, column_term = sb("keys", [P, DC, BATCH * CTX]), sb("column_term", [1, BATCH * CTX])
        xt, probs, probs_t = sb("xt", [P, 2, DC, P]), sb("probs", [P, 2, CTX]), sb("probs_t", [P, 2, 2, P])
        hq_t, xhq_t = sb("hq_t", [P, DC, TOKENS]), sb("xhq_t", [P, DC, TOKENS])
        neg_max, attended = sb("neg_max", [P, TILES]), sb("attended", [P, TILES])
        total, factor = sb("total", [P, 2]), sb("factor", [P, 2])
        tile_min, batch_min, shift, sums, inv_sums = sb("tile_min", [P, 2]), sb("batch_min", [1, 2]), sb("shift", [P, 2]), sb("sums", [P, 2]), sb("inv_sums", [P, 2])
        hc = sb("hc", [P, BATCH, DC])
        pa, pb = psum("pa", [P, 2, 512]), psum("pb", [P, 2, 512])
        pc, pd = psum("pc", [P, 2, 512]), psum("pd", [P, 2, 512])
        (loaded, w_loaded, wsim_turned, wsim_kept, term_done, keys_kept, norm_steps, staged, kept, turned, xt_kept, scored, maxed,
         exped, scaled, probs_turned, probs_kept, hq_done, hq_kept, xhq_kept, min_turned, min_steps, shift_done, exp_done, hc_done,
         hc_steps, out_done, added) = (sem(n) for n in (
            "loaded", "w_loaded", "wsim_turned", "wsim_kept", "term_done", "keys_kept", "norm_steps", "staged", "kept", "turned",
            "xt_kept", "scored", "maxed", "exped", "scaled", "probs_turned", "probs_kept", "hq_done", "hq_kept", "xhq_kept",
            "min_turned", "min_steps", "shift_done", "exp_done", "hc_done", "hc_steps", "out_done", "added"))
        block = stack.enter_context(nc.Block())

        @block.sync
        def _(sp):
            sp.dma_start(wsim_rows[:], I["L2_xattn_w_sim"].rearrange("(c p) -> c p", p=P)).then_inc(loaded, 16)
            sp.dma_start(b_sim[:], I["L2_xattn_b_sim"].rearrange("(a d) -> a d", a=1)).then_inc(loaded, 16)
            sp.dma_start(w[:], I["L2_xattn_W_qv"].rearrange("(k c p) d -> p k c d", k=4, p=P)).then_inc(w_loaded, 16)
            sp.dma_start(b_qv[:], I["L2_xattn_b_qv"].rearrange("(a d) -> a d", a=1)).then_inc(w_loaded, 16)

        @block.tensor
        def _(pe):
            pe.wait_ge(loaded, 32)
            pe.transpose(pa[:, 0, 0:6], wsim_rows[:], chip.ident[0:6, 0:6]).then_inc(wsim_turned, 1)
            pe.wait_ge(wsim_kept, 1)
            for c in range(DC):
                ins = pe.matmul(pb[0:1, 0, 0:BATCH * CTX], wsim[:, 2 + c:3 + c], chip.ctxt[:, c, :], start=c == 0, stop=c == DC - 1)
            ins.then_inc(term_done, 1)
            pe.wait_ge(keys_kept, DC + 1)
            with pe.Fori(0, BATCH_TILES) as i:
                for u in range(BATCH):
                    pe.wait_ge(staged, i * 2 + (u + 1))
                    for c in range(DC):
                        ins = pe.transpose(pa[:, u, c * P:(c + 1) * P], chip.stage[:, u, c * P:(c + 1) * P], chip.ident[:])
                    ins.then_inc(turned, 1)
                for u in range(BATCH):
                    pe.wait_ge(xt_kept, i * 2 + (u + 1))
                    for c in range(DC):
                        pe.matmul(pb[:, u, 0:CTX], xt[:, u, c, :], keys[:, c, u * CTX:(u + 1) * CTX], start=c == 0, stop=False)
                    pe.matmul(pb[:, u, 0:CTX], chip.ones[0:1, :], column_term[:, u * CTX:(u + 1) * CTX],
                              start=False, stop=True).then_inc(scored, 1)
                for u in range(BATCH):
                    pe.wait_ge(scaled, i * 4 + (2 * u + 2))
                    for c, (row, rows) in enumerate(CHUNKS):
                        ins = pe.transpose(pc[0:rows, u, c * P:(c + 1) * P], probs[:, u, row:row + rows], chip.ident[:])
                    ins.then_inc(probs_turned, 1)
                for u in range(BATCH):
                    pe.wait_ge(probs_kept, i * 4 + (2 * u + 2))
                    for d in range(DC):
                        for c, (row, rows) in enumerate(CHUNKS):
                            ins = pe.matmul(pd[:, u, d * P:(d + 1) * P], chip.ctx[0:rows, u, c, d * P:(d + 1) * P],
                                            probs_t[0:rows, u, c, :], start=c == 0, stop=c == 1)
                    ins.then_inc(hq_done, 1)
            pe.wait_ge(min_steps, 1)
            for b in range(BATCH):
                ins = pe.transpose(pa[0:1, 0, b * P:(b + 1) * P], tile_min[:, b:b + 1], chip.ident[:])
            ins.then_inc(min_turned, 1)
            pe.wait_ge(min_steps, 2)
            pe.matmul(pb[:, 0, 0:BATCH], chip.ones[0:1, :], batch_min[:], start=True, stop=True).then_inc(shift_done, 1)
            pe.wait_ge(exp_done, BATCH)
            pe.matmul(pc[:, 0, 0:BATCH], chip.ones[:], sums[:], start=True, stop=True)
            pe.wait_ge(kept, 2 + TILES)
            for b in range(BATCH):
                for c in range(DC):
                    for t in range(BATCH_TILES):
                        at = b * BATCH_TILES + t
                        ins = pe.matmul(pc[:, 1, b * DC + c:b * DC + c + 1], chip.xn[:, at, c * P:(c + 1) * P], attended[:, at:at + 1],
                                        start=t == 0, stop=t == BATCH_TILES - 1)
            ins.then_inc(hc_done, 1)
            pe.wait_ge(hc_steps, 2 + BATCH * DC)
            pe.wait_ge(w_loaded, 32)
            pe.wait_ge(xhq_kept, 2 * TILES + 1)
            for t in range(TILES):
                tokens = slice(t * P, (t + 1) * P)
                if t >= 2:
                    pe.wait_ge(added, t - 1)
                for c in range(DC):
                    pe.matmul(pd[:, t % 2, 0:D], chip.xt[:, c, tokens], w_hc[:, t // BATCH_TILES, c, :], start=c == 0, stop=False)
                    pe.matmul(pd[:, t % 2, 0:D], hq_t[:, c, tokens], w[:, 1, c, :], start=False, stop=False)
                    pe.matmul(pd[:, t % 2, 0:D], xhq_t[:, c, tokens], w[:, 2, c, :], start=False, stop=False)
                pe.matmul(pd[:, t % 2, 0:D], chip.ones[0:1, :], b_qv[:], start=False, stop=True).then_inc(out_done, 1)

        @block.scalar
        def _(act):
            with act.Fori(0, BATCH_TILES) as i:
                for u in range(BATCH):
                    act.wait_ge(turned, i * 2 + (u + 1))
                    act.wait_ge(xhq_kept, i * 4 + 1)
                    act.copy(xt[:, u, :, :], pa[:, u, 0:D].rearrange("p (c t) -> p c t", c=DC)).then_inc(xt_kept, 1)
                for u in range(BATCH):
                    act.wait_ge(maxed, i * 2 + (u + 1))
                    act.activation(probs[:, u, :], pb[:, u, 0:CTX], ACT.Exp, bias=column(neg_max, i + u * BATCH_TILES),
                                   accum_out=total[:, u:u + 1]).then_inc(exped, 1)
                for u in range(BATCH):
                    act.wait_ge(hq_done, i * 2 + (u + 1))
                    act.copy(hq_t[:, :, bass.ds((i + u * BATCH_TILES) * P, P)],
                             pd[:, u, 0:D].rearrange("p (c t) -> p c t", c=DC)).then_inc(hq_kept, 1)
            act.wait_ge(min_steps, 3)
            for b in range(BATCH):
                rows = slice(b * BATCH_TILES, (b + 1) * BATCH_TILES)
                act.activation(attended[:, rows], neg_max[:, rows], ACT.Exp, bias=shift[:, b:b + 1], scale=-1.0,
                               accum_out=sums[:, b:b + 1]).then_inc(exp_done, 1)

        @block.gpsimd
        def _(pool):
            pool.sem_inc(kept, 2)
            pool.sem_inc(xhq_kept, 1)
            with pool.Fori(0, BATCH_TILES) as i:
                for u in range(BATCH):
                    pool.wait_ge(staged, i * 2 + (u + 1))
                    pool.tensor_copy(tile_of(chip.xn, i + u * BATCH_TILES), chip.stage[:, u, :]).then_inc(kept, 1)
                for u in range(BATCH):
                    tokens = bass.ds((i + u * BATCH_TILES) * P, P)
                    pool.wait_ge(xt_kept, i * 2 + (u + 1))
                    pool.tensor_copy(chip.xt[:, :, tokens], xt[:, u, :, :]).then_inc(xhq_kept, 1)
                    pool.wait_ge(hq_kept, i * 2 + (u + 1))
                    pool.tensor_tensor(xhq_t[:, :, tokens], hq_t[:, :, tokens], xt[:, u, :, :], ALU.mult).then_inc(xhq_kept, 1)

        @block.vector
        def _(dve):
            dve.wait_ge(wsim_turned, 1)
            dve.tensor_copy(wsim[:], pa[:, 0, 0:6]).then_inc(wsim_kept, 1)
            dve.wait_ge(wsim_kept, 1)
            for c in range(DC):
                dve.tensor_scalar(keys[:, c, :], chip.ctxt[:, c, :], wsim[:, 4 + c:5 + c], wsim[:, c:c + 1],
                                  ALU.mult, ALU.add).then_inc(keys_kept, 1)
            row_statistics(dve, chip, norm_steps, 0, chip.x)
            dve.wait_ge(term_done, 1)
            dve.tensor_scalar(column_term[:], pb[0:1, 0, 0:BATCH * CTX], b_sim[:], None, ALU.add).then_inc(keys_kept, 1)
            with dve.Fori(0, BATCH_TILES) as i:
                for u in range(BATCH):
                    t = i + u * BATCH_TILES
                    dve.wait_ge(kept, i * 2 + (u + 1))
                    dve.tensor_scalar(chip.stage[:, u, :], tile_of(chip.x, t), column(chip.mean, t),
                                      column(chip.inv_std, t), ALU.subtract, ALU.mult).then_inc(staged, 1)
                for u in range(BATCH):
                    dve.wait_ge(scored, i * 2 + (u + 1))
                    dve.tensor_reduce(column(neg_max, i + u * BATCH_TILES), pb[:, u, 0:CTX], AX.X, ALU.max, negate=True).then_inc(maxed, 1)
                for u in range(BATCH):
                    dve.wait_ge(exped, i * 2 + (u + 1))
                    step = Steps(dve, scaled, i * 4 + 2 * u)
                    step(dve.reciprocal(factor[:, u:u + 1], total[:, u:u + 1]))
                    step(dve.tensor_scalar(probs[:, u, :], probs[:, u, :], factor[:, u:u + 1], None, ALU.mult))
                for u in range(BATCH):
                    dve.wait_ge(probs_turned, i * 2 + (u + 1))
                    for c, (row, rows) in enumerate(CHUNKS):
                        dve.tensor_copy(probs_t[0:rows, u, c, :], pc[0:rows, u, c * P:(c + 1) * P]).then_inc(probs_kept, 1)
            step = Steps(dve, min_steps)
            step(dve.tensor_reduce(tile_min[:], neg_max[:].rearrange("p (b t) -> p b t", b=BATCH), AX.X, ALU.min))
            dve.wait_ge(min_turned, 1)
            step(dve.tensor_reduce(batch_min[:], pa[0:1, 0, 0:BATCH * P].rearrange("p (b t) -> p b t", b=BATCH), AX.X, ALU.min))
            dve.wait_ge(shift_done, 1)
            step(dve.tensor_copy(shift[:], pb[:, 0, 0:BATCH]))
            dve.wait_ge(hc_done, 1)
            step = Steps(dve, hc_steps)
            step(dve.reciprocal(inv_sums[:], pc[:, 0, 0:BATCH]))
            step(dve.tensor_tensor(hc[:], pc[:, 1, 0:BATCH * DC].rearrange("p (b c) -> p b c", b=BATCH), spread(inv_sums[:], DC), ALU.mult))
            dve.wait_ge(w_loaded, 32)
            for b in range(BATCH):
                for c in range(DC):
                    step(dve.scalar_tensor_tensor(w_hc[:, b, c, :], w[:, 3, c, :], hc[:, b, c:c + 1], w[:, 0, c, :], ALU.mult, ALU.add))
            for t in range(TILES):
                dve.wait_ge(out_done, t + 1)
                dve.scalar_tensor_tensor(chip.x[:, t, :], pd[:, t % 2, 0:D], chip.gates[:, 2:3], chip.x[:, t, :],
                                         ALU.mult, ALU.add).then_inc(added, 1)



def l2_ffn(nc, chip, I):
    E, F = 8, 512
    FC = F // P
    BLOCK = 512
    BLOCKS = TOKENS // BLOCK
    with ExitStack() as stack:
        sb, psum, sem = scope(nc, stack, "l2f")
        gate_rows, gate_w = sb("gate_rows", [E, D]), sb("gate_w", [P, DC, E])
        gate_b, rms_w = sb("gate_b", [P, E]), sb("rms_w", [P, E])
        w, w_hi, w_lo = sb("w", [P, 2, 2, DC * F]), sb("w_hi", [P, 2, 2, DC * F], F32R), sb("w_lo", [P, 2, 2, DC * F], F32R)
        x_hi, x_lo = sb("x_hi", [P, DC, TOKENS], F32R), sb("x_lo", [P, DC, TOKENS], F32R)
        b1_rows, b1, b2 = sb("b1_rows", [E * FC, P]), sb("b1", [P, E * FC]), sb("b2", [E, D])
        b1_pair = sb("b1_pair", [P, 2 * FC])
        logits, squares = sb("logits", [P, TILES, E]), sb("squares", [P, TILES, E])
        best, root, weight, other = (sb(n, [P, TILES]) for n in ("best", "root", "weight", "other"))
        hidden = sb("hidden", [P, FC, BLOCK])
        hidden_hi, hidden_lo = sb("hidden_hi", [P, 2, FC, BLOCK], F32R), sb("hidden_lo", [P, 2, FC, BLOCK], F32R)
        y, b2_sum = chip.xn, sb("b2_sum", [P, D])
        p_h, p_y, p_s = psum("p_h", [P, FC, 512]), psum("p_y", [P, 2, 512]), psum("p_s", [P, 2, 512])
        turn = TurnSemaphores(sem, "t")
        (loaded, gate_turned, gate_kept, norm_steps, routed, squared, exped, route_steps, h_done, h_kept, pair_kept, y_done, y_kept, added) = (
            sem(n) for n in ("loaded", "gate_turned", "gate_kept", "norm_steps", "routed", "squared", "exped", "route_steps",
                             "h_done", "h_kept", "pair_kept", "y_done", "y_kept", "added"))
        w_hi_made, w_lo_made, x_hi_made, x_lo_made, lo_made, passed = (sem(n) for n in ("w_hi_made", "w_lo_made", "x_hi_made", "x_lo_made", "lo_made", "passed"))
        logits_made = sem("logits_made")
        w_loaded = [sem("w_loaded0"), sem("w_loaded1")]
        block = stack.enter_context(nc.Block())

        def load_expert(engine, e, u):
            for k, (name, width) in enumerate((("L2_ffn_w1", F), ("L2_ffn_w2", D))):
                engine.dma_start(w[:, u, k, :].rearrange("p (c n) -> p c n", n=width),
                                 expert(I[name], e).rearrange("(c p) n -> p c n", p=P)).then_inc(w_loaded[u], 16)

        def pairs(engine, run):
            with engine.Fori(0, E // 2 - 1) as i:
                run(i, True)
            run(E // 2 - 1, False)

        @block.sync
        def _(sp):
            sp.dma_start(gate_rows[:], I["L2_ffn_gate_w"]).then_inc(loaded, 16)
            sp.dma_start(b1_rows[:], I["L2_ffn_b1"].rearrange("e (c p) -> (e c) p", p=P)).then_inc(loaded, 16)
            sp.dma_start(b2[:], I["L2_ffn_b2"]).then_inc(loaded, 16)
            sp.dma_start(gate_b[:], I["L2_ffn_gate_b"].partition_broadcast(P)).then_inc(loaded, 16)
            sp.dma_start(rms_w[:], I["L2_ffn_rms_w"].partition_broadcast(P)).then_inc(loaded, 16)
            for u in range(2):
                load_expert(sp, u, u)
            with sp.Fori(1, E // 2) as i:
                for u in range(2):
                    sp.wait_ge(w_lo_made, i * 2 + (u - 1))
                    load_expert(sp, i * 2 + u, u)

        @block.gpsimd
        def _(pool):
            with pool.Fori(0, E // 2) as i:
                for u in range(2):
                    pool.wait_ge(w_loaded[u], i * 32 + 32)
                    pool.wait_ge(y_done, i * (4 * BLOCKS) + (2 * (u + 1) * BLOCKS + 1))
                    pool.sem_inc(passed, 1)
                    pool.tensor_copy(w_hi[:, u, :, :], w[:, u, :, :]).then_inc(w_hi_made, 1)

        @block.tensor
        def _(pe):
            pe.wait_ge(loaded, 80)
            for c in range(DC):
                pe.transpose(p_s[:, 0, c * E:(c + 1) * E], gate_rows[:, c * P:(c + 1) * P], chip.ident[0:E, 0:E])
            pe.transpose(p_s[:, 0, 32:32 + E * FC], b1_rows[:], chip.ident[0:E * FC, 0:E * FC])
            pe.matmul(p_s[:, 0, 128:128 + D], chip.ones[0:E, :], b2[:], start=True, stop=True).then_inc(gate_turned, 1)
            turn_pe(pe, chip, turn, p_h)
            pe.wait_ge(gate_kept, 3)
            pe.sem_inc(y_done, 1 + 4 * BLOCKS)
            for t in range(TILES):
                pe.wait_ge(turn.turned_read, t + 1)
                for c in range(DC):
                    ins = pe.matmul(p_s[:, 1, t * E:(t + 1) * E], chip.xt[:, c, t * P:(t + 1) * P], gate_w[:, c, :],
                                    start=c == 0, stop=c == DC - 1)
            ins.then_inc(routed, 1)
            def run(i, more):
                first = more

                def make_hidden(n):
                    u, b = n // BLOCKS, n % BLOCKS
                    at = i * (2 * BLOCKS) + n
                    if b == 0:
                        pe.wait_ge(w_lo_made, i * 2 + (u + 1))
                    if first:
                        pe.wait_ge(x_lo_made, b + 1)
                    tokens = slice(b * BLOCK, (b + 1) * BLOCK)
                    for f in range(FC):
                        pe.wait_ge(h_kept, at * FC + (f + 1))
                        for c in range(DC):
                            columns = slice(c * F + f * P, c * F + (f + 1) * P)
                            for part, (a, x) in enumerate(((w_hi, x_hi), (w_hi, x_lo), (w_lo, x_hi))):
                                ins = pe.matmul(p_h[:, f, :], a[:, u, 0, columns], x[:, c, tokens],
                                                start=c == 0 and part == 0, stop=c == DC - 1 and part == 2)
                        ins.then_inc(h_done, 1)

                def multiply_out(n):
                    u, b = n // BLOCKS, n % BLOCKS
                    at = i * (2 * BLOCKS) + n
                    pe.wait_ge(lo_made, at * FC + FC + FC)
                    for bank in range(2):
                        pe.wait_ge(y_kept, at * 2 + (bank + 1))
                        for half in range(2):
                            j = 2 * bank + half
                            for f in range(FC):
                                for part, (h, a) in enumerate(((hidden_hi, w_hi), (hidden_hi, w_lo), (hidden_lo, w_hi))):
                                    ins = pe.matmul(p_y[:, bank, half * D:(half + 1) * D], h[:, n % 2, f, j * P:(j + 1) * P],
                                                    a[:, u, 1, f * D:(f + 1) * D], start=f == 0 and part == 0,
                                                    stop=f == FC - 1 and part == 2)
                        ins.then_inc(y_done, 1)

                make_hidden(0)
                for n in range(2 * BLOCKS):
                    if n + 1 < 2 * BLOCKS:
                        make_hidden(n + 1)
                    multiply_out(n)

            pairs(pe, run)

        @block.scalar
        def _(act):
            turn_act(act, chip, turn, p_h)
            act.wait_ge(gate_kept, 3)
            for b in range(BLOCKS):
                tokens = slice(b * BLOCK, (b + 1) * BLOCK)
                act.wait_ge(turn.turned_read, 4 * (b + 1))
                act.copy(x_hi[:, :, tokens], chip.xt[:, :, tokens]).then_inc(x_hi_made, 1)
            act.sem_inc(h_kept, FC)
            with act.Fori(0, E // 2) as i:
                act.wait_ge(h_kept, i * (2 * BLOCKS * FC) + FC)
                act.copy(b1_pair[:], b1[:, bass.ds(i * (2 * FC), 2 * FC)]).then_inc(pair_kept, 1)
                act.wait_ge(pair_kept, i + 1)
                for n in range(2 * BLOCKS):
                    at = i * (2 * BLOCKS) + n
                    act.wait_ge(y_done, i * (4 * BLOCKS) + max(2 * (n - 1), 0) + (1 + 4 * BLOCKS))
                    for f in range(FC):
                        bias = column(b1_pair, (n // BLOCKS) * FC + f)
                        act.wait_ge(lo_made, at * FC + (f + 1))
                        act.wait_ge(h_done, at * FC + (f + 1))
                        act.activation(hidden_hi[:, n % 2, f, :], p_h[:, f, :], ACT.Gelu, bias=bias)
                        act.activation(hidden[:, f, :], p_h[:, f, :], ACT.Gelu, bias=bias).then_inc(h_kept, 1)
            act.wait_ge(logits_made, 1)
            act.activation(logits[:], logits[:], ACT.Exp, scale=2.0).then_inc(exped, 1)

        @block.vector
        def _(dve):
            def split_weights(e, u):
                dve.wait_ge(w_hi_made, e + 1)
                dve.tensor_tensor(w_lo[:, u, :, :], w[:, u, :, :], w_hi[:, u, :, :].bitcast(F32), ALU.subtract).then_inc(w_lo_made, 1)

            row_statistics(dve, chip, norm_steps, 0, chip.x)
            dve.wait_ge(gate_turned, 1)
            dve.tensor_copy(gate_w[:], p_s[:, 0, 0:DC * E].rearrange("p (c e) -> p c e", c=DC)).then_inc(gate_kept, 1)
            dve.tensor_copy(b1[:], p_s[:, 0, 32:32 + E * FC]).then_inc(gate_kept, 1)
            dve.tensor_copy(b2_sum[:], p_s[:, 0, 128:128 + D]).then_inc(gate_kept, 1)
            normalize_dve(dve, chip, turn, chip.x)
            split_weights(0, 0)
            for b in range(BLOCKS):
                tokens = slice(b * BLOCK, (b + 1) * BLOCK)
                dve.wait_ge(x_hi_made, b + 1)
                dve.tensor_tensor(x_lo[:, :, tokens], chip.xt[:, :, tokens], x_hi[:, :, tokens].bitcast(F32), ALU.subtract
                                  ).then_inc(x_lo_made, 1)
            dve.wait_ge(routed, 1)
            step = Steps(dve, route_steps)
            step(dve.tensor_tensor(logits[:], p_s[:, 1, 0:TILES * E].rearrange("p (t e) -> p t e", e=E),
                                   gate_b[:].unsqueeze(1).to_broadcast([P, TILES, E]), ALU.add))
            step(dve.tensor_tensor(squares[:], logits[:], logits[:], ALU.mult))
            step(dve.tensor_reduce(best[:], squares[:], AX.X, ALU.add))
            inverse_root(dve, step, root[:], best[:], 1.0 / E, 1.1920929e-07, (weight[:], other[:]))
            step(dve.tensor_tensor(logits[:], logits[:], spread(root[:], E), ALU.mult))
            step(dve.tensor_tensor(logits[:], logits[:], rms_w[:].unsqueeze(1).to_broadcast([P, TILES, E]), ALU.mult))
            step(dve.tensor_reduce(best[:], logits[:], AX.X, ALU.max))
            step(dve.tensor_tensor(logits[:], logits[:], spread(best[:], E), ALU.subtract))
            dve.sem_inc(logits_made, 1)
            dve.wait_ge(turn.turned, TILES)
            step(dve.tensor_copy(y[:], b2_sum[:].unsqueeze(1).to_broadcast([P, TILES, D])))
            dve.sem_inc(y_kept, 2)
            dve.sem_inc(lo_made, FC)

            def add_up(i, n):
                b = n % BLOCKS
                for bank in range(2):
                    dve.wait_ge(y_done, i * (4 * BLOCKS) + (2 * n + bank + 2 + 4 * BLOCKS))
                    part = y[:, b * 4 + 2 * bank:b * 4 + 2 * bank + 2, :].rearrange("p t d -> p (t d)")
                    dve.tensor_tensor(part, p_y[:, bank, :], part, ALU.add).then_inc(y_kept, 1)

            def run(i, more):
                for n in range(2 * BLOCKS):
                    at = i * (2 * BLOCKS) + n
                    for f in range(FC):
                        dve.wait_ge(h_kept, at * FC + (f + 1 + FC))
                        dve.tensor_tensor(hidden_lo[:, n % 2, f, :], hidden[:, f, :], hidden_hi[:, n % 2, f, :].bitcast(F32),
                                          ALU.subtract).then_inc(lo_made, 1)
                    if n >= 1:
                        add_up(i, n - 1)
                    if n == 1:
                        split_weights(i * 2 + 1, 1)
                    if n == BLOCKS + 1 and more:
                        split_weights(i * 2 + 2, 0)
                add_up(i, 2 * BLOCKS - 1)

            pairs(dve, run)
            dve.wait_ge(exped, 1)
            step = Steps(dve, route_steps, 20)
            step(dve.tensor_reduce(weight[:], logits[:], AX.X, ALU.add))
            step(dve.reciprocal(weight[:], weight[:]))
            step(dve.tensor_scalar(other[:], weight[:], 1e-6, None, ALU.add))
            step(dve.reciprocal(other[:], other[:]))
            step(dve.tensor_tensor(weight[:], weight[:], other[:], ALU.mult))
            step(dve.tensor_scalar(weight[:], weight[:], chip.gates[:, 6:7], None, ALU.mult))
            with dve.Fori(0, TILES // 4) as i:
                for u in range(4):
                    t = i * 4 + u
                    dve.scalar_tensor_tensor(tile_of(chip.x, t), tile_of(y, t), column(weight, t), tile_of(chip.x, t),
                                             ALU.mult, ALU.add).then_inc(added, 1)



HEAD = 64
KEYS = SEQ + CTX
KEY_CHUNKS = 10
BLOCK = 512
BLOCKS_PER_BATCH = SEQ // BLOCK
SLOTS_OF_UNIT = 2 * BLOCKS_PER_BATCH * KEY_CHUNKS
GROUPS = 4
Q_PARTS = ("q0", "q1", "k0", "k1", "kc")
V_PARTS = ("v0", "v1", "v2", "v3", "v4")
FIRST_OUT, LAST_OUT = ("o0", "o1", "o2", "o3"), ("o4", "o5", "o6", "o7")


def key_chunk(c):
    return c * P, min(P, KEYS - c * P)


def part_columns(part):
    if part == "kc":
        return slice(SEQ, KEYS)
    return slice(int(part[1]) * BLOCK, (int(part[1]) + 1) * BLOCK)


def head_rows(h):
    return (slice(0, HEAD), slice(HEAD, P)) if h == 0 else (slice(HEAD, P), slice(0, HEAD))


def extra_rows(h):
    return slice(HEAD, HEAD + 8) if h == 0 else slice(0, 8)


def second_rows(h):
    return slice(0, HEAD + 8) if h == 0 else slice(0, P)


class Uses:

    def __init__(self, names, done, read, maxima):
        self.names, self.done, self.read, self.maxima = names, done, read, maxima

    def bank(self, name):
        return self.names.index(name) % 2

    def done_with(self, name):
        return self.done + (self.names.index(name) + 1)

    def read_before(self, name):
        return self.read + self.names.index(name) // 2

    def read_with(self, name):
        return self.read + (self.names.index(name) // 2 + 1)


class Attention:

    def __init__(self, sb, psum, sem, projected, gate, split=False, out_t=None):
        self.gate, self.split = gate, split
        self.lag = 4 if split else 2
        self.pt_slots = 6 if split else 4
        self.exp_slots = 4
        self.prepares = 8 if split else 7
        self.q1 = sb("q1", [P, 2, 2, SEQ], F32R)
        self.q2 = sb("q2", [P, 2, 2, SEQ], F32R)
        self.k1 = sb("k1", [P, 2, 2, KEYS], F32R)
        self.k2 = sb("k2", [P, 2, 2, KEYS], F32R)
        self.v = sb("v", [P, 2, KEY_CHUNKS, 2, HEAD + 1], F32R if split else F32)
        self.pt = sb("pt", [P, 4, BLOCK])
        if split:
            self.v_lo = sb("v_lo", [P, 2, KEY_CHUNKS, 2, HEAD + 1], F32R)
            self.pt_hi, self.pt_lo = sb("pt_hi", [P, self.pt_slots, BLOCK], F32R), sb("pt_lo", [P, self.pt_slots, BLOCK], F32R)
            self.v_kept, self.lo_made = sem("v_kept"), sem("lo_made")
        self.maxima = sb("maxima", [P, 16])
        self.minus = sb("minus", [8, 8])
        self.out = sb("out", [P, 2, BLOCK])
        self.totals = sb("totals", [P, BLOCK // P])
        self.inverse = sb("inverse", [1, BLOCK])
        self.shared = sb("shared", [P, BLOCK])
        self.out_t = sb("out_t", [P, 2, SEQ]) if out_t is None else out_t
        self.banks = banks = psum("banks", [P, 6, 512])
        self.s_bank, self.st_bank, self.o_bank = banks[:, 0:3, :], banks[:, 3:5, :], banks[:, 5, :]
        self.first_banks = (banks[:, 0:3, :], banks[:, 3:6, :])
        self.side = psum("side", [P, 2, 512])
        self.side_read = [sem("side_read0"), sem("side_read1")]
        self.prepared, self.side_done, self.hi_kept, self.dup_kept = sem("prepared"), sem("side_done"), sem("hi_kept"), sem("dup_kept")
        self.scored, self.maxed, self.st_done, self.exped = sem("scored"), sem("maxed"), sem("st_done"), sem("exped")
        self.pv_done, self.o_kept, self.moved = sem("pv_done"), sem("o_kept"), sem("moved")
        self.inverted, self.returned, self.row_returned = sem("inverted"), sem("returned"), sem("row_returned")
        self.spread_done, self.ot_done, self.passed = sem("spread_done"), sem("ot_done"), sem("passed")
        self.parts = Q_PARTS + V_PARTS if projected else ()
        self.first_order = list(self.parts + ("nA", "nB"))
        if projected:
            self.order = list(Q_PARTS + ("v0",) + LAST_OUT + V_PARTS[1:] + ("nA",) + FIRST_OUT + ("nB",))
        else:
            self.order = list(LAST_OUT + ("nA",) + FIRST_OUT + ("nB",))
        self.prologue = Uses(self.first_order, 0, 0, 0)

    def uses_before(self, unit):
        first, each = len(self.first_order), len(self.order)
        return unit * each + first, unit * (each // 2) + first // 2

    def cycle(self, unit):
        done, read = self.uses_before(unit)
        return Uses(self.order, done, read, unit * 16 + 16)

    def last(self, unit):
        done, read = self.uses_before(unit)
        return Uses(list(LAST_OUT + FIRST_OUT), done, read, 0)

    def epilogue(self, unit):
        done, read = self.uses_before(unit)
        return Uses(list(LAST_OUT), done + 8, read + 4, 0)


class Projection:

    def __init__(self, pe, act, dve, kept, w_out_ready, w_out):
        self.pe, self.act, self.dve, self.kept, self.w_out_ready, self.w_out = pe, act, dve, kept, w_out_ready, w_out


class Mask:
    def __init__(self, row, ones, columns):
        self.row, self.ones, self.columns = row, ones, columns




def attention_prepare(pool, chip, a):
    ones = lambda ap: pool.memset(ap.bitcast(F32), 1.0).then_inc(a.prepared, 1)
    zeros = lambda ap: pool.memset(ap.bitcast(F32), 0.0).then_inc(a.prepared, 1)
    ones(a.k2[HEAD:HEAD + 8, :, 0, :])
    zeros(a.k2[0:HEAD, :, 1, :])
    zeros(a.q2[0:HEAD, :, 1, :])
    pool.wait_ge(a.prepared, 2)
    ones(a.k2[0:8, :, 1, :])
    ones(a.v[:, :, :, :, HEAD:HEAD + 1])
    if a.split:
        zeros(a.v_lo[:, :, :, :, HEAD:HEAD + 1])
    zeros(a.out_t[:, 1, :])
    pool.tensor_scalar(a.minus[:], chip.ident[0:8, 0:8], -1.0, None, ALU.mult).then_inc(a.prepared, 1)


def number(unit, g):
    return unit * GROUPS + (g + 1)


def side_pe(pe, chip, a, uses, name, unit, u, project, group=None):
    bank = a.side[:, uses.bank(name), :]
    if not (isinstance(unit, int) and uses is a.prologue and uses.read_before(name) == 0):
        pe.wait_ge(a.side_read[uses.bank(name)], uses.read_before(name))
    if name[0] == "n":
        h = "AB".index(name[1])
        pe.wait_ge(a.maxed, uses.maxima + 8 * (h + 1))
        ins = pe.transpose(bank[0:8, 0:P], a.maxima[:, h * 8:h * 8 + 8], chip.ident[:])
    elif name[0] == "o":
        t = int(name[1])
        if t == 0:
            pe.wait_ge(a.ot_done, number(unit, 1) + 2)
            project.w_out_ready(pe, unit, u)
        if t == 4:
            pe.wait_ge(a.ot_done, group + 2)
        ins = pe.matmul(bank[:, 0:D], a.out_t[:, u, t * P:(t + 1) * P], project.w_out(unit, u, t), start=True, stop=True)
    else:
        ins = project.pe(pe, bank, name, unit, u)
    ins.then_inc(a.side_done, 1)


def scores_pe(pe, a, unit, u, n, mask):
    h, t = n // 8, n % 8
    hi, _ = head_rows(h)
    banks = a.s_bank if unit is not None else a.first_banks[n % 2]
    if n == 0:
        pe.wait_ge(a.hi_kept, 10 if unit is None else unit * 10 + 10)
    if unit is not None:
        pe.wait_ge(a.maxed, unit * 16 + n)
    elif n >= 2:
        pe.wait_ge(a.maxed, n - 1)
    lhs = a.q1[hi, u, h, t * P:(t + 1) * P]
    for c in range(3):
        at, end = c * BLOCK, min((c + 1) * BLOCK, KEYS)
        masked = mask is not None and c == 2
        ins = pe.matmul(banks[:, c, 0:end - at], lhs, a.k1[hi, u, h, at:end], start=True, stop=not masked)
        if masked:
            ins = pe.matmul(banks[:, c, 0:end - at], mask.ones[0:1, :], mask.row[0:1, u * CTX:(u + 1) * CTX], start=False, stop=True)
    ins.then_inc(a.scored, 1)


def score_slot(n):
    return 8 + 2 * n if n < 8 else 23 + (n - 8) * 13 // 7


def side_slots(projected):
    at = {}
    if projected:
        for j, name in enumerate(Q_PARTS + ("v0",)):
            at[name] = 2 + j
        for j, name in enumerate(LAST_OUT):
            at[name] = 8 + j
        for j, name in enumerate(V_PARTS[1:]):
            at[name] = 12 + j
    else:
        for j, name in enumerate(LAST_OUT):
            at[name] = 8 + j
    at["nA"], at["nB"] = 24, 38
    for j, name in enumerate(FIRST_OUT):
        at[name] = 32 + j
    return at


def attention_pe(pe, chip, a, unit, u, uses, project, mask=None, following=True):
    slots = side_slots(bool(a.parts))
    pe.wait_ge(a.dup_kept, unit * 10 + 10)
    before = uses.read
    for bank in range(2):
        pe.wait_ge(a.side_read[bank], before)
    if project.kept is not None:
        project.kept(pe, unit)

    def multiply_values(n):
        b, h, c = n // 20, (n // 10) % 2, n % 10
        row, rows = key_chunk(c)
        if a.split:
            pe.wait_ge(a.lo_made, unit * SLOTS_OF_UNIT + (n + 1 + a.exp_slots))
        else:
            pe.wait_ge(a.exped, unit * SLOTS_OF_UNIT + (n + 1 + 2))
        if c == 0:
            pe.wait_ge(a.o_kept, number(unit, n // 10))
        slot = n % a.pt_slots
        parts = ((a.v, a.pt_hi), (a.v_lo, a.pt_hi), (a.v, a.pt_lo)) if a.split else ((a.v, a.pt),)
        for k, (v, pt) in enumerate(parts):
            ins = pe.matmul(a.o_bank[0:HEAD + 1, :], v[0:rows, u, c, h, :], pt[0:rows, slot, :],
                            start=c == 0 and k == 0, stop=c == KEY_CHUNKS - 1 and k == len(parts) - 1)
        ins.then_inc(a.pv_done, 1)

    for n in range(SLOTS_OF_UNIT):
        b, h, c = n // 20, (n // 10) % 2, n % 10
        row, rows = key_chunk(c)
        pe.wait_ge(a.exped, unit * SLOTS_OF_UNIT + (n + 1))
        queries = slice(b * BLOCK, (b + 1) * BLOCK)
        second = second_rows(h)
        pe.matmul(a.st_bank[0:rows, n % 2, :], a.k1[:, u, h, row:row + rows], a.q1[:, u, h, queries], start=True, stop=False)
        pe.matmul(a.st_bank[0:rows, n % 2, :], a.k2[second, u, h, row:row + rows], a.q2[second, u, h, queries],
                  start=False, stop=True).then_inc(a.st_done, 1)
        for name, slot in slots.items():
            if slot == n and name in uses.names:
                side_pe(pe, chip, a, uses, name, unit, u if name in FIRST_OUT else 1 - u, project, number(unit, -1))
        if following:
            for m in range(16):
                if score_slot(m) == n:
                    scores_pe(pe, a, unit + 1, 1 - u, m, mask)
        if n >= a.lag:
            multiply_values(n - a.lag)
    for n in range(SLOTS_OF_UNIT - a.lag, SLOTS_OF_UNIT):
        multiply_values(n)


def attention_act(act, a, unit, u, uses, scale, project, mask=None, following=True):
    slots = side_slots(bool(a.parts))
    for n in range(SLOTS_OF_UNIT):
        b, h, c = n // 20, (n // 10) % 2, n % 10
        row, rows = key_chunk(c)
        act.wait_ge(a.pv_done, unit * SLOTS_OF_UNIT + (n + 1))
        act.wait_ge(a.st_done, unit * SLOTS_OF_UNIT + (n + 1))
        if n % 10 == a.lag and n > 10:
            keep_group(act, a, unit, n // 10 - 1)
        bias = mask.columns[0:rows, u * 2 + c - 8:u * 2 + c - 7] if mask is not None and c >= 8 else 0.0
        if a.split:
            act.wait_ge(a.lo_made, unit * SLOTS_OF_UNIT + (n + 1))
            act.activation(a.pt_hi[0:rows, n % a.pt_slots, :], a.st_bank[0:rows, n % 2, :], ACT.Exp, bias=bias, scale=scale)
        act.activation(a.pt[0:rows, n % 4, :], a.st_bank[0:rows, n % 2, :], ACT.Exp, bias=bias, scale=scale).then_inc(a.exped, 1)
        if following:
            for name, slot in slots.items():
                if slot == n and name in uses.names:
                    keep_part_act(act, a, uses, name, unit + 1, 1 - u)
            if project.act is not None:
                project.act(act, unit + 1, 1 - u, n)
    keep_group(act, a, unit, GROUPS - 1)


def keep_group(act, a, unit, g):
    act.wait_ge(a.pv_done, unit * SLOTS_OF_UNIT + (10 * (g + 1) + a.pt_slots))
    act.wait_ge(a.ot_done, number(unit, g))
    act.copy(a.out[0:HEAD + 1, g % 2, :], a.o_bank[0:HEAD + 1, :]).then_inc(a.o_kept, 1)


def keep_part_act(act, a, uses, name, unit, u):
    if name[0] in "no":
        return
    bank = a.side[:, uses.bank(name), :]
    act.wait_ge(a.side_done, uses.done_with(name))
    if name[0] == "v":
        j = int(name[1])
        for c in (2 * j, 2 * j + 1):
            _, rows = key_chunk(c)
            ins = act.copy(a.v[0:rows, u, c, :, 0:HEAD],
                           bank[0:rows, (c % 2) * P:(c % 2 + 1) * P].rearrange("p (h d) -> p h d", h=2))
        ins.then_inc(a.v_kept if a.split else a.side_read[uses.bank(name)], 1)
        return
    to, columns = (a.q1 if name[0] == "q" else a.k1), part_columns(name)
    for h in range(2):
        hi, _ = head_rows(h)
        act.copy(to[hi, u, h, columns], bank[hi, 0:columns.stop - columns.start]).then_inc(a.hi_kept, 1)


def keep_part_dve(dve, a, uses, name, unit, u):
    bank = a.side[:, uses.bank(name), :]
    if name[0] == "n":
        h = "AB".index(name[1])
        dve.wait_ge(a.side_done, uses.done_with(name))
        dve.tensor_tensor(a.q2[extra_rows(h), u, h, :].rearrange("p (t q) -> p t q", q=P),
                          bank[0:8, 0:P].unsqueeze(1).to_broadcast([8, 8, P]), spread(a.minus[:], P), ALU.mult
                          ).then_inc(a.side_read[uses.bank(name)], 1)
        return
    if name[0] == "v" and a.split:
        j = int(name[1])
        dve.wait_ge(a.v_kept, unit * 5 + (j + 1))
        for c in (2 * j, 2 * j + 1):
            _, rows = key_chunk(c)
            ins = dve.tensor_tensor(a.v_lo[0:rows, u, c, :, 0:HEAD],
                                    bank[0:rows, (c % 2) * P:(c % 2 + 1) * P].rearrange("p (h d) -> p h d", h=2),
                                    a.v[0:rows, u, c, :, 0:HEAD].bitcast(F32), ALU.subtract)
        ins.then_inc(a.side_read[uses.bank(name)], 1)
    if name not in Q_PARTS:
        return
    columns = part_columns(name)
    dve.wait_ge(a.hi_kept, unit * 10 + 2 * (Q_PARTS.index(name) + 1))
    for h in range(2):
        hi, other = head_rows(h)
        source = a.q1 if name[0] == "q" else a.k1
        out = a.q2[hi, u, h, columns] if name[0] == "q" else a.k1[other, u, h, columns]
        ins = dve.tensor_tensor(out, bank[hi, 0:columns.stop - columns.start], source[hi, u, h, columns].bitcast(F32), ALU.subtract)
    ins.then_inc(a.side_read[uses.bank(name)], 1)


def add_output(dve, chip, a, uses, name, u):
    t = int(name[1]) + u * BATCH_TILES
    dve.wait_ge(a.side_done, uses.done_with(name))
    dve.scalar_tensor_tensor(chip.x[:, t, :], a.side[:, uses.bank(name), 0:D], a.gate, chip.x[:, t, :],
                             ALU.mult, ALU.add).then_inc(a.side_read[uses.bank(name)], 1)


def largest(dve, a, unit, n):
    banks = a.s_bank if unit is not None else a.first_banks[n % 2]
    dve.wait_ge(a.scored, (n + 1) if unit is None else unit * 16 + (n + 1))
    dve.tensor_reduce(a.maxima[:, n:n + 1], banks.rearrange("p a b -> p (a b)")[:, 0:KEYS], AX.X, ALU.max).then_inc(a.maxed, 1)


def attention_dve(dve, chip, a, unit, u, uses, project, following=True):
    slots = side_slots(bool(a.parts))
    for n in range(SLOTS_OF_UNIT):
        g, k = (3 if n < 10 else n // 10 - 1), number(unit, n // 10 - 1)
        if n % 10 == (4 if n < 10 else 7 if a.split else 6):
            invert_group(dve, a, k, g)
        for name, slot in slots.items():
            if slot == n and name in uses.names:
                if name in LAST_OUT:
                    add_output(dve, chip, a, uses, name, 1 - u)
                elif name in FIRST_OUT:
                    add_output(dve, chip, a, uses, name, u)
                else:
                    keep_part_dve(dve, a, uses, name, unit + 1, 1 - u)
        if following:
            if project.dve is not None:
                project.dve(dve, unit + 1, 1 - u, n)
            for m in range(16):
                if score_slot(m) == n:
                    largest(dve, a, unit + 1, m)
        if a.split:
            slot, rows = n % a.pt_slots, key_chunk(n % 10)[1]
            dve.wait_ge(a.exped, unit * SLOTS_OF_UNIT + (n + 1 + 2))
            dve.tensor_tensor(a.pt_lo[0:rows, slot, :], a.pt[0:rows, n % 4, :], a.pt_hi[0:rows, slot, :].bitcast(F32),
                              ALU.subtract).then_inc(a.lo_made, 1)



def move_totals(sp, a, k, g):
    sp.wait_ge(a.o_kept, k + 1)
    sp.dma_start(a.totals[:], a.out[HEAD:HEAD + 1, g % 2, :]).then_inc(a.moved, 16)
    sp.wait_ge(a.inverted, k + 1)
    sp.wait_ge(a.spread_done, k + 1)
    sp.dma_start(a.inverse[:], a.totals[:]).then_inc(a.returned, 16)
    sp.wait_ge(a.returned, k * 16 + 16)
    sp.sem_inc(a.row_returned, 1)


def invert_group(dve, a, k, g):
    dve.wait_ge(a.moved, k * 16 + 16)
    dve.reciprocal(a.totals[:], a.totals[:]).then_inc(a.inverted, 1)


def scale_group(pool, a, k, g, parity):
    pool.wait_ge(a.ot_done, k + 1)
    pool.wait_ge(a.returned, k * 16 + 16)
    pool.sem_inc(a.passed, 1)
    pool.partition_broadcast(a.shared[0:HEAD, :], a.inverse[:], channels=HEAD).then_inc(a.spread_done, 1)
    pool.wait_ge(a.spread_done, k + 2)
    pool.sem_inc(a.passed, 1)
    b, (hi, _) = g // 2, head_rows(g % 2)
    pool.tensor_tensor(a.out_t[hi, parity, b * BLOCK:(b + 1) * BLOCK], a.out[0:HEAD, g % 2, :], a.shared[0:HEAD, :],
                       ALU.mult).then_inc(a.ot_done, 1)


def attention_pool(pool, a, unit, u, following=True):
    scale_group(pool, a, number(unit, -1), 3, 1 - u)
    if following:
        pool.wait_ge(a.ot_done, number(unit, -1) + 2)
        pool.sem_inc(a.passed, 1)
        double_parts(pool, a, unit + 1, 1 - u)
    pool.wait_ge(a.dup_kept, unit * 10 + (20 if following else 10))
    for g in range(GROUPS - 1):
        scale_group(pool, a, number(unit, g), g, u)


def attention_sync(sp, a, unit, u, extra=None):
    move_totals(sp, a, number(unit, -1), 3)
    if extra is not None:
        extra("o7")
    move_totals(sp, a, number(unit, 0), 0)
    if extra is not None:
        extra("v4")
    for g in (1, 2):
        move_totals(sp, a, number(unit, g), g)


def attention_start_act(act, chip, a):
    act.wait_ge(a.prepared, a.prepares)
    act.sem_inc(a.exped, 2)
    for n in range(BLOCK // P):
        act.mul(a.out[0:HEAD, 1, n * P:(n + 1) * P], chip.ones[0:HEAD, :], 0.0)
        ins = act.copy(a.out[HEAD:HEAD + 1, 1, n * P:(n + 1) * P], chip.ones[HEAD:HEAD + 1, :])
    ins.then_inc(a.o_kept, 1)


def attention_end(sp, dve, pool, a, last):
    k = number(last, 3)
    if sp is not None:
        move_totals(sp, a, k, 3)
    if dve is not None:
        invert_group(dve, a, k, 3)
    if pool is not None:
        scale_group(pool, a, k, 3, 1)


def double_parts(pool, a, unit, u):
    for j, name in enumerate(Q_PARTS):
        pool.wait_ge(a.hi_kept, unit * 10 + 2 * (j + 1))
        pool.sem_inc(a.passed, 1)
        columns = part_columns(name)
        for h in range(2):
            hi, other = head_rows(h)
            if name[0] == "q":
                out, source = a.q1[other, u, h, columns], a.q1[hi, u, h, columns]
            else:
                out, source = a.k2[hi, u, h, columns], a.k1[hi, u, h, columns]
            pool.tensor_copy(out, source.bitcast(F32)).then_inc(a.dup_kept, 1)


def first_maxima_pe(pe, chip, a, project, mask=None):
    pe.wait_ge(a.prepared, a.prepares)
    for name in a.parts:
        side_pe(pe, chip, a, a.prologue, name, 0, 0, project)
    for h in range(2):
        for m in range(8):
            scores_pe(pe, a, None, 0, 8 * h + m, mask)
        side_pe(pe, chip, a, a.prologue, "n" + "AB"[h], 0, 0, project)


def first_maxima_dve(dve, a):
    for h in range(2):
        for m in range(8):
            largest(dve, a, None, 8 * h + m)
        keep_part_dve(dve, a, a.prologue, "n" + "AB"[h], 0, 0)


def attention_units(engine, pairs, cycle):
    if pairs > 2:
        with engine.Fori(0, pairs - 1) as i:
            for u in range(BATCH):
                cycle(i * BATCH + u, u, True)
    else:
        for u in range(BATCH):
            cycle(u, u, True)
    cycle(BATCH * (pairs - 1), 0, True)
    cycle(BATCH * (pairs - 1) + 1, 1, False)


def add_bias_pool(pool, chip, sem, gb_made, gb):
    pool.wait_ge(gb_made, 1)
    pool.wait_ge(sem, NORM_STEPS + TILES)
    pool.tensor_tensor(chip.x[:], chip.x[:], gb.unsqueeze(1).to_broadcast([P, TILES, D]), ALU.add).then_inc(gb_made, 1)


def normalize_twice_dve(dve, chip, sem):
    row_statistics(dve, chip, sem, 0, chip.x)
    with dve.Fori(0, TILES // 4) as i:
        for v in range(4):
            t = i * 4 + v
            dve.tensor_scalar(tile_of(chip.xn, t), tile_of(chip.x, t), column(chip.mean, t), column(chip.inv_std, t),
                              ALU.subtract, ALU.mult).then_inc(sem, 1)
    dve.wait_ge(sem, NORM_STEPS + TILES)
    row_statistics(dve, chip, sem, NORM_STEPS + TILES, chip.xn)



def l1_attention(nc, chip, I):
    PAIRS = 2
    INNER = 2 * HEAD * PAIRS
    HEADS = 2 * PAIRS
    CT = 2 * BATCH
    SCALE = HEAD ** -0.5
    OFF = 1e30
    with ExitStack() as kept_stack:
        sb, _, sem = scope(nc, kept_stack, "l1a")
        k_t = sb("k_t", [P, PAIRS, BATCH * KEYS])
        v_all = sb("v_all", [P, TILES + CT, INNER])
        wo = sb("wo", [P, PAIRS, D])
        mask_bytes, mask_flat = sb("mask_bytes", [1, BATCH * CTX], mybir.dt.uint8), sb("mask_flat", [1, BATCH * CTX])
        mask_row, mask_ones = sb("mask_row", [1, BATCH * CTX], F32R), sb("mask_ones", [1, P], F32R)
        mask_columns = sb("mask_columns", [P, CT])
        q_t = chip.xt
        wo_loaded = sem("wo_loaded")

        with ExitStack() as stack:
            sb, psum, sem = scope(nc, stack, "l1p")
            w = sb("w", [P, DC, 3 * INNER])
            rows_in, columns = sb("rows_in", [10, P]), sb("columns", [P, 10])
            gb = sb("gb", [P, D])
            c_stats, c_stage, ctxn_t = sb("c_stats", [P, CT, 6]), sb("c_stage", [P, CT, D]), sb("ctxn_t", [P, DC, BATCH * CTX])
            c_mean, c_inv, c_a, c_b, c_c = (sb(n, [P, CT]) for n in ("c_mean", "c_inv", "c_a", "c_b", "c_c"))
            qk = sb("qk", [P, TILES + CT, 2 * INNER])
            squares = sb("squares", [P, 2, 2 * INNER])
            sums, inv, half, value = (sb(n, [P, TILES + CT, 2 * HEADS]) for n in ("sums", "inv", "half", "value"))
            banks, pt, pc = psum("banks", [P, 4, 512]), psum("pt", [P, 2, 512]), psum("pc", [P, 2, 512])
            pq, pv = banks[:, 0:2, :], banks[:, 2:4, :]
            turn = TurnSemaphores(sem, "t")
            (loaded, w_loaded, made, gb_made, norm_steps, c_steps, c_staged, rows_turned, rows_kept, c_turned, c_kept,
             projected, qk_kept, squared, v_kept, root_steps, scaled, qk_turned, q_kept, kk_kept, mask_steps, mask_done, mask_kept) = (
                sem(n) for n in (
                    "loaded", "w_loaded", "made", "gb_made", "norm_steps", "c_steps", "c_staged", "rows_turned",
                    "rows_kept", "c_turned", "c_kept", "projected", "qk_kept", "squared", "v_kept", "root_steps", "scaled",
                    "qk_turned", "q_kept", "kk_kept", "mask_steps", "mask_done", "mask_kept"))
            block = stack.enter_context(nc.Block())

            def tile_rows(t):
                return P if t < TILES or t % 2 == 0 else CTX_REST

            @block.sync
            def _(sp):
                for k, name in enumerate(("ln_x_g", "ln_x_b", "ln_l_g", "ln_l_b")):
                    sp.dma_start(rows_in[2 * k:2 * k + 2, :], I["L1_xattn_" + name].rearrange("(c p) -> c p", p=P)).then_inc(loaded, 16)
                for k, name in enumerate(("q_gamma", "k_gamma")):
                    for h in range(2):
                        sp.dma_start(rows_in[8 + k:9 + k, h * HEAD:(h + 1) * HEAD],
                                     I["L1_xattn_" + name].rearrange("(a d) -> a d", a=1)).then_inc(loaded, 16)
                sp.dma_start(mask_bytes[:], I["mask_BxS2_bk0"].rearrange("b c -> (b c)").rearrange("(a d) -> a d", a=1)).then_inc(loaded, 16)
                sp.dma_start(gb[:], I["L1_xattn_b_out"].partition_broadcast(P)).then_inc(loaded, 16)
                sp.dma_start(w[:, :, 0:INNER], I["L1_xattn_W_q"].rearrange("(c p) n -> p c n", p=P)).then_inc(w_loaded, 16)
                sp.dma_start(w[:, :, INNER:3 * INNER], I["L1_xattn_W_kv"].rearrange("(c p) n -> p c n", p=P)).then_inc(w_loaded, 16)
                sp.dma_start(wo[:], I["L1_xattn_W_out"].rearrange("(c p) n -> p c n", p=P)).then_inc(wo_loaded, 16)

            LOADED = 10 * 16

            @block.gpsimd
            def _(pool):
                pool.memset(c_stats[:], 0.0).then_inc(made, 1)
                pool.memset(sums[:], 1.0).then_inc(made, 1)
                pool.memset(mask_ones[:].bitcast(F32), 1.0).then_inc(made, 1)
                add_bias_pool(pool, chip, norm_steps, gb_made, gb[:])

            @block.tensor
            def _(pe):
                pe.wait_ge(loaded, LOADED)
                pe.transpose(pt[:, 0, 0:10], rows_in[:], chip.ident[0:10, 0:10]).then_inc(rows_turned, 1)
                pe.wait_ge(mask_steps, 2)
                for b in range(BATCH):
                    for c, (row, rows) in enumerate(CHUNKS):
                        at = b * CTX + row
                        ins = pe.matmul(pc[0:rows, 0, 2 * b + c:2 * b + c + 1], mask_flat[0:1, at:at + rows], chip.ones[0:1, 0:1],
                                        start=True, stop=True)
                ins.then_inc(mask_done, 1)
                turn_pe(pe, chip, turn, banks)
                for k in range(CT):
                    rows = tile_rows(TILES + k)
                    pe.wait_ge(c_staged, k + 1)
                    if k == 0:
                        pe.wait_ge(rows_kept, 1)
                    if k >= 2:
                        pe.wait_ge(c_kept, k - 1)
                    for c in range(DC):
                        ins = pe.transpose(pt[:, k % 2, c * P:c * P + rows], c_stage[0:rows, k, c * P:(c + 1) * P], chip.ident[0:rows, 0:rows])
                    ins.then_inc(c_turned, 1)
                pe.wait_ge(w_loaded, 32)
                pe.wait_ge(turn.turned_read, TILES)
                pe.wait_ge(c_kept, CT)
                for t in range(TILES + CT):
                    rows, bank = tile_rows(t), t % 2
                    if t >= 2:
                        pe.wait_ge(squared, t - 1)
                        pe.wait_ge(v_kept, t - 1)
                    if t < TILES:
                        source, at, first = chip.xt, t * P, 0
                    else:
                        source, at, first = ctxn_t, (t - TILES) // 2 * CTX + CHUNKS[t % 2][0], INNER
                    for c in range(DC):
                        pe.matmul(pq[0:rows, bank, first:2 * INNER], source[:, c, at:at + rows], w[:, c, first:2 * INNER],
                                  start=c == 0, stop=c == DC - 1)
                    for c in range(DC):
                        ins = pe.matmul(pv[0:rows, bank, 0:INNER], source[:, c, at:at + rows], w[:, c, 2 * INNER:3 * INNER],
                                        start=c == 0, stop=c == DC - 1)
                    ins.then_inc(projected, 1)
                for t in range(TILES + CT):
                    rows, bank = tile_rows(t), t % 2
                    pe.wait_ge(scaled, t + 1)
                    if t >= 2:
                        pe.wait_ge(kk_kept, t - 1)
                    for j in range(0 if t < TILES else PAIRS, 2 * PAIRS):
                        ins = pe.transpose(pt[:, bank, j * P:j * P + rows], qk[0:rows, t, j * P:(j + 1) * P], chip.ident[0:rows, 0:rows])
                    ins.then_inc(qk_turned, 1)

            @block.scalar
            def _(act):
                act.wait_ge(rows_turned, 1)
                act.copy(columns[:], pt[:, 0, 0:10]).then_inc(rows_kept, 1)
                act.wait_ge(rows_kept, 1)
                act.wait_ge(mask_done, 1)
                for b in range(BATCH):
                    for c, (row, rows) in enumerate(CHUNKS):
                        act.copy(mask_columns[0:rows, 2 * b + c:2 * b + c + 1], pc[0:rows, 0, 2 * b + c:2 * b + c + 1]).then_inc(mask_kept, 1)
                turn_act(act, chip, turn, banks, scale=columns[:, 4:6], bias=columns[:, 6:8])
                for k in range(CT):
                    rows = tile_rows(TILES + k)
                    act.wait_ge(c_turned, k + 1)
                    at = k // 2 * CTX + CHUNKS[k % 2][0]
                    for c in range(DC):
                        ins = act.activation(ctxn_t[:, c, at:at + rows], pt[:, k % 2, c * P:c * P + rows], ACT.Identity,
                                             bias=columns[:, 2 + c:3 + c], scale=columns[:, c:c + 1])
                    ins.then_inc(c_kept, 1)
                for t in range(TILES + CT):
                    rows, bank, first = tile_rows(t), t % 2, 0 if t < TILES else INNER
                    act.wait_ge(projected, t + 1)
                    act.copy(qk[0:rows, t, first:2 * INNER], pq[0:rows, bank, first:2 * INNER]).then_inc(qk_kept, 1)
                    if t >= 2:
                        act.wait_ge(root_steps, t - 1)
                    act.activation(squares[0:rows, bank, first:2 * INNER], pq[0:rows, bank, first:2 * INNER], ACT.Square).then_inc(squared, 1)
                    act.copy(v_all[0:rows, t, :], pv[0:rows, bank, 0:INNER]).then_inc(v_kept, 1)
                for t in range(TILES + CT):
                    rows, bank = tile_rows(t), t % 2
                    act.wait_ge(qk_turned, t + 1)
                    if t < TILES:
                        b, at = t // BATCH_TILES, t % BATCH_TILES * P
                        act.mul(q_t[:, :, t * P:(t + 1) * P], pt[:, bank, 0:INNER].rearrange("p (j q) -> p j q", j=PAIRS),
                                columns[:, 8:9]).then_inc(q_kept, 1)
                    else:
                        b, at = (t - TILES) // 2, SEQ + CHUNKS[t % 2][0]
                    act.mul(k_t[:, :, b * KEYS + at:b * KEYS + at + rows],
                            pt[:, bank, INNER:2 * INNER].rearrange("p (j q) -> p j q", j=PAIRS)[:, :, 0:rows], columns[:, 9:10]
                            ).then_inc(kk_kept, 1)

            @block.vector
            def _(dve):
                dve.wait_ge(loaded, LOADED)
                dve.tensor_scalar(gb[:], gb[:], chip.gates[:, 1:2], None, ALU.mult).then_inc(gb_made, 1)
                step = Steps(dve, mask_steps)
                step(dve.tensor_copy(mask_flat[:], mask_bytes[:]))
                step(dve.tensor_scalar(mask_flat[:], mask_flat[:], 1.0, OFF, ALU.subtract, ALU.mult))
                step(dve.tensor_copy(mask_row[:], mask_flat[:]))
                dve.wait_ge(made, 3)
                for k in range(CT):
                    rows = tile_rows(TILES + k)
                    dve.bn_stats(c_stats[0:rows, k, :], chip.ctx[0:rows, k // 2, k % 2, :]).then_inc(c_steps, 1)
                dve.wait_ge(c_steps, CT)
                aggregate(dve, c_steps, CT, c_stats[:], c_mean[:], c_inv[:], (c_a[:], c_b[:], c_c[:]))
                for k in range(CT):
                    rows = tile_rows(TILES + k)
                    dve.tensor_scalar(c_stage[0:rows, k, :], chip.ctx[0:rows, k // 2, k % 2, :], c_mean[0:rows, k:k + 1],
                                      c_inv[0:rows, k:k + 1], ALU.subtract, ALU.mult).then_inc(c_staged, 1)
                normalize_twice_dve(dve, chip, norm_steps)
                normalize_dve(dve, chip, turn, chip.xn)
                for t in range(TILES + CT):
                    rows, first = tile_rows(t), 0 if t < TILES else INNER
                    dve.wait_ge(squared, t + 1)
                    dve.tensor_reduce(sums[0:rows, t, first // HEAD:2 * HEADS],
                                      squares[0:rows, t % 2, first:2 * INNER].rearrange("p (h d) -> p h d", d=HEAD), AX.X, ALU.add
                                      ).then_inc(root_steps, 1)
                dve.wait_ge(root_steps, TILES + CT)
                step = Steps(dve, root_steps, TILES + CT)
                flat = lambda tensor: tensor[:].rearrange("p t h -> p (t h)")
                step(dve.tensor_scalar(sums[:], sums[:], HEAD * 1e-16, None, ALU.max))
                inverse_root(dve, step, flat(inv), flat(sums), 1.0 / HEAD, 0.0, (flat(value), flat(half)))
                dve.wait_ge(qk_kept, TILES + CT)
                for t in range(TILES + CT):
                    rows, first = tile_rows(t), 0 if t < TILES else INNER
                    part = qk[0:rows, t, first:2 * INNER].rearrange("p (h d) -> p h d", d=HEAD)
                    dve.tensor_tensor(part, part, spread(inv[0:rows, t, first // HEAD:2 * HEADS], HEAD), ALU.mult).then_inc(scaled, 1)

        with ExitStack() as stack:
            sb, psum, sem = scope(nc, stack, "l1a2")
            a = Attention(sb, psum, sem, projected=False, gate=chip.gates[:, 1:2],
                                  out_t=chip.xn[:, 0:8, :].rearrange("p (u t) d -> p u (t d)", u=2))
            lo_kept = sem("lo_kept")
            mask = Mask(row=mask_row, ones=mask_ones, columns=mask_columns)
            block = stack.enter_context(nc.Block())

            def source_of(name, pair, b):
                columns = part_columns(name)
                if name[0] == "q":
                    return q_t[:, pair, b * SEQ + columns.start:b * SEQ + columns.stop]
                return k_t[:, pair, b * KEYS + columns.start:b * KEYS + columns.stop]

            def keep_hi_act(act, unit, u, n):
                if 2 <= n < 7:
                    name = Q_PARTS[n - 2]
                    to = a.q1 if name[0] == "q" else a.k1
                    for h in range(2):
                        hi, _ = head_rows(h)
                        act.copy(to[hi, u, h, part_columns(name)], source_of(name, unit // 2, u)[hi]).then_inc(a.hi_kept, 1)
                if n == 7:
                    for h in range(2):
                        at = unit // 2 * P + h * HEAD
                        act.copy(a.v[:, u, 0:8, h, 0:HEAD], v_all[:, u * 8:u * 8 + 8, at:at + HEAD])
                        for c in range(2):
                            rows = CHUNKS[c][1]
                            act.copy(a.v[0:rows, u, 8 + c, h, 0:HEAD], v_all[0:rows, TILES + 2 * u + c, at:at + HEAD])

            def keep_lo_dve(dve, unit, u, n):
                if not 2 <= n < 7:
                    return
                name = Q_PARTS[n - 2]
                dve.wait_ge(a.hi_kept, unit * 10 + 2 * (n - 1))
                for h in range(2):
                    hi, other = head_rows(h)
                    columns = part_columns(name)
                    hi_values = (a.q1 if name[0] == "q" else a.k1)[hi, u, h, columns].bitcast(F32)
                    out = a.q2[hi, u, h, columns] if name[0] == "q" else a.k1[other, u, h, columns]
                    ins = dve.tensor_tensor(out, source_of(name, unit // 2, u)[hi], hi_values, ALU.subtract)
                ins.then_inc(lo_kept, 1)

            project = Projection(
                pe=None, act=keep_hi_act, dve=keep_lo_dve, kept=lambda pe, unit: pe.wait_ge(lo_kept, unit * 5 + 5),
                w_out_ready=lambda pe, unit, u: None,
                w_out=lambda unit, u, t: wo[:, (unit if t < 4 else max(unit - 1, 0)) // 2, :])
            uses_of = lambda unit, following: (a.cycle if following else a.last)(unit)

            @block.tensor
            def _(pe):
                pe.sem_inc(a.pv_done, a.pt_slots)
                pe.wait_ge(wo_loaded, 16)
                first_maxima_pe(pe, chip, a, project, mask)
                attention_units(pe, PAIRS, lambda unit, u, following: attention_pe(
                    pe, chip, a, unit, u, uses_of(unit, following), project, mask, following))
                last = BATCH * PAIRS - 1
                for name in LAST_OUT:
                    side_pe(pe, chip, a, a.epilogue(last), name, last, 1, project, number(last, 3))

            @block.scalar
            def _(act):
                attention_start_act(act, chip, a)
                for n in range(8):
                    keep_hi_act(act, 0, 0, n)
                attention_units(act, PAIRS, lambda unit, u, following: attention_act(
                    act, a, unit, u, uses_of(unit, following), SCALE, project, mask, following))

            @block.vector
            def _(dve):
                dve.wait_ge(a.prepared, a.prepares)
                for n in range(8):
                    keep_lo_dve(dve, 0, 0, n)
                first_maxima_dve(dve, a)
                attention_units(dve, PAIRS, lambda unit, u, following: attention_dve(
                    dve, chip, a, unit, u, uses_of(unit, following), project, following))
                attention_end(None, dve, None, a, BATCH * PAIRS - 1)
                for name in LAST_OUT:
                    add_output(dve, chip, a, a.epilogue(BATCH * PAIRS - 1), name, 1)

            @block.gpsimd
            def _(pool):
                attention_prepare(pool, chip, a)
                pool.wait_ge(a.prepared, a.prepares)
                pool.sem_inc(a.spread_done, 1)
                pool.sem_inc(a.ot_done, 1)
                double_parts(pool, a, 0, 0)
                attention_units(pool, PAIRS, lambda unit, u, following: attention_pool(pool, a, unit, u, following))
                attention_end(None, None, pool, a, BATCH * PAIRS - 1)

            @block.sync
            def _(sp):
                attention_units(sp, PAIRS, lambda unit, u, following: attention_sync(sp, a, unit, u))
                attention_end(sp, None, None, a, BATCH * PAIRS - 1)



def l3_attention(nc, chip, I):
    PAIRS = 8
    INNER = 2 * HEAD * PAIRS
    SCALE = HEAD ** -0.5
    with ExitStack() as stack:
        sb, psum, sem = scope(nc, stack, "l3a")
        w = sb("w", [P, 4, DC, P])
        wo = sb("wo", [P, D])
        ln_rows, ln = sb("ln_rows", [2 * DC, P]), sb("ln", [P, 2 * DC])
        gb = sb("gb", [P, D])
        a = Attention(sb, psum, sem, projected=True, gate=chip.gates[:, 3:4], split=True)
        turn = TurnSemaphores(sem, "t")
        loaded, norm_steps, gb_made, ln_turned, ln_kept, w_loaded, wo_loaded = (sem(n) for n in (
            "loaded", "norm_steps", "gb_made", "ln_turned", "ln_kept", "w_loaded", "wo_loaded"))
        block = stack.enter_context(nc.Block())

        def load_weights(sp, pair):
            for k, (name, at) in enumerate((("L3_xattn_Wq", 0), ("L3_xattn_Wkv", 0), ("L3_xattn_Wkv", INNER), ("L3_xattn_Wm", 0))):
                sp.dma_start(w[:, k, :, :], I[name].rearrange("(c p) n -> p c n", p=P)[:, :, bass.ds(pair * P + at, P)]).then_inc(w_loaded, 16)

        def load_w_out(sp, pair):
            sp.dma_start(wo[:], I["L3_xattn_Wo"][bass.ds(pair * P, P), :]).then_inc(wo_loaded, 16)

        def project_pe(pe, bank, name, unit, u):
            if name == "q0" and u == 0:
                first = isinstance(unit, int) and unit == 0
                pe.wait_ge(w_loaded, 64 if first else unit * 32 + 96)
            base = u * SEQ
            if name[0] == "v":
                for chunk in (2 * int(name[1]), 2 * int(name[1]) + 1):
                    at, rows = key_chunk(chunk)
                    out = bank[0:rows, (chunk % 2) * P:(chunk % 2 + 1) * P]
                    for c in range(DC):
                        tokens = chip.xt[:, c, base + at:base + at + rows] if at < SEQ else \
                            chip.ctxt[:, c, u * CTX + at - SEQ:u * CTX + at - SEQ + rows]
                        ins = pe.matmul(out, tokens, w[:, 2 if at < SEQ else 3, c, :], start=c == 0, stop=c == DC - 1)
                return ins
            k = {"q": 0, "k": 1}[name[0]]
            if name == "kc":
                out, source, at, k = bank[:, 0:CTX], chip.ctxt, u * CTX, 3
            else:
                out, source, at = bank[:, 0:BLOCK], chip.xt, base + int(name[1]) * BLOCK
            for c in range(DC):
                ins = pe.matmul(out, w[:, k, c, :], source[:, c, at:at + out.shape[1]], start=c == 0, stop=c == DC - 1)
            return ins

        def w_out_ready(pe, unit, u):
            pe.wait_ge(wo_loaded, unit * 8 + (32 - 8 * u))

        project = Projection(pe=project_pe, act=None, dve=None, kept=None, w_out_ready=w_out_ready,
                                  w_out=lambda unit, u, t: wo[:])

        @block.sync
        def _(sp):
            sp.dma_start(ln_rows[0:DC, :], I["L3_xattn_ln_g"].rearrange("(c p) -> c p", p=P)).then_inc(loaded, 16)
            sp.dma_start(ln_rows[DC:2 * DC, :], I["L3_xattn_ln_b"].rearrange("(c p) -> c p", p=P)).then_inc(loaded, 16)
            sp.dma_start(gb[:], I["L3_xattn_bo"].partition_broadcast(P)).then_inc(loaded, 16)
            load_weights(sp, 0)
            load_w_out(sp, 0)

            def cycle(unit, u, following, pair, following_pair):
                uses = (a.cycle if following else a.last)(unit)

                def extra(name):
                    if u == 1:
                        return
                    if name == "o7":
                        sp.wait_ge(a.side_done, uses.done_with("o7"))
                        load_w_out(sp, pair)
                    elif following_pair:
                        sp.wait_ge(a.side_done, uses.done_with("v4"))
                        load_weights(sp, pair + 1)
                attention_sync(sp, a, unit, u, extra)

            with sp.Fori(0, PAIRS - 1) as i:
                for u in range(BATCH):
                    cycle(i * BATCH + u, u, True, i, True)
            cycle(BATCH * (PAIRS - 1), 0, True, PAIRS - 1, False)
            cycle(BATCH * (PAIRS - 1) + 1, 1, False, PAIRS - 1, False)
            attention_end(sp, None, None, a, BATCH * PAIRS - 1)

        @block.tensor
        def _(pe):
            pe.sem_inc(a.pv_done, a.pt_slots)
            pe.wait_ge(loaded, 48)
            pe.transpose(a.side[:, 0, 0:2 * DC], ln_rows[:], chip.ident[0:2 * DC, 0:2 * DC]).then_inc(ln_turned, 1)
            turn_pe(pe, chip, turn, a.banks)
            pe.wait_ge(turn.turned_read, TILES)
            pe.wait_ge(wo_loaded, 16)
            first_maxima_pe(pe, chip, a, project)
            attention_units(pe, PAIRS, lambda unit, u, following: attention_pe(
                pe, chip, a, unit, u, (a.cycle if following else a.last)(unit), project, following=following))
            last = BATCH * PAIRS - 1
            for name in LAST_OUT:
                side_pe(pe, chip, a, a.epilogue(last), name, last, 1, project, number(last, 3))

        @block.scalar
        def _(act):
            attention_start_act(act, chip, a)
            act.wait_ge(ln_turned, 1)
            act.copy(ln[:], a.side[:, 0, 0:2 * DC]).then_inc(ln_kept, 1)
            act.wait_ge(ln_kept, 1)
            turn_act(act, chip, turn, a.banks, scale=ln[:, 0:DC], bias=ln[:, DC:2 * DC])
            for name in a.parts:
                keep_part_act(act, a, a.prologue, name, 0, 0)
            attention_units(act, PAIRS, lambda unit, u, following: attention_act(
                act, a, unit, u, (a.cycle if following else a.last)(unit), SCALE, project, following=following))

        @block.vector
        def _(dve):
            dve.wait_ge(loaded, 48)
            dve.tensor_scalar(gb[:], gb[:], a.gate, None, ALU.mult).then_inc(gb_made, 1)
            normalize_twice_dve(dve, chip, norm_steps)
            normalize_dve(dve, chip, turn, chip.xn)
            dve.wait_ge(a.prepared, a.prepares)
            dve.wait_ge(gb_made, 2)
            dve.sem_inc(a.lo_made, a.exp_slots)
            for name in a.parts:
                keep_part_dve(dve, a, a.prologue, name, 0, 0)
            first_maxima_dve(dve, a)
            attention_units(dve, PAIRS, lambda unit, u, following: attention_dve(
                dve, chip, a, unit, u, (a.cycle if following else a.last)(unit), project, following=following))
            attention_end(None, dve, None, a, BATCH * PAIRS - 1)
            for name in LAST_OUT:
                add_output(dve, chip, a, a.epilogue(BATCH * PAIRS - 1), name, 1)

        @block.gpsimd
        def _(pool):
            attention_prepare(pool, chip, a)
            add_bias_pool(pool, chip, norm_steps, gb_made, gb[:])
            pool.wait_ge(gb_made, 2)
            pool.wait_ge(a.prepared, a.prepares)
            pool.sem_inc(a.spread_done, 1)
            pool.sem_inc(a.ot_done, 1)
            double_parts(pool, a, 0, 0)
            attention_units(pool, PAIRS, lambda unit, u, following: attention_pool(pool, a, unit, u, following=following))
            attention_end(None, None, pool, a, BATCH * PAIRS - 1)



def l3_ffn(nc, chip, I):
    E, F, K = 32, 256, 4
    G, KEPT_GROUPS = 8, 4
    FC = F // P
    CAP = TOKENS * K * 5 // (E * 4)
    SLOTS_USED = E * CAP
    PIECES = ((0, P), (P, P), (2 * P, CAP - 2 * P))
    FAR = 65536.0
    CLEAR = 8
    CLEARS = SLOTS_USED // (P * CLEAR)
    slots_x = nc.dram_tensor("l3f_slots_x", [SLOTS_USED + K * TOKENS, D], F32, kind="Internal").ap()
    slots_y = nc.dram_tensor("l3f_slots_y", [SLOTS_USED, D], F32, kind="Internal").ap()
    with ExitStack() as stack:
        sb, psum, sem = scope(nc, stack, "l3f")
        wg_rows, wg = sb("wg_rows", [E, D]), sb("wg", [P, DC, E])
        sw1, sw3, sw2 = sb("sw1", [P, DC, F]), sb("sw3", [P, DC, F]), sb("sw2", [P, FC, D])
        w1, w3, w2 = sb("w1", [P, 2, DC, F]), sb("w3", [P, 2, DC, F]), sb("w2", [P, 2, FC, D])
        zeros = sb("zeros", [P, CLEAR * D])
        scores, chosen, product = (sb(n, [P, TILES, E]) for n in ("scores", "chosen", "product"))
        picked = [sb(f"picked{k}", [P, TILES, E]) for k in range(K)]
        groups, group_pick, group_kept, group_order = (sb(n, [P, TILES, G]) for n in ("groups", "group_pick", "group_kept", "group_order"))
        order = sb("order", [P, TILES, E])
        restart, bases, rank, upto = (sb(n, [P, E, TILES]) for n in ("restart", "bases", "rank", "upto"))
        best, total = sb("best", [P, TILES]), sb("total", [P, TILES])
        weight, place, fits, spare = (sb(n, [P, K, TILES]) for n in ("weight", "place", "fits", "spare"))
        scatter_index, gather_index = sb("scatter_index", [P, K, TILES], I32), sb("gather_index", [P, K, TILES], I32)
        z_silu, z_hidden = sb("z_silu", [P, FC, 512]), sb("z_hidden", [P, FC, 512])
        x_rows, xt = sb("x_rows", [P, 2, 3, D]), sb("xt", [P, 2, DC, CAP])
        silu, hidden, y_rows = sb("silu", [P, FC, CAP]), sb("hidden", [P, FC, CAP]), sb("y_rows", [P, 2, 3, D])
        fetched = [chip.xt[:].rearrange("p c (t d) -> p (c t) d", d=D)] + [sb(f"fetched{k}", [P, TILES, D]) for k in range(1, K)]
        p_xt, p_h, p_y = psum("p_xt", [P, DC, 512]), psum("p_h", [P, 4, 512]), psum("p_y", [P, 2, 512])
        turn = TurnSemaphores(sem, "t")
        (loaded, s_loaded, zeroed, cleared, constants, norm_steps, wg_turned, wg_kept, routed, exped, chose, ranked, route_steps,
         placed, scattered, z_done, z_silu_kept, z_kept, z_out, z_added, x_turned, xt_kept, h_done, silu_kept, h_kept, y_done,
         y_kept, y_free, added) = (sem(n) for n in (
            "loaded", "s_loaded", "zeroed", "cleared", "constants", "norm_steps", "wg_turned", "wg_kept", "routed", "exped", "chose",
            "ranked", "route_steps", "placed", "scattered", "z_done", "z_silu_kept", "z_kept", "z_out", "z_added", "x_turned",
            "xt_kept", "h_done", "silu_kept", "h_kept", "y_done", "y_kept", "y_free", "added"))
        w_loaded = [sem("w_loaded0"), sem("w_loaded1")]
        x_loaded = [sem("x_loaded0"), sem("x_loaded1")]
        y_stored = [sem("y_stored0"), sem("y_stored1")]
        gathered = [sem(f"gathered{q}") for q in range(TILES // 2)]
        block = stack.enter_context(nc.Block())

        def load_expert(sp, e, u):
            for w, name, inner in ((w1, "L3_ffn_w1", DC), (w3, "L3_ffn_w3", DC), (w2, "L3_ffn_w2", FC)):
                sp.dma_start(w[:, u, :, :], expert(I[name], e).rearrange("(c p) f -> p c f", p=P)).then_inc(w_loaded[u], 16)

        def slot_rows(slots, rows, e, u):
            last, n = PIECES[2]
            return ((slots[bass.ds(e * CAP, 2 * P), :].rearrange("(t p) d -> p t d", p=P), rows[:, u, 0:2, :]),
                    (slots[bass.ds(e * CAP + last, n), :], rows[0:n, u, 2, :]))

        def load_rows(sp, e, u):
            for dram, rows in slot_rows(slots_x, x_rows, e, u):
                sp.dma_start(rows, dram).then_inc(x_loaded[u], 16)

        def experts(engine, run):
            with engine.Fori(0, E // 2 - 1) as i:
                for u in range(2):
                    run(i * 2 + u, u, i, True)
            for u in range(2):
                run(E - 2 + u, u, E // 2 - 1, False)

        @block.sync
        def _(sp):
            sp.dma_start(wg_rows[:], I["L3_ffn_wg"]).then_inc(loaded, 16)
            for w, name in ((sw1, "L3_ffn_sw1"), (sw3, "L3_ffn_sw3"), (sw2, "L3_ffn_sw2")):
                sp.dma_start(w[:], I[name].rearrange("(c p) f -> p c f", p=P)).then_inc(s_loaded, 16)
            sp.wait_ge(zeroed, 1)
            for n in range(CLEARS):
                rows = slots_x[n * P * CLEAR:(n + 1) * P * CLEAR, :].rearrange("(p n) d -> p (n d)", p=P)
                sp.dma_start(rows, zeros[:]).then_inc(cleared, 16)
            for u in range(2):
                load_expert(sp, u, u)
            sp.wait_ge(placed, 1)
            sp.wait_ge(scattered, 16 * K * TILES)
            for u in range(2):
                load_rows(sp, u, u)

            def run(e, u, i, more):
                if more:
                    sp.wait_ge(x_turned, e + 1)
                    load_rows(sp, e + 2, u)
                    sp.wait_ge(y_done, e * 3 + 4)
                    load_expert(sp, e + 2, u)
            experts(sp, run)

        @block.gpsimd
        def _(pool):
            pool.sem_inc(y_free, 2)
            pool.memset(zeros[:], 0.0).then_inc(zeroed, 1)
            routing_constants(pool, constants, order[:], restart[:], None, ascending=False)
            iota = dict(allow_small_or_imprecise_dtypes=True)
            pool.iota(group_order[:], [[0, TILES], [-1, G]], base=G, channel_multiplier=0, **iota).then_inc(constants, 1)
            pool.iota(bases[:], [[CAP, E], [0, TILES]], base=0, channel_multiplier=0, **iota).then_inc(constants, 1)
            pool.iota(spare[:], [[TOKENS, K], [P, TILES]], base=SLOTS_USED, channel_multiplier=1, **iota).then_inc(constants, 1)
            pool.wait_ge(placed, 1)
            pool.wait_ge(turn.staged, TILES)
            pool.wait_ge(cleared, 16 * CLEARS)
            for t in range(TILES):
                for k in range(K):
                    pool.indirect_dma_start(slots_x, bass.IndirectOffsetOnAxis(scatter_index[:, k, t:t + 1], 0), chip.xn[:, t, :], None
                                            ).then_inc(scattered, 16)

            def run(e, u, i, more):
                pool.wait_ge(y_kept, e * 3 + 4)
                for dram, rows in slot_rows(slots_y, y_rows, e, u):
                    pool.dma_start(dram, rows).then_inc(y_stored[u], 16)
                pool.wait_ge(y_stored[u], i * 32 + 32)
                pool.sem_inc(y_free, 1)
            experts(pool, run)
            for t in range(TILES):
                for k in range(K):
                    pool.indirect_dma_start(fetched[k][:, t, :], None, slots_y, bass.IndirectOffsetOnAxis(gather_index[:, k, t:t + 1], 0)
                                            ).then_inc(gathered[t // 2], 16)

        @block.tensor
        def _(pe):
            pe.wait_ge(loaded, 16)
            for c in range(DC):
                ins = pe.transpose(p_y[:, 0, c * E:(c + 1) * E], wg_rows[:, c * P:(c + 1) * P], chip.ident[0:E, 0:E])
            ins.then_inc(wg_turned, 1)
            turn_pe(pe, chip, turn, p_h)
            pe.wait_ge(wg_kept, 1)
            for t in range(TILES):
                pe.wait_ge(turn.turned_read, t + 1)
                for c in range(DC):
                    ins = pe.matmul(p_y[:, 1, t * E:(t + 1) * E], chip.xt[:, c, t * P:(t + 1) * P], wg[:, c, :],
                                    start=c == 0, stop=c == DC - 1)
            ins.then_inc(routed, 1)

            def shared_block(b):
                pe.wait_ge(z_kept, b * FC)
                for f in range(FC):
                    for k, w in ((0, sw1), (2, sw3)):
                        for c in range(DC):
                            ins = pe.matmul(p_h[:, k + f, :], w[:, c, f * P:(f + 1) * P], chip.xt[:, c, b * 512:(b + 1) * 512],
                                            start=c == 0, stop=c == DC - 1)
                    ins.then_inc(z_done, 1)
                for t in range(4):
                    at = 4 * b + t
                    pe.wait_ge(z_kept, (b + 1) * FC)
                    if at >= 2:
                        pe.wait_ge(z_added, at - 1)
                    for f in range(FC):
                        ins = pe.matmul(p_xt[:, t % 2, 0:D], z_hidden[:, f, t * P:(t + 1) * P], sw2[:, f, :],
                                        start=f == 0, stop=f == FC - 1)
                    ins.then_inc(z_out, 1)

            pe.wait_ge(chose, 1)
            rhs = chosen[:].rearrange("p t e -> p e t")
            pe.matmul(p_y[:, 0, :].rearrange("p (e t) -> p e t", e=E), chip.before[:], rhs, start=True, stop=True)
            pe.matmul(p_y[:, 1, :].rearrange("p (e t) -> p e t", e=E), chip.ones[:], rhs, start=True, stop=True).then_inc(ranked, 1)
            pe.wait_ge(s_loaded, 48)
            for b in range(4):
                shared_block(b)

            def turn_rows(e, u, i):
                pe.wait_ge(x_loaded[u], i * 32 + 32)
                pe.wait_ge(xt_kept, e * DC + 1)
                for c in range(DC):
                    for j, (at, n) in enumerate(PIECES):
                        ins = pe.transpose(p_xt[:, c, at:at + n], x_rows[0:n, u, j, c * P:(c + 1) * P], chip.ident[0:n, 0:n])
                ins.then_inc(x_turned, 1)

            def run(e, u, i, more):
                pe.wait_ge(w_loaded[u], i * 48 + 48)
                pe.wait_ge(xt_kept, e * DC + (DC + 1))
                pe.wait_ge(h_kept, e * FC + 1)
                for f in range(FC):
                    for k, w in ((0, w1), (2, w3)):
                        for c in range(DC):
                            ins = pe.matmul(p_h[:, k + f, 0:CAP], w[:, u, c, f * P:(f + 1) * P], xt[:, u, c, :],
                                            start=c == 0, stop=c == DC - 1)
                    ins.then_inc(h_done, 1)
                if more or u == 0:
                    turn_rows(e + 1, 1 - u, i + u)
                pe.wait_ge(h_kept, e * FC + (FC + 1))
                pe.wait_ge(y_kept, e * 3 + 1)
                for j, (at, n) in enumerate(PIECES):
                    for f in range(FC):
                        ins = pe.matmul(p_y[0:n, j // 2, j % 2 * D:j % 2 * D + D], hidden[:, f, at:at + n], w2[:, u, f, :],
                                        start=f == 0, stop=f == FC - 1)
                    ins.then_inc(y_done, 1)

            pe.wait_ge(z_added, TILES)
            pe.sem_inc(y_done, 1)
            turn_rows(0, 0, 0)
            experts(pe, run)

        @block.scalar
        def _(act):
            turn_act(act, chip, turn, p_h)
            act.wait_ge(route_steps, 2)
            act.activation(scores[:], scores[:], ACT.Exp).then_inc(exped, 1)
            for b in range(4):
                for f in range(FC):
                    act.wait_ge(z_done, b * FC + f + 1)
                    if b >= 1:
                        act.wait_ge(z_kept, (b - 1) * FC + f + 1)
                    act.activation(z_silu[:, f, :], p_h[:, f, :], ACT.Silu).then_inc(z_silu_kept, 1)

            def run(e, u, i, more):
                for f in range(FC):
                    act.wait_ge(h_done, e * FC + (f + 1))
                    act.wait_ge(h_kept, e * FC + 1)
                    act.activation(silu[:, f, :], p_h[:, f, 0:CAP], ACT.Silu).then_inc(silu_kept, 1)
            experts(act, run)

        @block.vector
        def _(dve):
            row_statistics(dve, chip, norm_steps, 0, chip.x)
            dve.wait_ge(wg_turned, 1)
            dve.tensor_copy(wg[:], p_y[:, 0, 0:DC * E].rearrange("p (c e) -> p c e", c=DC)).then_inc(wg_kept, 1)
            normalize_dve(dve, chip, turn, chip.x)
            dve.wait_ge(routed, 1)
            step = Steps(dve, route_steps)
            p_logits = p_y[:, 1, :].rearrange("p (t e) -> p t e", e=E)
            step(dve.tensor_reduce(best[:], p_logits, AX.X, ALU.max))
            step(dve.tensor_tensor(scores[:], p_logits, spread(best[:], E), ALU.subtract))
            dve.wait_ge(exped, 1)
            step(dve.tensor_reduce(total[:], scores[:], AX.X, ALU.add))
            step(dve.reciprocal(total[:], total[:]))
            step(dve.tensor_tensor(scores[:], scores[:], spread(total[:], E), ALU.mult))
            dve.wait_ge(constants, 5)
            step(dve.tensor_scalar(restart[:], restart[:], 0.0, None, ALU.is_gt))
            step(dve.tensor_reduce(groups[:].rearrange("p t g -> p (t g)"), scores[:].rearrange("p t (g n) -> p (t g) n", g=G), AX.X, ALU.max))
            for k in range(KEPT_GROUPS):
                choose(dve, step, groups[:], group_pick[:], group_order[:], total[:], best[:], 2.0)
            step(dve.tensor_scalar(group_kept[:], groups[:], 0.0, 2.0, ALU.is_ge, ALU.mult))
            step(dve.tensor_tensor(scores[:].rearrange("p t (g n) -> p (t g) n", g=G), scores[:].rearrange("p t (g n) -> p (t g) n", g=G),
                                   spread(group_kept[:].rearrange("p t g -> p (t g)"), E // G), ALU.subtract))
            for k in range(K):
                choose(dve, step, scores[:], picked[k][:], order[:], weight[:, k, :], best[:], 2.0)
            step(dve.tensor_tensor(chosen[:], picked[0][:], picked[1][:], ALU.add))
            for k in range(2, K):
                step(dve.tensor_tensor(chosen[:], chosen[:], picked[k][:], ALU.add))
            dve.sem_inc(chose, 1)
            step(dve.tensor_reduce(total[:], weight[:].rearrange("p k t -> p t k"), AX.X, ALU.add))
            step(dve.tensor_scalar(total[:], total[:], 1e-9, None, ALU.add))
            step(dve.reciprocal(total[:], total[:]))
            step(dve.tensor_scalar(total[:], total[:], chip.gates[:, 7:8], None, ALU.mult))
            step(dve.tensor_tensor(weight[:], weight[:], total[:].unsqueeze(1).to_broadcast([P, K, TILES]), ALU.mult))
            dve.wait_ge(ranked, 1)
            within, tile_total = (p_y[:, n, :].rearrange("p (e t) -> p e t", e=E) for n in range(2))
            ranks_dve(dve, step, rank[:], upto[:], within, tile_total, restart[:])
            step(dve.tensor_scalar(upto[:], rank[:], float(CAP), FAR, ALU.is_ge, ALU.mult))
            step(dve.tensor_tensor(rank[:], rank[:], upto[:], ALU.add))
            step(dve.tensor_tensor(rank[:], rank[:], bases[:], ALU.add))
            for k in range(K):
                step(dve.tensor_tensor(product[:], picked[k][:], rank[:].rearrange("p e t -> p t e"), ALU.mult))
                step(dve.tensor_reduce(place[:, k, :], product[:], AX.X, ALU.add))
            step(dve.tensor_scalar(fits[:], place[:], FAR, None, ALU.is_lt))
            step(dve.tensor_tensor(place[:], place[:], fits[:], ALU.mult))
            step(dve.tensor_copy(gather_index[:], place[:]))
            step(dve.tensor_tensor(weight[:], weight[:], fits[:], ALU.mult))
            step(dve.tensor_scalar(fits[:], fits[:], -1.0, 1.0, ALU.mult, ALU.add))
            step(dve.tensor_tensor(fits[:], fits[:], spare[:], ALU.mult))
            step(dve.tensor_tensor(place[:], place[:], fits[:], ALU.add))
            step(dve.tensor_copy(scatter_index[:], place[:]))
            dve.sem_inc(placed, 1)
            for b in range(4):
                for f in range(FC):
                    dve.wait_ge(z_silu_kept, b * FC + f + 1)
                    if b >= 1:
                        dve.wait_ge(z_out, 4 * b)
                    dve.tensor_tensor(z_hidden[:, f, :], z_silu[:, f, :], p_h[:, 2 + f, :], ALU.mult).then_inc(z_kept, 1)
                for t in range(4 * b, 4 * b + 4):
                    dve.wait_ge(z_out, t + 1)
                    dve.scalar_tensor_tensor(chip.x[:, t, :], p_xt[:, t % 2, 0:D], chip.gates[:, 7:8], chip.x[:, t, :],
                                             ALU.mult, ALU.add).then_inc(z_added, 1)

            def keep_xt(e, u):
                dve.wait_ge(x_turned, e + 1)
                for c in range(DC):
                    dve.tensor_copy(xt[:, u, c, :], p_xt[:, c, 0:CAP]).then_inc(xt_kept, 1)

            def run(e, u, i, more):
                for f in range(FC):
                    dve.wait_ge(silu_kept, e * FC + (f + 1))
                    dve.wait_ge(y_done, e * 3 + 1)
                    dve.tensor_tensor(hidden[:, f, :], silu[:, f, :], p_h[:, 2 + f, 0:CAP], ALU.mult).then_inc(h_kept, 1)
                if more or u == 0:
                    keep_xt(e + 1, 1 - u)
                dve.wait_ge(y_free, e + 1)
                dve.wait_ge(y_done, e * 3 + 3)
                dve.tensor_copy(y_rows[:, u, 0:2, :].rearrange("p j d -> p (j d)"), p_y[:, 0, :]).then_inc(y_kept, 2)
                dve.wait_ge(y_done, e * 3 + 4)
                rows = PIECES[2][1]
                dve.tensor_copy(y_rows[0:rows, u, 2, :], p_y[0:rows, 1, 0:D]).then_inc(y_kept, 1)

            for counted in (xt_kept, h_kept, y_kept):
                dve.sem_inc(counted, 1)
            keep_xt(0, 0)
            experts(dve, run)
            for t in range(TILES):
                if t % 2 == 0:
                    dve.wait_ge(gathered[t // 2], 2 * K * 16)
                step = Steps(dve, added, K * t)
                for k in range(K):
                    step(dve.scalar_tensor_tensor(chip.x[:, t, :], fetched[k][:, t, :], weight[:, k, t:t + 1], chip.x[:, t, :],
                                                  ALU.mult, ALU.add))


def store(nc, chip, out):
    with ExitStack() as stack:
        _, _, sem = scope(nc, stack, "store")
        stored = sem("stored")
        block = stack.enter_context(nc.Block())

        @block.sync
        def _(sp):
            sp.dma_start(out.rearrange("b (t p) d -> p (b t) d", p=P), chip.x[:]).then_inc(stored, 16)
            sp.wait_ge(stored, 16)


def build(nc, I, out):
    with ExitStack() as stack:
        chip = Chip(nc, stack)
        setup(nc, chip, I)
        l0_attention(nc, chip, I)
        l0_ffn(nc, chip, I)
        l1_attention(nc, chip, I)
        l1_ffn(nc, chip, I)
        l2_attention(nc, chip, I)
        l2_ffn(nc, chip, I)
        l3_attention(nc, chip, I)
        l3_ffn(nc, chip, I)
        store(nc, chip, out)


def kernel(**inputs):
    import numpy as np
    import concourse.bacc as bacc
    from concourse.bass_utils import run_bass_kernel_spmd

    nc = bacc.Bacc("TRN2", target_bir_lowering=False, num_devices=1)
    arrays, I = {}, {}
    for name in inputs:
        a = np.ascontiguousarray(inputs[name])
        arrays[f"in_{name}"] = a
        I[name] = nc.dram_tensor(f"in_{name}", a.shape, mybir.dt.from_np(a.dtype), kind="ExternalInput").ap()
    out = nc.dram_tensor("out_0_dram", (BATCH, SEQ, D), F32, kind="ExternalOutput").ap()
    build(nc, I, out)
    r = run_bass_kernel_spmd(nc, [arrays], core_ids=[0])
    return r.results[0]["out_0_dram"]
```
